# Optimizing a Trainium2 kernel written in Bass

```python
import numpy as np
import jax
import jax.numpy as jnp

def _softmax(x, axis=-1):
    return jax.nn.softmax(x, axis=axis)

def _gelu(x):
    return jax.nn.gelu(x, approximate=True)

def _silu(x):
    return jax.nn.silu(x)

def _sigmoid(x):
    return jax.nn.sigmoid(x)

def _layernorm(x, axis=-1, eps=1e-05):
    m = jnp.mean(x, axis=axis, keepdims=True)
    v = jnp.var(x, axis=axis, keepdims=True)
    return (x - m) / jnp.sqrt(v + eps)

def _scatter_add(tgt, idx, src, axis=0):
    return tgt.at[idx].add(src)

def _segment_sum(src, seg, n):
    return jax.ops.segment_sum(src, seg, n)
kernel_name = 'mk_lm_tower_d2_tok_ids1024_r4_bf258d'

def setup_inputs(seed: int=0):
    np.random.seed(seed)
    _w = jnp.asarray

    def _rec_inputs():
        import jax
        import jax.numpy as jnp
        _rk = jax.random.key(seed)
        x = jax.random.randint(jax.random.fold_in(_rk, 1), (2, 1024), 0, 12564, jnp.int32)
        return x
    x = _rec_inputs()

    def _L0_tok_setup():
        import jax, jax.numpy as jnp
        import numpy as np
        VOCAB = 50257
        DIM = 256
        GROUP = 128

        def _sign_ste_fwd_only(x):
            s = jnp.sign(x)
            return jnp.where(s == 0, jnp.asarray(1.0, x.dtype), s)

        def quantize_literati(w, scales, group_size=GROUP):
            V, D = w.shape
            G = group_size
            w_groups = w.reshape(V, D // G, G)
            signs = _sign_ste_fwd_only(w_groups)
            s = jnp.maximum(scales, 1e-08)[..., None]
            return (signs * s).reshape(V, D)
        key = jax.random.key(seed)
        k1, k2, k3 = jax.random.split(key, 3)
        input_ids = jax.random.randint(k1, (8, 512), 0, VOCAB)
        weight = jax.random.normal(k2, (VOCAB, DIM), dtype=jnp.float32) * 0.02
        scales = jax.random.uniform(k3, (VOCAB, DIM // GROUP), dtype=jnp.float32) * 0.1 + 0.05
        return {'input_ids': input_ids, 'weight': weight, 'scales': scales}
    _L0_tok_all = _L0_tok_setup()
    _L0_tok_in = {k: v for k, v in _L0_tok_all.items() if k in ('weight', 'scales')}
    del _L0_tok_all

    def _L0_attn_setup():
        import jax, jax.numpy as jnp
        import numpy as np
        D_MODEL = 256
        NUM_HEADS = 16
        HEAD_DIM = D_MODEL // NUM_HEADS
        EPS = 1e-08
        key = jax.random.key(seed)
        ks = jax.random.split(key, 6)
        B, T = (4, 512)
        s = 0.02
        return {'x': jax.random.normal(ks[0], (B, T, D_MODEL), dtype=jnp.float32), 'Wq': jax.random.normal(ks[1], (D_MODEL, D_MODEL), dtype=jnp.float32) * s, 'Wk': jax.random.normal(ks[2], (D_MODEL, D_MODEL), dtype=jnp.float32) * s, 'Wv': jax.random.normal(ks[3], (D_MODEL, D_MODEL), dtype=jnp.float32) * s, 'Wo': jax.random.normal(ks[4], (D_MODEL, D_MODEL), dtype=jnp.float32) * s, 'bo': jnp.zeros((D_MODEL,), dtype=jnp.float32)}
    _L0_attn_all = _L0_attn_setup()
    _L0_attn_in = {k: v for k, v in _L0_attn_all.items() if k in ('Wq', 'Wk', 'Wv', 'Wo', 'bo')}
    del _L0_attn_all

    def _L0_ffn_setup():
        import jax, jax.numpy as jnp
        import numpy as np
        D_MODEL = 256
        FFN = 256
        N_EXPERTS = 8
        N_SHARED = 1
        TOP_K = 2
        B, S = (2, 512)

        def _swiglu(h):
            a, b = jnp.split(h, 2, axis=-1)
            return jax.nn.silu(a) * b
        key = jax.random.key(seed)
        ks = jax.random.split(key, 12)
        sc = 0.02
        return {'x': jax.random.normal(ks[0], (B, S, D_MODEL), dtype=jnp.float32), 'gate_w': jax.random.normal(ks[1], (D_MODEL, N_EXPERTS), dtype=jnp.float32) * sc, 'gate_b': jnp.zeros((N_EXPERTS,), dtype=jnp.float32), 'sw1': jax.random.normal(ks[2], (N_SHARED, D_MODEL, 2 * FFN), dtype=jnp.float32) * sc, 'sb1': jnp.zeros((N_SHARED, 2 * FFN), dtype=jnp.float32), 'sw2': jax.random.normal(ks[3], (N_SHARED, FFN, D_MODEL), dtype=jnp.float32) * sc, 'sb2': jnp.zeros((N_SHARED, D_MODEL), dtype=jnp.float32), 'rw1': jax.random.normal(ks[4], (N_EXPERTS, D_MODEL, 2 * FFN), dtype=jnp.float32) * sc, 'rb1': jnp.zeros((N_EXPERTS, 2 * FFN), dtype=jnp.float32), 'rw2': jax.random.normal(ks[5], (N_EXPERTS, FFN, D_MODEL), dtype=jnp.float32) * sc, 'rb2': jnp.zeros((N_EXPERTS, D_MODEL), dtype=jnp.float32)}
    _L0_ffn_all = _L0_ffn_setup()
    _L0_ffn_in = {k: v for k, v in _L0_ffn_all.items() if k in ('gate_w', 'gate_b', 'sw1', 'sb1', 'sw2', 'sb2', 'rw1', 'rb1', 'rw2', 'rb2')}
    del _L0_ffn_all

    def _L1_attn_setup():
        import jax, jax.numpy as jnp
        import numpy as np
        D_MODEL = 256
        N_HEADS = 16
        ORDER = 6
        M = 2 * ORDER - 1
        D_HEAD = D_MODEL // N_HEADS

        def _collapsed_beta() -> np.ndarray:
            j = np.arange(ORDER, dtype=np.float64)
            alpha = (j + 1.0) ** (-1.5)
            tail = np.cumsum(alpha[::-1])[::-1]
            beta = np.concatenate([[0.0], tail[1:], np.zeros(ORDER - 1)])
            return (beta / beta.sum()).astype(np.float32)

        def _cheb_features(x, m):
            ts = [jnp.ones_like(x), x]
            for _ in range(m - 2):
                ts.append(2.0 * x * ts[-1] - ts[-2])
            return jnp.stack(ts[:m], axis=-1)
        key = jax.random.key(seed)
        k1, k2, k3 = jax.random.split(key, 3)
        B, S = (2, 1024)
        x = jax.random.normal(k1, (B, S, D_MODEL), dtype=jnp.float32)
        w_in = jax.random.normal(k2, (3 * D_MODEL, D_MODEL), dtype=jnp.float32) * D_MODEL ** (-0.5)
        w_out = jax.random.normal(k3, (D_MODEL, D_MODEL), dtype=jnp.float32) * D_MODEL ** (-0.5)
        beta = jnp.tile(jnp.asarray(_collapsed_beta())[None, :], (N_HEADS, 1))
        return {'x': x, 'w_in': w_in, 'w_out': w_out, 'beta': beta}
    _L1_attn_all = _L1_attn_setup()
    _L1_attn_in = {k: v for k, v in _L1_attn_all.items() if k in ('w_in', 'w_out', 'beta')}
    del _L1_attn_all

    def _L1_ffn_setup():
        import jax, jax.numpy as jnp
        import numpy as np
        H = 256
        F = 1024
        E = 8
        TOP_K = 2
        B, S = (1, 512)
        key = jax.random.key(seed)
        k0, k1, k2, k3 = jax.random.split(key, 4)
        hidden_states = jax.random.normal(k0, (B, S, H), dtype=jnp.float32)
        gate_w = jax.random.normal(k1, (E, H), dtype=jnp.float32) * 0.02
        gate_up_w = jax.random.normal(k2, (E, 2 * F, H), dtype=jnp.float32) * 0.02
        down_w = jax.random.normal(k3, (E, H, F), dtype=jnp.float32) * 0.02
        return {'hidden_states': hidden_states, 'gate_w': gate_w, 'gate_up_w': gate_up_w, 'down_w': down_w}
    _L1_ffn_all = _L1_ffn_setup()
    _L1_ffn_in = {k: v for k, v in _L1_ffn_all.items() if k in ('gate_w', 'gate_up_w', 'down_w')}
    del _L1_ffn_all
    return {'x': x, 'L0_tok_weight': _L0_tok_in['weight'], 'L0_tok_scales': _L0_tok_in['scales'], 'L0_attn_Wq': _L0_attn_in['Wq'], 'L0_attn_Wk': _L0_attn_in['Wk'], 'L0_attn_Wv': _L0_attn_in['Wv'], 'L0_attn_Wo': _L0_attn_in['Wo'], 'L0_attn_bo': _L0_attn_in['bo'], 'L0_ffn_gate_w': _L0_ffn_in['gate_w'], 'L0_ffn_gate_b': _L0_ffn_in['gate_b'], 'L0_ffn_sw1': _L0_ffn_in['sw1'], 'L0_ffn_sb1': _L0_ffn_in['sb1'], 'L0_ffn_sw2': _L0_ffn_in['sw2'], 'L0_ffn_sb2': _L0_ffn_in['sb2'], 'L0_ffn_rw1': _L0_ffn_in['rw1'], 'L0_ffn_rb1': _L0_ffn_in['rb1'], 'L0_ffn_rw2': _L0_ffn_in['rw2'], 'L0_ffn_rb2': _L0_ffn_in['rb2'], 'L1_attn_w_in': _L1_attn_in['w_in'], 'L1_attn_w_out': _L1_attn_in['w_out'], 'L1_attn_beta': _L1_attn_in['beta'], 'L1_ffn_gate_w': _L1_ffn_in['gate_w'], 'L1_ffn_gate_up_w': _L1_ffn_in['gate_up_w'], 'L1_ffn_down_w': _L1_ffn_in['down_w']}

def reference(x, L0_tok_weight, L0_tok_scales, L0_attn_Wq, L0_attn_Wk, L0_attn_Wv, L0_attn_Wo, L0_attn_bo, L0_ffn_gate_w, L0_ffn_gate_b, L0_ffn_sw1, L0_ffn_sb1, L0_ffn_sw2, L0_ffn_sb2, L0_ffn_rw1, L0_ffn_rb1, L0_ffn_rw2, L0_ffn_rb2, L1_attn_w_in, L1_attn_w_out, L1_attn_beta, L1_ffn_gate_w, L1_ffn_gate_up_w, L1_ffn_down_w):
    import jax
    import jax.numpy as jnp

    def _L0_tok_ref(input_ids, weight, scales):
        import jax, jax.numpy as jnp
        import numpy as np
        VOCAB = 50257
        DIM = 256
        GROUP = 128

        def _sign_ste_fwd_only(x):
            s = jnp.sign(x)
            return jnp.where(s == 0, jnp.asarray(1.0, x.dtype), s)

        def quantize_literati(w, scales, group_size=GROUP):
            V, D = w.shape
            G = group_size
            w_groups = w.reshape(V, D // G, G)
            signs = _sign_ste_fwd_only(w_groups)
            s = jnp.maximum(scales, 1e-08)[..., None]
            return (signs * s).reshape(V, D)
        w_q = quantize_literati(weight, scales)
        return jnp.take(w_q, input_ids, axis=0)

    def _L0_attn_ref(x, Wq, Wk, Wv, Wo, bo):
        import jax, jax.numpy as jnp
        import numpy as np
        D_MODEL = 256
        NUM_HEADS = 16
        HEAD_DIM = D_MODEL // NUM_HEADS
        EPS = 1e-08
        B, T, _ = x.shape
        H, D = (NUM_HEADS, HEAD_DIM)
        scale = jnp.sqrt(jnp.asarray(D, dtype=x.dtype))
        q = (x @ Wq.T).reshape(B, T, H, D).transpose(0, 2, 1, 3)
        k = (x @ Wk.T).reshape(B, T, H, D).transpose(0, 2, 1, 3)
        v = (x @ Wv.T).reshape(B, T, H, D).transpose(0, 2, 1, 3)
        s = jnp.einsum('bhtd,bhsd->bhts', q, k) / scale
        m = jnp.max(s, axis=-1, keepdims=True)
        e = jnp.exp(s - m)
        num = jnp.einsum('bhts,bhsd->bhtd', e, v)
        den = jnp.sum(e, axis=-1, keepdims=True) + EPS
        out = (num / den).transpose(0, 2, 1, 3).reshape(B, T, H * D)
        return out @ Wo.T + bo

    def _L0_ffn_ref(x, gate_w, gate_b, sw1, sb1, sw2, sb2, rw1, rb1, rw2, rb2):
        import jax, jax.numpy as jnp
        import numpy as np
        D_MODEL = 256
        FFN = 256
        N_EXPERTS = 8
        N_SHARED = 1
        TOP_K = 2
        B, S = (2, 512)

        def _swiglu(h):
            a, b = jnp.split(h, 2, axis=-1)
            return jax.nn.silu(a) * b
        hs = jnp.einsum('bsd,ndf->nbsf', x, sw1) + sb1[:, None, None, :]
        shared_out = jnp.einsum('nbsf,nfd->bsd', _swiglu(hs), sw2) + sb2.sum(0)
        probs = jax.nn.softmax(x @ gate_w + gate_b, axis=-1)
        topk_probs, topk_idx = jax.lax.top_k(probs, TOP_K)
        cw = jnp.sum(jax.nn.one_hot(topk_idx, N_EXPERTS, dtype=x.dtype) * topk_probs[..., None], axis=2)
        hr = jnp.einsum('bsd,edf->ebsf', x, rw1) + rb1[:, None, None, :]
        out_e = jnp.einsum('ebsf,efd->ebsd', _swiglu(hr), rw2) + rb2[:, None, None, :]
        routed_out = jnp.einsum('ebsd,bse->bsd', out_e, cw)
        return shared_out + routed_out

    def _L1_attn_ref(x, w_in, w_out, beta):
        import jax, jax.numpy as jnp
        import numpy as np
        D_MODEL = 256
        N_HEADS = 16
        ORDER = 6
        M = 2 * ORDER - 1
        D_HEAD = D_MODEL // N_HEADS

        def _collapsed_beta() -> np.ndarray:
            j = np.arange(ORDER, dtype=np.float64)
            alpha = (j + 1.0) ** (-1.5)
            tail = np.cumsum(alpha[::-1])[::-1]
            beta = np.concatenate([[0.0], tail[1:], np.zeros(ORDER - 1)])
            return (beta / beta.sum()).astype(np.float32)

        def _cheb_features(x, m):
            ts = [jnp.ones_like(x), x]
            for _ in range(m - 2):
                ts.append(2.0 * x * ts[-1] - ts[-2])
            return jnp.stack(ts[:m], axis=-1)
        B, S, _ = x.shape
        qkv = x @ w_in.T
        q, k, v = jnp.split(qkv, 3, axis=-1)

        def to_heads(t):
            return t.reshape(B, S, N_HEADS, D_HEAD).transpose(0, 2, 1, 3)
        q, k, v = (to_heads(q), to_heads(k), to_heads(v))
        scale = D_HEAD ** (-0.5)
        q = jnp.clip(q * scale, -1.0, 1.0)
        k = jnp.clip(k * scale, -1.0, 1.0)
        tq = _cheb_features(q, M)
        tk = _cheb_features(k, M)
        tq = tq * beta[None, :, None, None, :]
        kv = jnp.einsum('bhskm,bhsv->bhkmv', tk, v)
        out = jnp.einsum('bhsdm,bhdmv->bhsv', tq, kv)
        out = out.transpose(0, 2, 1, 3).reshape(B, S, D_MODEL)
        return out @ w_out.T

    def _L1_ffn_ref(hidden_states, gate_w, gate_up_w, down_w):
        import jax, jax.numpy as jnp
        import numpy as np
        H = 256
        F = 1024
        E = 8
        TOP_K = 2
        B, S = (1, 512)
        b, s, h = hidden_states.shape
        x = hidden_states.reshape(-1, h)
        router_logits = x @ gate_w.T
        probs = jax.nn.softmax(router_logits.astype(jnp.float32), axis=-1)
        topw, sel = jax.lax.top_k(probs, TOP_K)
        topw = topw / jnp.sum(topw, axis=-1, keepdims=True)
        topw = topw.astype(x.dtype)
        combine = jnp.sum(jax.nn.one_hot(sel, E, dtype=x.dtype) * topw[..., None], axis=1)
        gu = jnp.einsum('th,efh->etf', x, gate_up_w)
        gate, up = (gu[..., :F], gu[..., F:])
        hact = up * jax.nn.gelu(gate, approximate=False)
        expert_out = jnp.einsum('etf,ehf->eth', hact, down_w)
        out = jnp.einsum('eth,te->th', expert_out, combine)
        return out.reshape(b, s, h)
    h = _L0_tok_ref(x, L0_tok_weight, L0_tok_scales)
    h = h + _L0_attn_ref(_layernorm(h, axis=-1), L0_attn_Wq, L0_attn_Wk, L0_attn_Wv, L0_attn_Wo, L0_attn_bo)
    h = h + _L0_ffn_ref(_layernorm(h, axis=-1), L0_ffn_gate_w, L0_ffn_gate_b, L0_ffn_sw1, L0_ffn_sb1, L0_ffn_sw2, L0_ffn_sb2, L0_ffn_rw1, L0_ffn_rb1, L0_ffn_rw2, L0_ffn_rb2)
    h = h + _L1_attn_ref(_layernorm(h, axis=-1), L1_attn_w_in, L1_attn_w_out, L1_attn_beta)
    h = h + _L1_ffn_ref(_layernorm(h, axis=-1), L1_ffn_gate_w, L1_ffn_gate_up_w, L1_ffn_down_w)
    return h

_drawn_inputs = setup_inputs


def setup_inputs(seed=0):
    import zlib

    import numpy as np

    out = dict(_drawn_inputs(seed))
    spreads = {'L0_attn_bo': (0.0, 0.1),
     'L0_ffn_gate_b': (0.0, 0.1),
     'L0_ffn_sb1': (0.0, 0.721),
     'L0_ffn_sb2': (0.0, 0.1),
     'L0_ffn_rb1': (0.0, 0.8),
     'L0_ffn_rb2': (0.0, 0.373)}
    factors = {'L0_attn_Wq': 8.0,
     'L0_attn_Wk': 8.0,
     'L0_attn_Wv': 2.974,
     'L0_attn_Wo': 2.942,
     'L0_ffn_rw1': 4.583,
     'L0_ffn_rw2': 4.325,
     'L1_ffn_gate_w': 30.733,
     'L1_ffn_gate_up_w': 22.487,
     'L1_ffn_down_w': 24.798,
     'L0_ffn_sw1': 6.087,
     'L0_ffn_sw2': 4.068}
    for name, (base, spread) in spreads.items():
        noise = np.random.default_rng([zlib.crc32(name.encode()), seed]).standard_normal(out[name].shape)
        drawn = base * np.exp(spread * noise) if base else spread * noise
        out[name] = jnp.asarray(drawn.astype(out[name].dtype))
    for name, factor in factors.items():
        out[name] = (out[name] * factor).astype(out[name].dtype)
    return out
```

```python
from contextlib import ExitStack

import numpy as np
import concourse.bass as bass
from concourse import mybir

F32 = mybir.dt.float32
BF16 = mybir.dt.bfloat16
I32 = mybir.dt.int32
U32 = mybir.dt.uint32
ALU = mybir.AluOpType
ACT = mybir.ActivationFunctionType
AX = mybir.AxisListType

P = 128
B, S, D = 2, 1024, 256
T = B * S
NT = T // P
KD = D // P
H, DH = 16, 16
HG = 4
NG = H // HG
NIT = B * NG
QT = S // P
N = 512
NE = 8
TOP_K = 2
NRT = (TOP_K * T) // P + NE - 1
F0, F1 = 256, 1024
M = 11
VOCAB = 50257
LN_EPS = 1e-5
DEN_EPS = 1e-8

C_W = D
C_ID = D + NE + 1
ROW = C_ID + 1
TRASH = P

Q_PARTS = (0, 0, 1, 1, 0, 2)
K_PARTS = (0, 1, 0, 1, 2, 0)
KROWS = 16 * len(Q_PARTS)
KMAX = KROWS + 3

K_IDENT = 0
K_TRI = K_IDENT + P
K_BLOCK = K_TRI + P
K_LT = K_BLOCK + P
K_J128 = K_LT + NE * NE
K_J = K_J128 + NT
K_PAD = K_J + NRT
K_TOK = K_PAD + ROW
K_ALL = K_TOK + NT

ARENA = 35840


class Arena:

    def __init__(self, tensor, at):
        self.tensor, self.at = tensor, at

    def take(self, words, parts=P):
        piece = self.tensor[0:parts, self.at:self.at + words]
        self.at += words
        assert self.at <= ARENA, self.at
        return piece


def step_counter(engine, sem, start=0):
    count = [start]

    def link(ins):
        ins.then_inc(sem, 1)
        count[0] += 1
        engine.wait_ge(sem, count[0])

    return link



def norm_stats(nc, dve, link, mem, stats_done, means_done, ready, var_ready, sd_ready):
    for i in range(NT):
        ready(i)
        nc.vector.bn_stats(mem.bn[:, i, :], mem.h[:, i, :]).then_inc(stats_done, 1)
    for i in range(NT):
        dve.wait_ge(stats_done, i + 1)
        nc.vector.bn_aggr(mem.mv[:, i, :], mem.bn[:, i, :]).then_inc(means_done, 1)
    dve.wait_ge(means_done, NT)
    link(nc.vector.tensor_scalar(mem.ve[:, :], mem.mv[:, :, 1], LN_EPS, None, ALU.add))
    nc.vector.tensor_copy(mem.r2[:, :], mem.ve[:, :]).then_inc(var_ready, 1)
    dve.wait_ge(sd_ready, 1)
    link(nc.vector.reciprocal(mem.rstd[:, :], mem.sd[:, :]))
    link(nc.vector.tensor_tensor(mem.r2[:, :], mem.rstd[:, :], mem.rstd[:, :], ALU.mult))
    link(nc.vector.tensor_tensor(mem.r2[:, :], mem.r2[:, :], mem.ve[:, :], ALU.mult))
    link(nc.vector.tensor_scalar(mem.r2[:, :], mem.r2[:, :], -0.5, 1.5, ALU.mult, ALU.add))
    link(nc.vector.tensor_tensor(mem.rstd[:, :], mem.rstd[:, :], mem.r2[:, :], ALU.mult))


def norm_root(nc, act, mem, var_ready, sd_ready):
    act.wait_ge(var_ready, 1)
    nc.scalar.activation(mem.sd[:, :], mem.r2[:, :], ACT.Sqrt).then_inc(sd_ready, 1)


def norm_apply(nc, mem, xn_ready):
    for i in range(NT):
        nc.vector.tensor_scalar(mem.xw[:, i, 0:D], mem.h[:, i, :], mem.mv[:, i, 0:1], mem.rstd[:, i:i + 1],
                                ALU.subtract, ALU.mult).then_inc(xn_ready, 1)


def transpose_rows(nc, pe, mem, source, ready, turned):
    for i in range(NT):
        ready(i)
        for k in range(KD):
            ins = nc.tensor.transpose(mem.ps[:, 2 * (i // 4) + k, (i % 4) * P:(i % 4 + 1) * P],
                                      source(i, k), mem.ident)
            if i % 4 == 3:
                ins.then_inc(turned, 1)


def keep_turned(nc, act, mem, turned, xT_ready):
    for c in range(NT // 4):
        for k in range(KD):
            act.wait_ge(turned, 2 * c + k + 1)
            nc.scalar.activation(mem.xT[:, k, c * N:(c + 1) * N], mem.ps[:, 2 * c + k, :],
                                 ACT.Copy).then_inc(xT_ready, 1)



def stage_embed_qkv(nc, mem, io, sem):
    a = Arena(mem.arena, 0)
    emb = a.take(NT * (D + 2)).rearrange("p (i c) -> p i c", i=NT)
    parts = a.take(4 * 3 * N // 2).bitcast(BF16).rearrange("p (s a n) -> p s a n", s=4, a=3)
    rest = a.take(2 * N).rearrange("p (s n) -> p s n", s=2)
    wqk = a.take(2 * KD * D).rearrange("p (w k n) -> p w k n", w=2, k=KD)
    wv = a.take(KD * D).rearrange("p (k n) -> p k n", k=KD)
    sc2 = a.take(NT * 2).rearrange("p (i g) -> p i g", i=NT)
    assert a.at <= mem.V_at

    ids_in, w_in, const_in = sem("ids_in"), sem("w_in"), sem("const_in")
    gathered = [sem(f"gathered{c}") for c in range(4)]
    step, var_ready, sd_ready = sem("a_step"), sem("a_var"), sem("a_sd")
    xn_ready, turned, xT_ready = sem("a_xn"), sem("a_turned"), sem("a_xT")
    qk_ps, v_ps, part1, rest_ok, part2, part3 = (sem("a_" + n) for n in ("qk_ps", "v_ps", "part1", "rest", "part2", "part3"))
    filled = sem("a_filled")
    v_kept, h_ready, stats_done, means_done = sem("a_v_kept"), sem("a_h"), sem("a_stats"), sem("a_means")
    stored = [sem(f"a_stored{i}") for i in range(4)]
    NP = 16

    with nc.Block() as block:
        @block.sync
        def _(sp):
            sp.dma_start(mem.ids[:, :], io["ids"]).then_inc(ids_in, 16)
            sp.dma_start(mem.const[:, :], io["const"]).then_inc(const_in, 16)
            sp.dma_start(wqk[:, 0, :, :], io["wq"]).then_inc(w_in, 16)
            sp.dma_start(wqk[:, 1, :, :], io["wk"]).then_inc(w_in, 16)
            sp.dma_start(wv, io["wv"]).then_inc(w_in, 16)
            sp.dma_start(mem.wo, io["wo"]).then_inc(w_in, 16)
            sp.dma_start(mem.bo, io["bo"].partition_broadcast(P)).then_inc(w_in, 16)
            sp.wait_ge(const_in, 16)
            pad = mem.const[:, K_PAD:K_PAD + ROW]
            for rows, n in ((mem.rows0[T:, :], NRT), (mem.rows1, NRT)):
                sp.dma_start(rows.rearrange("(j p) c -> p j c", p=P),
                             pad[:, None, :].broadcast_to([P, n, ROW])).then_inc(mem.pads_in, 16)
            for n in range(NP):
                c, w, o = n // 4, (n // 2) % 2, n % 2
                sp.wait_ge(part3, n + 1)
                b, t0 = c // 2, (c % 2) * N
                dst = mem.qk_dram[w, :, b * D + o * P:b * D + (o + 1) * P, t0:t0 + N]
                sp.dma_start(dst.rearrange("a p t -> p a t"), parts[:, n % 4, :, :]).then_inc(stored[n % 4], 16)
            for i in range(4):
                sp.wait_ge(stored[i], 16 * NP // 4)
            sp.wait_ge(w_in, 16 * 5)
            sp.wait_ge(mem.pads_in, 32)

        @block.gpsimd
        def _(pool):
            nc.gpsimd.memset(mem.KO[KROWS:KMAX, :, :, :], 1.0).then_inc(filled, 1)
            pool.wait_ge(filled, 1)
            nc.gpsimd.memset(mem.vst[:, :, :, :, DH:DH + 1], 1.0).then_inc(filled, 1)
            pool.wait_ge(filled, 2)
            nc.gpsimd.memset(mem.vst[:, :, :, :, DH + 1:32], 0.0).then_inc(filled, 1)
            pool.wait_ge(filled, 3)
            nc.gpsimd.memset(mem.MP[:, :, :], 0.0).then_inc(filled, 1)
            pool.wait_ge(ids_in, 16)
            for i in range(NT):
                nc.gpsimd.indirect_dma_start(
                    out=emb[:, i, :], out_offset=None, in_=io["tok"],
                    in_offset=bass.IndirectOffsetOnAxis(ap=mem.ids[:, i:i + 1].bitcast(U32), axis=0),
                    bounds_check=VOCAB - 1, oob_is_err=False).then_inc(gathered[i // 4], 16)

        @block.vector
        def _(dve):
            link = step_counter(dve, step)
            dve.wait_ge(const_in, 16)
            nc.vector.tensor_copy(mem.ident_bf[:, :], mem.ident)
            nc.vector.memset(mem.ones_bf[:, :], 1.0)
            nc.vector.memset(mem.zero_bf[:, :], 0.0)
            nc.vector.memset(mem.ones[:, :], 1.0)
            nc.vector.tensor_copy(mem.tri_bf[:, :], mem.const[:, K_TRI:K_TRI + P])
            for c in range(4):
                g = slice(4 * c, 4 * c + 4)
                dve.wait_ge(gathered[c], 64)
                nc.vector.tensor_scalar(sc2[:, g, :], emb[:, g, D:D + 2], 1e-8, 2.0, ALU.max, ALU.mult).then_inc(h_ready, 1)
                nc.vector.tensor_scalar(emb[:, g, 0:D], emb[:, g, 0:D], 0.0, 0.5, ALU.is_ge, ALU.subtract).then_inc(h_ready, 1)
                dve.wait_ge(h_ready, 3 * c + 2)
                nc.vector.tensor_tensor(
                    mem.h[:, g, :].rearrange("p i (g c) -> p i g c", g=2),
                    emb[:, g, 0:D].rearrange("p i (g c) -> p i g c", g=2),
                    sc2[:, g, :, None].broadcast_to([P, 4, 2, P]), ALU.mult).then_inc(h_ready, 1)

            def tile_of_h(i):
                if i % 4 == 0:
                    dve.wait_ge(h_ready, 3 * (i // 4) + 3)

            norm_stats(nc, dve, link, mem, stats_done, means_done, tile_of_h, var_ready, sd_ready)
            norm_apply(nc, mem, xn_ready)

            def third_part(n):
                dve.wait_ge(part2, n + 1)
                nc.vector.tensor_tensor(parts[:, n % 4, 2, :], rest[:, n % 2, :], parts[:, n % 4, 1, :],
                                        ALU.subtract).then_inc(part3, 1)

            for n in range(NP):
                dve.wait_ge(part1, n + 1)
                if n >= 2:
                    dve.wait_ge(part3, n - 1)
                nc.vector.scalar_tensor_tensor(rest[:, n % 2, :], mem.ps[:, n % 4, :], 0.25 if (n // 2) % 2 == 0 else 1.0,
                                               parts[:, n % 4, 0, :], ALU.mult, ALU.subtract).then_inc(rest_ok, 1)
                if n >= 1:
                    third_part(n - 1)
                if n % 2 == 1:
                    j = n // 2
                    dve.wait_ge(v_ps, j + 1)
                    b, c0 = j // 4, 2 * (j % 4)
                    for g in range(NG):
                        nc.vector.tensor_copy(
                            mem.V[:, b * NG + g, c0:c0 + 2, :],
                            mem.ps[:, 4 + j % 4, :].rearrange("p (c x) -> p c x", c=2)[:, :, g * 64:(g + 1) * 64],
                        ).then_inc(v_kept, 1)
            third_part(NP - 1)

        @block.scalar
        def _(act):
            norm_root(nc, act, mem, var_ready, sd_ready)
            keep_turned(nc, act, mem, turned, xT_ready)

            def second_part(n):
                act.wait_ge(rest_ok, n + 1)
                nc.scalar.activation(parts[:, n % 4, 1, :], rest[:, n % 2, :], ACT.Copy).then_inc(part2, 1)

            for n in range(NP):
                act.wait_ge(qk_ps, n + 1)
                if n >= 4:
                    act.wait_ge(stored[n % 4], 16 * (n // 4))
                nc.scalar.activation(parts[:, n % 4, 0, :], mem.ps[:, n % 4, :], ACT.Copy,
                                     scale=0.25 if (n // 2) % 2 == 0 else 1.0).then_inc(part1, 1)
                if n >= 1:
                    second_part(n - 1)
            second_part(NP - 1)

        @block.tensor
        def _(pe):
            pe.wait_ge(const_in, 16)
            transpose_rows(nc, pe, mem, lambda i, k: mem.xw[:, i, k * P:(k + 1) * P],
                           lambda i: pe.wait_ge(xn_ready, i + 1), turned)
            pe.wait_ge(xT_ready, 8)
            pe.wait_ge(w_in, 16 * 5)
            for n in range(NP):
                c, w, o = n // 4, (n // 2) % 2, n % 2
                if n >= 4:
                    pe.wait_ge(rest_ok, n - 3)
                for k in range(KD):
                    ins = nc.tensor.matmul(mem.ps[:, n % 4, :], wqk[:, w, k, o * P:(o + 1) * P],
                                           mem.xT[:, k, c * N:(c + 1) * N], start=(k == 0), stop=(k == KD - 1))
                ins.then_inc(qk_ps, 1)
                if n % 2 == 1:
                    j = n // 2
                    if j >= 4:
                        pe.wait_ge(v_kept, NG * (j - 3))
                    for i in (2 * j, 2 * j + 1):
                        for k in range(KD):
                            ins = nc.tensor.matmul(mem.ps[:, 4 + j % 4, (i % 2) * D:(i % 2 + 1) * D],
                                                   mem.xT[:, k, i * P:(i + 1) * P], wv[:, k, :],
                                                   start=(k == 0), stop=(k == KD - 1))
                    ins.then_inc(v_ps, 1)



def stage_attention(nc, mem, sem):
    qk_in = [sem(f"b_qk_in{s}") for s in range(3)]
    row_out = sem("b_row_out")
    row_in = [sem(f"b_row_in{q}") for q in range(2)]
    st_ready, exp_done, pv_done = (sem("b_" + n) for n in ("st", "exp", "pv"))
    ms_ready, ms_free, nm_ready, mp_step, mt_ready, mt_kept = (
        sem("b_" + n) for n in ("ms", "ms_free", "nm", "mp", "mt", "mt_kept"))
    v_staged, po_ready, outT_ready, norm_step, norm_done = (
        sem("b_" + n) for n in ("v_staged", "po", "outT", "norm_step", "norm"))
    UH = 2 * QT
    MH = HG * 4 * 2
    QO, KO = mem.QO, mem.KO

    def halves(it):
        return ((it, 0), (it, 1))

    def iterations(body, engine):
        body(0, 0)
        with engine.Fori(0, 2) as r:
            for s in (1, 2, 3):
                body(3 * r + s, s % 3)
        body(NIT - 1, (NIT - 1) % 3, last=True)

    with nc.Block() as block:
        @block.sync
        def _(sp):
            def load(it):
                for w, X, PARTS in ((0, QO, Q_PARTS), (1, KO, K_PARTS)):
                    for j, part in enumerate(PARTS):
                        src = mem.qk_dram[w, part, it * 64:(it + 1) * 64, :].rearrange("(h d) t -> d h t", h=HG)
                        sp.dma_start(X[16 * j:16 * j + 16, it % 3, :, :], src).then_inc(qk_in[it % 3], 16)

            def max_rows(G):
                it, qb = G // 2, G % 2
                sp.wait_ge(mt_kept, G + 1)
                if G >= 2:
                    sp.wait_ge(row_in[qb], 16 * (G // 2))
                sp.dma_start(mem.row_dram[qb], mem.mTs[0:48, qb, :]).then_inc(row_out, 16)
                sp.wait_ge(row_out, 16 * (G + 1))
                sp.dma_start(QO[KROWS:KMAX, it % 3, :, qb * N:(qb + 1) * N],
                             mem.row_dram[qb].rearrange("(a h q) p -> a h (q p)", a=3, h=HG)).then_inc(row_in[qb], 16)

            load(0)
            load(1)
            max_rows(0)
            max_rows(1)
            for it in range(NIT):
                if it + 2 < NIT:
                    if it >= 1:
                        sp.wait_ge(pv_done, 2 * UH * it)
                    load(it + 2)
                for G in (2 * it + 2, 2 * it + 3):
                    if G < 2 * NIT:
                        max_rows(G)

        @block.gpsimd
        def _(pool):
            def max_parts(G, qb):
                pool.wait_ge(nm_ready, G + 1)
                if not (type(G) is int and G < 2):
                    pool.wait_ge(mt_ready, G - 1)
                nm = mem.NM[:, qb, :]
                mp = mem.MP[:, qb:qb + 1, 0:48].rearrange("p o (a c) -> p o a c", a=3)
                nc.gpsimd.tensor_copy(mp[:, 0, 0, :], nm).then_inc(mp_step, 1)
                pool.wait_ge(mp_step, 4 * G + 1)
                nc.gpsimd.tensor_tensor(mem.mr[:, qb, :], nm, mp[:, 0, 0, :], ALU.subtract).then_inc(mp_step, 1)
                pool.wait_ge(mp_step, 4 * G + 2)
                nc.gpsimd.tensor_copy(mp[:, 0, 1, :], mem.mr[:, qb, :]).then_inc(mp_step, 1)
                pool.wait_ge(mp_step, 4 * G + 3)
                nc.gpsimd.tensor_tensor(mp[:, 0, 2, :], mem.mr[:, qb, :], mp[:, 0, 1, :],
                                        ALU.subtract).then_inc(mp_step, 1)

            def stage_v(it, slot):
                nc.gpsimd.tensor_copy(mem.vst[:, slot, :, :, 0:DH],
                                      mem.V[:, bass.ds(it, 1), :, :].rearrange("p o c (h d) -> p (o c) h d", h=HG),
                                      ).then_inc(v_staged, 1)

            def body(it, s, last=False):
                if not last:
                    pool.wait_ge(pv_done, UH * (2 * it + 1))
                    stage_v(it + 1, (s + 1) % 3)
                    max_parts(2 * it + 2, 0)
                    max_parts(2 * it + 3, 1)

            stage_v(0, 0)
            max_parts(0, 0)
            max_parts(1, 1)
            nc.gpsimd.tensor_tensor(mem.h[:, :, :], mem.h[:, :, :],
                                    mem.bo[:, None, :].broadcast_to([P, NT, D]), ALU.add)
            for it in range(NIT):
                body(it, it % 3, last=(it == NIT - 1))

        @block.scalar
        def _(act):
            def keep_rows(G, qb, bank):
                act.wait_ge(mt_ready, G + 1)
                if not (type(G) is int and G < 2):
                    act.wait_ge(row_out, 16 * (G - 1))
                nc.scalar.activation(mem.mTs[0:48, qb, :],
                                     mem.ps[0:48, bank, 0:64].bitcast(BF16), ACT.Copy).then_inc(mt_kept, 1)

            def keep_out(half, qb):
                act.wait_ge(pv_done, UH * (half + 1))
                if not (type(half) is int and half < 2):
                    act.wait_ge(outT_ready, half - 1)
                nc.scalar.activation(mem.po[:, qb, :], mem.ps[:, 6 + qb, :], ACT.Copy).then_inc(po_ready, 1)

            def body(it, s, last=False):
                for qb in (0, 1):
                    for u in range(UH):
                        U = 2 * UH * it + UH * qb + u
                        act.wait_ge(st_ready, U + 1)
                        if not (type(it) is int and U < 4):
                            act.wait_ge(pv_done, U - 3)
                        nc.scalar.activation(mem.e[:, u % 4, :], mem.ps[:, 2 * (u % 2):2 * (u % 2) + 2, :],
                                             ACT.Exp).then_inc(exp_done, 1)
                        if u == 1 and not (type(it) is int and it == 0 and qb == 0):
                            keep_out(2 * it + qb - 1, 1 - qb)
                        if u == 7:
                            if not (last and qb == 1) and not (type(it) is int and it == 0 and qb == 0):
                                keep_rows(2 * it + qb + 1, 1 - qb, 7 - qb)

            keep_rows(0, 0, 6)
            keep_rows(1, 1, 7)
            iterations(body, nc.scalar)
            keep_out(2 * NIT - 1, 1)

        @block.vector
        def _(dve):
            def row_max(G, qb, mb):
                if mb == 0 and not (type(G) is int and G < 2):
                    dve.wait_ge(nm_ready, G - 1)
                dve.wait_ge(ms_ready, MH * G + mb + 1)
                hh, qt, kh = mb // 8, (mb // 2) % 4, mb % 2
                nc.vector.tensor_reduce(mem.MX[:, qb, hh, qt, kh:kh + 1], mem.ps[:, 4 + mb % 2, :],
                                        AX.X, ALU.max).then_inc(ms_free, 1)

            def negate_max(G, qb):
                dve.wait_ge(ms_free, MH * (G + 1))
                if not (type(G) is int and G < 2):
                    dve.wait_ge(mp_step, 4 * (G - 1))
                nc.vector.tensor_reduce(mem.NM[:, qb, :], mem.MX[:, qb, :, :, :].rearrange("p h q k -> p (h q) k"),
                                        AX.X, ALU.max, negate=True).then_inc(nm_ready, 1)

            def normalise(half, it, qb):
                dve.wait_ge(outT_ready, half + 1)
                if not (type(half) is int and half < 1):
                    dve.wait_ge(norm_done, half)
                o = mem.ps[:, 6 + qb, :].rearrange("p (q h c) -> p q h c", q=4, h=HG)
                nc.vector.tensor_scalar(mem.den[:, :].rearrange("p (q h) -> p q h", q=4), o[:, :, :, DH],
                                        DEN_EPS, None, ALU.add).then_inc(norm_step, 1)
                dve.wait_ge(norm_step, 2 * half + 1)
                nc.vector.reciprocal(mem.den[:, :], mem.den[:, :]).then_inc(norm_step, 1)
                dve.wait_ge(norm_step, 2 * half + 2)
                nc.vector.tensor_tensor(
                    mem.ao[:, bass.ds(it // 2, 1), 4 * qb:4 * qb + 4, bass.ds((it % 2) * 64, 64)].rearrange(
                        "p o q (h d) -> p (o q) h d", h=HG),
                    o[:, :, :, 0:DH],
                    mem.den[:, :].rearrange("p (q h) -> p q h", q=4)[:, :, :, None].broadcast_to([P, 4, HG, DH]),
                    ALU.mult).then_inc(norm_done, 1)

            def body(it, s, last=False):
                for qb in (0, 1):
                    first = type(it) is int and it == 0 and qb == 0
                    for u in range(UH):
                        if not last:
                            row_max(2 * it + 2 + qb, qb, 2 * u)
                            row_max(2 * it + 2 + qb, qb, 2 * u + 1)
                        if u == 1 and not first and not (last and qb == 1):
                            negate_max(2 * it + qb + 1, 1 - qb)
                        if u == 12 and not first:
                            normalise(2 * it + qb - 1, it if qb == 1 else it - 1, 1 - qb)

            for G in (0, 1):
                for mb in range(MH):
                    row_max(G, G, mb)
                negate_max(G, G)
            iterations(body, nc.vector)
            normalise(2 * NIT - 1, NIT - 1, 1)

        @block.tensor
        def _(pe):
            def score_block(G, qb, s, mb, first=False):
                if not first:
                    pe.wait_ge(ms_free, MH * G + mb - 1)
                hh, qt, kh = mb // 8, (mb // 2) % 4, mb % 2
                q0 = qb * N + qt * P
                nc.tensor.matmul(mem.ps[:, 4 + mb % 2, :], QO[0:KROWS, s, hh, q0:q0 + P],
                                 KO[0:KROWS, s, hh, kh * N:(kh + 1) * N], start=True, stop=True).then_inc(ms_ready, 1)

            def turn_max(G, qb, bank):
                pe.wait_ge(mp_step, 4 * G + 4)
                nc.tensor.transpose(mem.ps[:, bank, 0:64].bitcast(BF16), mem.MP[:, qb, :],
                                    mem.ident_bf[:, :]).then_inc(mt_ready, 1)

            def turn_out(half, G, qb):
                pe.wait_ge(po_ready, half + 1)
                if G is not None:
                    pe.wait_ge(mt_kept, G + 1)
                for q in range(4):
                    ins = nc.tensor.transpose(mem.ps[:, 6 + qb, q * P:(q + 1) * P],
                                              mem.po[:, qb, q * P:(q + 1) * P], mem.ident)
                ins.then_inc(outT_ready, 1)

            def scores_t(it, s, qb, u, wait):
                U = 2 * UH * it + UH * qb + u
                if u == 0:
                    pe.wait_ge(row_in[qb], 16 * (it + 1))
                if wait:
                    pe.wait_ge(exp_done, U - 1)
                kc, pair = u // 2, u % 2
                for j in range(2):
                    hh = 2 * pair + j
                    ins = nc.tensor.matmul(mem.ps[:, 2 * (u % 2) + j, :], KO[0:KMAX, s, hh, kc * P:(kc + 1) * P],
                                           QO[0:KMAX, s, hh, qb * N:(qb + 1) * N], start=True, stop=True)
                ins.then_inc(st_ready, 1)

            def times_v(it, s, qb, u):
                U = 2 * UH * it + UH * qb + u
                pe.wait_ge(exp_done, U + 1)
                kc, pair = u // 2, u % 2
                for j in range(2):
                    hh = 2 * pair + j
                    ins = nc.tensor.matmul(mem.ps[32 * hh:32 * hh + 32, 6 + qb, :], mem.vst[:, s, kc, hh, :],
                                           mem.e[:, u % 4, j * N:(j + 1) * N], start=(kc == 0), stop=(kc == QT - 1))
                ins.then_inc(pv_done, 1)

            def body(it, s, last=False):
                fixed0 = type(it) is int and it == 0
                for qb in (0, 1):
                    first = fixed0 and qb == 0
                    for u in range(UH):
                        if u < UH - 1:
                            scores_t(it, s, qb, u + 1, not (first and u == 0))
                        elif qb == 0:
                            scores_t(it, s, 1, 0, True)
                        elif not last:
                            scores_t(it + 1, (s + 1) % 3, 0, 0, True)
                        if not last:
                            if qb == 0 and u == 0:
                                pe.wait_ge(qk_in[(s + 1) % 3], slot_value(it, s))
                            score_block(2 * it + 2 + qb, qb, (s + 1) % 3, 2 * u)
                            score_block(2 * it + 2 + qb, qb, (s + 1) % 3, 2 * u + 1)
                        if u == 0:
                            if qb == 0:
                                pe.wait_ge(v_staged, it + 1)
                            if fixed0:
                                pe.wait_ge(mt_kept, qb + 1)
                            else:
                                pe.wait_ge(norm_done, 2 * it + qb - 1)
                        if u == 5 and not first and not (last and qb == 1):
                            pe.wait_ge(po_ready, 2 * it + qb)
                            turn_max(2 * it + qb + 1, 1 - qb, 7 - qb)
                        if u == 9 and not first:
                            turn_out(2 * it + qb - 1, None if (last and qb == 1) else 2 * it + qb + 1, 1 - qb)
                        times_v(it, s, qb, u)

            def slot_value(it, s):
                if type(it) is int:
                    return 192 * ((it + 1) // 3 + 1)
                return slot_fill[s]

            slot_fill = {}
            pe.wait_ge(qk_in[0], 192)
            for G in (0, 1):
                for mb in range(MH):
                    score_block(G, G, 0, mb, first=(G == 0 and mb < 2))
                turn_max(G, G, 6 + G)
            scores_t(0, 0, 0, 0, False)
            body(0, 0)
            with nc.tensor.Fori(0, 2) as r:
                for s in (1, 2, 3):
                    slot_fill[s % 3] = 192 * (r + ((s + 1) // 3) + 1)
                    body(3 * r + s, s % 3)
            body(NIT - 1, (NIT - 1) % 3, last=True)
            turn_out(2 * NIT - 1, None, 1)



def project_and_add(nc, pe, mem, aT, w, start, done):
    for i in range(NT):
        start(i)
        for k in range(KD):
            ins = nc.tensor.matmul(mem.ps[:, i // 2, (i % 2) * D:(i % 2 + 1) * D], aT[:, k, i * P:(i + 1) * P],
                                   w[:, k, :], start=(k == 0), stop=(k == KD - 1))
        ins.then_inc(done, 1)


def add_projection(nc, dve, mem, projected, h_ready):
    for i in range(NT):
        dve.wait_ge(projected, 2 * (i // 2) + 2)
        nc.vector.tensor_tensor(mem.h[:, i, :], mem.ps[:, i // 2, (i % 2) * D:(i % 2 + 1) * D],
                                mem.h[:, i, :], ALU.add).then_inc(h_ready, 1)


def stage_router(nc, mem, io, sem, layer):
    t = f"c{layer}_"
    if layer == 0:
        a = Arena(mem.arena, mem.aoT_at)
        aT = a.take(KD * T).rearrange("p (k t) -> p k t", k=KD)
        w_out, n_shared, rows = mem.wo, NT, mem.rows0
    else:
        aT, w_out, n_shared, rows = mem.xT, mem.w_out, 0, mem.rows1
    a = Arena(mem.arena, mem.aoT_at + KD * T if layer == 0 else 0)
    cmp = a.take(2 * NT * NE * NE).rearrange("p (s n) -> p s n", s=2)
    acc, gate, gate_in = mem.acc[layer], mem.gate, sem(t + "gate_in")
    turned0, kept0, projected, h_ready = (sem(t + n) for n in ("turned0", "kept0", "projected", "h"))
    step, stats_done, means_done = (sem(t + n) for n in ("step", "stats", "means"))
    var_ready, sd_ready, xn_ready, turned, xT_ready = (sem(t + n) for n in ("var", "sd", "xn", "turned", "xT"))
    logits, shifted, exped, mask_ready, counted, slots_ready, sent, stored = (
        sem(t + n) for n in ("logits", "shifted", "exped", "mask", "counted", "slots", "sent", "stored"))

    with nc.Block() as block:
        @block.sync
        def _(sp):
            sp.dma_start(gate[:, :, :], io[f"gate{layer}"]).then_inc(gate_in, 16)
            if layer == 0:
                sp.dma_start(mem.gate_b[:, :], io["gate_b"].partition_broadcast(P)).then_inc(gate_in, 16)
                sp.dma_start(mem.w1, io["w1"].rearrange("e p n -> p e n")).then_inc(mem.experts_in, 16)
                sp.dma_start(mem.w2, io["w2"].rearrange("e p n -> p e n")).then_inc(mem.experts_in, 16)
                sp.dma_start(mem.b1, io["b1"].partition_broadcast(P)).then_inc(mem.experts_in, 16)
                sp.dma_start(mem.b2, io["b2"].partition_broadcast(P)).then_inc(mem.experts_in, 16)
            sp.wait_ge(h_ready, NT)
            sp.dma_start(acc[0:T, :].rearrange("(i p) c -> p i c", p=P), mem.h[:, :, :]).then_inc(stored, 16)
            sp.dma_start(acc[T:T + TRASH, :], mem.h[:, 0, :]).then_inc(stored, 16)
            if n_shared:
                sp.wait_ge(slots_ready, 1)
                sp.dma_start(rows[0:T, :].rearrange("(i p) c -> p i c", p=P), mem.xw[:, :, :]).then_inc(stored, 16)
            sp.wait_ge(stored, 48 if n_shared else 32)

        @block.gpsimd
        def _(pool):
            pool.wait_ge(slots_ready, 1)
            for k in range(TOP_K):
                for i in range(NT):
                    nc.gpsimd.indirect_dma_start(
                        out=rows, out_offset=bass.IndirectOffsetOnAxis(ap=mem.slots[:, k, i:i + 1].bitcast(U32), axis=0),
                        in_=mem.xw[:, i, :], in_offset=None,
                        bounds_check=(n_shared + NRT) * P - 1, oob_is_err=False).then_inc(sent, 16)
            pool.wait_ge(sent, 16 * TOP_K * NT)

        @block.scalar
        def _(act):
            if layer == 0:
                for c in range(NT // 4):
                    for k in range(KD):
                        act.wait_ge(turned0, 2 * c + k + 1)
                        nc.scalar.activation(aT[:, k, c * N:(c + 1) * N], mem.ps[:, 2 * c + k, :],
                                             ACT.Copy).then_inc(kept0, 1)
            norm_root(nc, act, mem, var_ready, sd_ready)
            keep_turned(nc, act, mem, turned, xT_ready)
            act.wait_ge(shifted, 1)
            nc.scalar.activation(mem.lg[:, :], mem.lg[:, :], ACT.Exp).then_inc(exped, 1)

        @block.vector
        def _(dve):
            link = step_counter(dve, step)
            const = mem.const
            add_projection(nc, dve, mem, projected, h_ready)
            norm_stats(nc, dve, link, mem, stats_done, means_done, lambda i: dve.wait_ge(h_ready, i + 1),
                       var_ready, sd_ready)
            norm_apply(nc, mem, xn_ready)
            tok = mem.xw[:, :, :].rearrange("p i c -> p (i c)").bitcast(I32).rearrange("p (i c) -> p i c", i=NT)
            nc.vector.tensor_copy(tok[:, :, C_ID], const[:, K_TOK:K_TOK + NT])
            nc.vector.tensor_copy(mem.xw[:, :, C_W + NE:C_W + NE + 1], mem.ones[:, 0:NT, None])

            lg = mem.lg[:, :].rearrange("p (i e) -> p i e", i=NT)
            dve.wait_ge(gate_in, 32 if layer == 0 else 16)
            dve.wait_ge(logits, 1)
            l_ps = mem.ps[:, 0, 0:NT * NE].rearrange("p (i e) -> p i e", i=NT)
            if layer == 0:
                link(nc.vector.tensor_tensor(lg, l_ps, mem.gate_b[:, None, :].broadcast_to([P, NT, NE]), ALU.add))
            else:
                link(nc.vector.tensor_copy(lg, l_ps))
            link(nc.vector.tensor_reduce(mem.s16[:, :], lg, AX.X, ALU.max))
            link(nc.vector.tensor_tensor(lg, lg, mem.s16[:, :, None].broadcast_to([P, NT, NE]), ALU.subtract))
            nc.vector.memset(mem.r2[:, :], 0.0).then_inc(shifted, 1)
            dve.wait_ge(exped, 1)
            link(nc.vector.tensor_reduce(mem.s16[:, :], lg, AX.X, ALU.add))
            link(nc.vector.reciprocal(mem.s16[:, :], mem.s16[:, :]))
            link(nc.vector.tensor_tensor(lg, lg, mem.s16[:, :, None].broadcast_to([P, NT, NE]), ALU.mult))

            over_e = lg[:, :, None, :].broadcast_to([P, NT, NE, NE])
            own = lg[:, :, :, None].broadcast_to([P, NT, NE, NE])
            gt = cmp[:, 0, :].rearrange("p (i e f) -> p i e f", i=NT, e=NE)
            eq = cmp[:, 1, :].rearrange("p (i e f) -> p i e f", i=NT, e=NE)
            lower = const[:, K_LT:K_LT + NE * NE].rearrange("p (e f) -> p e f", e=NE)
            link(nc.vector.tensor_tensor(gt, over_e, own, ALU.is_gt))
            link(nc.vector.tensor_tensor(eq, over_e, own, ALU.is_equal))
            link(nc.vector.tensor_tensor(eq, eq, lower[:, None, :, :].broadcast_to([P, NT, NE, NE]), ALU.mult))
            link(nc.vector.tensor_tensor(gt, gt, eq, ALU.add))
            rank = mem.rank[:, :].rearrange("p (i e) -> p i e", i=NT)
            link(nc.vector.tensor_reduce(rank, gt, AX.X, ALU.add))
            mask = mem.mask[:, 2, :].rearrange("p (i e) -> p i e", i=NT)
            link(nc.vector.tensor_scalar(mem.mask_bf[:, :], mem.rank[:, :], float(TOP_K), None, ALU.is_lt))
            nc.vector.tensor_scalar(mem.mask[:, 2, :], mem.rank[:, :], float(TOP_K), None, ALU.is_lt).then_inc(mask_ready, 1)
            for k in range(TOP_K):
                link(nc.vector.tensor_scalar(mem.mask[:, k, :], mem.rank[:, :], float(k), None, ALU.is_equal))
            cw = mem.xw[:, :, C_W:C_W + NE]
            dve.wait_ge(mask_ready, 1)
            link(nc.vector.tensor_tensor(cw, lg, mask, ALU.mult))
            if layer == 1:
                link(nc.vector.tensor_reduce(mem.s16[:, :], cw, AX.X, ALU.add))
                link(nc.vector.reciprocal(mem.s16[:, :], mem.s16[:, :]))
                link(nc.vector.tensor_tensor(cw, cw, mem.s16[:, :, None].broadcast_to([P, NT, NE]), ALU.mult))

            dve.wait_ge(counted, 1)
            j128 = const[:, K_J128:K_J128 + NT]
            c128 = cmp[:, 0, 0:NE * NT].rearrange("p (e j) -> p e j", e=NE)
            n_of = mem.ps[:, 2, 0:NE]
            small = mem.small
            tiles, base, has, order = small[:, 0, :], small[:, 1, :], small[:, 2, :], small[:, 3, :]
            link(nc.vector.tensor_copy(small[:, 4, :], n_of))
            link(nc.vector.tensor_tensor(c128, small[:, 4, :, None].broadcast_to([P, NE, NT]),
                                         j128[:, None, :].broadcast_to([P, NE, NT]), ALU.is_gt))
            link(nc.vector.tensor_reduce(tiles, c128, AX.X, ALU.add))
            ee = cmp[:, 1, 0:NE * NE].rearrange("p (e f) -> p e f", e=NE)
            link(nc.vector.tensor_tensor(ee, tiles[:, None, :].broadcast_to([P, NE, NE]), lower, ALU.mult))
            link(nc.vector.tensor_reduce(base, ee, AX.X, ALU.add))

            slotm = mem.rank[:, :].rearrange("p (i e) -> p i e", i=NT)
            link(nc.vector.scalar_tensor_tensor(slotm, base[:, None, :].broadcast_to([P, NT, NE]), float(P),
                                                mem.ps[:, 1, 0:NT * NE].rearrange("p (i e) -> p i e", i=NT),
                                                ALU.mult, ALU.add))
            for k in range(TOP_K):
                sel = mem.mask[:, k, :]
                link(nc.vector.tensor_tensor(sel, sel, mem.rank[:, :], ALU.mult))
                link(nc.vector.tensor_reduce(mem.s16[:, :], sel.rearrange("p (i e) -> p i e", i=NT), AX.X, ALU.add))
                link(nc.vector.tensor_scalar(mem.slots[:, k, :], mem.s16[:, :], float(n_shared * P), None, ALU.add))
            nc.vector.memset(mem.r2[:, :], 0.0).then_inc(slots_ready, 1)

            jj = const[:, K_J:K_J + NRT]
            ge = cmp[:, 0, 0:NRT * NE].rearrange("p (j e) -> p j e", j=NRT)
            tf = mem.tf
            link(nc.vector.tensor_tensor(ge, jj[:, :, None].broadcast_to([P, NRT, NE]),
                                         base[:, None, :].broadcast_to([P, NRT, NE]), ALU.is_ge))
            link(nc.vector.tensor_reduce(tf[:, 0, :], ge, AX.X, ALU.add))
            if layer == 0:
                nc.vector.memset(mem.tab[:, 0, 0:NT], NE)
            link(nc.vector.tensor_scalar(mem.tab[:, 0, n_shared:n_shared + NRT], tf[:, 0, :], -1.0, None, ALU.add))
            if layer == 1:
                link(nc.vector.tensor_scalar(has, tiles, 0.0, None, ALU.is_gt))
                link(nc.vector.tensor_tensor(ge, ge, has[:, None, :].broadcast_to([P, NRT, NE]), ALU.mult))
                link(nc.vector.tensor_reduce(tf[:, 1, :], ge, AX.X, ALU.add))
                link(nc.vector.tensor_scalar(mem.tab[:, 1, 0:NRT], tf[:, 1, :], 32.0, None, ALU.mult))
                link(nc.vector.tensor_scalar(mem.tab[:, 3, 0:NRT], tf[:, 1, :], 1.0, None, ALU.subtract))
                link(nc.vector.tensor_scalar(mem.tab[:, 2, 0:NRT], mem.tab[:, 3, 0:NRT], 1, None, ALU.bitwise_and))
                link(nc.vector.tensor_tensor(ee, has[:, None, :].broadcast_to([P, NE, NE]), lower, ALU.mult))
                link(nc.vector.tensor_reduce(order, ee, AX.X, ALU.add))
                place = const[:, K_J:K_J + NE]
                at = cmp[:, 0, 0:NE * NE].rearrange("p (o e) -> p o e", o=NE)
                link(nc.vector.tensor_tensor(at, place[:, :, None].broadcast_to([P, NE, NE]),
                                             order[:, None, :].broadcast_to([P, NE, NE]), ALU.is_equal))
                link(nc.vector.tensor_tensor(at, at, has[:, None, :].broadcast_to([P, NE, NE]), ALU.mult))
                link(nc.vector.tensor_tensor(ee, at, place[:, None, :].broadcast_to([P, NE, NE]), ALU.mult))
                link(nc.vector.tensor_reduce(small[:, 4, :], ee, AX.X, ALU.add))
                link(nc.vector.tensor_copy(mem.places[:, 0, :], small[:, 4, :]))
                link(nc.vector.tensor_scalar(small[:, 5, :], base, -float(NRT), None, ALU.add))
                link(nc.vector.tensor_tensor(ee, at, small[:, 5, None, :].broadcast_to([P, NE, NE]), ALU.mult))
                link(nc.vector.tensor_reduce(small[:, 4, :], ee, AX.X, ALU.add))
                link(nc.vector.tensor_scalar(mem.places[:, 1, :], small[:, 4, :], float(NRT + 1), None, ALU.add))

        @block.tensor
        def _(pe):
            if layer == 0:
                def attended(i, k):
                    return mem.ao[:, (i // QT) * KD + k, i % QT, :]

                transpose_rows(nc, pe, mem, attended, lambda i: None, turned0)
                pe.wait_ge(kept0, 8)
            project_and_add(nc, pe, mem, aT, w_out, lambda i: None, projected)
            transpose_rows(nc, pe, mem, lambda i, k: mem.xw[:, i, k * P:(k + 1) * P],
                           lambda i: pe.wait_ge(xn_ready, i + 1), turned)
            pe.wait_ge(xT_ready, 8)
            pe.wait_ge(gate_in, 32 if layer == 0 else 16)
            for i in range(NT):
                for k in range(KD):
                    ins = nc.tensor.matmul(mem.ps[:, 0, i * NE:(i + 1) * NE], mem.xT[:, k, i * P:(i + 1) * P],
                                           gate[:, k, :], start=(k == 0), stop=(k == KD - 1))
            ins.then_inc(logits, 1)
            pe.wait_ge(mask_ready, 1)
            nc.tensor.matmul(mem.ps[:, 1, 0:NT * NE], mem.zero_bf, mem.mask_bf, start=True, stop=False)
            for d in range(1, NT):
                nc.tensor.matmul(mem.ps[:, 1, d * NE:NT * NE], mem.ones_bf[:, :], mem.mask_bf[:, 0:(NT - d) * NE],
                                 start=False, stop=False, skip_group_check=True)
            nc.tensor.matmul(mem.ps[:, 1, 0:NT * NE], mem.tri_bf, mem.mask_bf, start=False, stop=True)
            for i in range(NT):
                ins = nc.tensor.matmul(mem.ps[:, 2, 0:NE], mem.ones_bf[:, :], mem.mask_bf[:, i * NE:(i + 1) * NE],
                                       start=(i == 0), stop=(i == NT - 1))
            ins.then_inc(counted, 1)



def stage_experts(nc, mem, io, sem, layer):
    t = f"d{layer}_"
    if layer == 0:
        F, n_tiles, rows = F0, NT + NRT, mem.rows0
        a = Arena(mem.arena, mem.tiles0_at)
    else:
        F, n_tiles, rows = F1, NRT, mem.rows1
        a = Arena(mem.arena, 0)
    FT = F // P
    acc = mem.acc[layer]
    xg = a.take(4 * ROW).rearrange("p (s c) -> p s c", s=4)
    meta = a.take(4 * (ROW - D)).rearrange("p (s c) -> p s c", s=4)
    xgT = a.take(2 * D).rearrange("p (s k t) -> p s k t", s=2, k=KD)
    pre = a.take(2 * 2 * F0).rearrange("p (s f) -> p s f", s=2)
    g = a.take(2 * F).rearrange("p (s f) -> p s f", s=2)
    hact = a.take(2 * F).rearrange("p (s f) -> p s f", s=2)
    hT = a.take(2 * F).rearrange("p (s c t) -> p s c t", s=2, c=FT)
    y0 = a.take(2 * D).rearrange("p (s c) -> p s c", s=2)
    y = a.take(4 * D).rearrange("p (s c) -> p s c", s=4)
    if layer == 1:
        assert a.at <= mem.ring_at
    XT, GU = 0, (1, 2) if layer == 0 else (1, 3)
    HT, Y = (3, 4) if layer == 0 else (5, 7)

    loaded = [sem(f"{t}loaded{s}") for s in range(4)]
    xT_ps, xT_kept, gu_ps, pre_ready, g_ready, hact_ready, hT_ps, hT_kept, y_ps, y_step, y_ready, added, w_loaded = (
        sem(t + n) for n in ("xT_ps", "xT_kept", "gu", "pre", "g", "hact", "hT_ps", "hT_kept", "y_ps", "y_step",
                             "y", "added", "w_loaded"))
    meta_kept, h_back, may_add = sem(t + "meta"), sem(t + "h_back"), sem(t + "may_add")
    Y1 = 1

    def steps(body, engine):
        for j in range(HEAD):
            body(j, j % 4)
        with engine.Fori(0, (n_tiles - 2 - HEAD) // 4) as r:
            for u in range(HEAD, HEAD + 4):
                body(4 * r + u, u % 4, r, u)
        for j in range(n_tiles - 2, n_tiles + 1):
            body(j, j % 4)

    HEAD = 5
    assert (n_tiles - 2 - HEAD) % 4 == 0

    def fixed(j):
        return type(j) is int

    with nc.Block() as block:
        @block.sync
        def _(sp):
            if layer == 1:
                sp.sem_inc(y_ps, Y1)
                for o in range(NE):
                    if o >= 2:
                        first = nc.sync.value_load(mem.places[0:1, 1, o - 1:o], min_val=1, max_val=NRT + 1)
                    e = nc.sync.value_load(mem.places[0:1, 0, o:o + 1], min_val=0, max_val=NE - 1)
                    if o >= 2:
                        sp.wait_ge(y_ps, first)
                    sp.dma_start(mem.ring_gu[:, o % 2, :],
                                 io["gu"][bass.ds(e, 1), :, :].rearrange("o p n -> (o p) n")).then_inc(w_loaded, 16)
                    sp.dma_start(mem.ring_dn[:, o % 2, :],
                                 io["dn"][bass.ds(e, 1), :, :].rearrange("o p n -> (o p) n")).then_inc(w_loaded, 16)
                    sp.wait_ge(w_loaded, 32 * (o + 1))
            else:
                sp.sem_inc(y_ps, Y1)
                sp.wait_ge(mem.experts_in, 64)
                sp.wait_ge(added, 16 * n_tiles)
                sp.dma_start(mem.h[:, :, :], acc[0:T, :].rearrange("(i p) c -> p i c", p=P)).then_inc(h_back, 16)
                sp.wait_ge(h_back, 16)

        @block.gpsimd
        def _(pool):
            def load(j, slot, row0):
                nc.gpsimd.dma_start(xg[:, slot, :], rows[row0, :]).then_inc(loaded[slot], 16)

            def body(j, s, r=None, u=None):
                if not fixed(j) or j + 4 < n_tiles:
                    row0 = j * P + 4 * P if fixed(j) else nc.gpsimd.snap(j * P + 4 * P)
                    pool.wait_ge(xT_kept, 2 * j + 2)
                    pool.wait_ge(meta_kept, j + 1)
                    load(j + 4, s, bass.ds(row0, P))
                if not fixed(j) or j >= 1:
                    pool.wait_ge(y_ready, j)
                    if not fixed(j) or j >= 2:
                        pool.wait_ge(added, 16 * j - 16)
                    pool.sem_inc(may_add, 1)
                    nc.gpsimd.indirect_dma_start(
                        out=acc, out_offset=bass.IndirectOffsetOnAxis(
                            ap=meta[:, (s - 1) % 4, C_ID - D:C_ID - D + 1].bitcast(U32), axis=0),
                        in_=y[:, (s - 1) % 4, :], in_offset=None, compute_op=ALU.add).then_inc(added, 16)

            for j in range(4):
                load(j, j, bass.ds(j * P, P))
            for j in range(HEAD):
                body(j, j % 4)
            n_loop = (n_tiles - 4 - HEAD) // 4
            with nc.gpsimd.Fori(0, n_loop) as r:
                for u in range(HEAD, HEAD + 4):
                    body(4 * r + u, u % 4, r, u)
            for j in range(4 * n_loop + HEAD, n_tiles + 1):
                body(j, j % 4)
            pool.wait_ge(added, 16 * n_tiles)

        @block.scalar
        def _(act):
            def body(j, s, r=None, u=None):
                p = s % 2
                if not fixed(j) or j < n_tiles - 1:
                    keep_rows(j + 1, (s + 1) % 4)
                if not fixed(j) or j >= 1:
                    act.wait_ge(hT_ps, j)
                    if not fixed(j) or j >= 3:
                        act.wait_ge(y_ps, j - 2 + Y1)
                    for q in range(0, FT, 4):
                        w = min(4, FT) * P
                        nc.scalar.activation(
                            hT[:, 1 - p, q:q + min(4, FT), :].rearrange("p c t -> p (c t)"),
                            mem.ps[:, HT + q // 4, 0:w], ACT.Copy).then_inc(hT_kept, 1)
                if not fixed(j) or j < n_tiles:
                    if not fixed(j) or j >= 2:
                        act.wait_ge(hact_ready, j - 1)
                    if layer == 0:
                        act.wait_ge(pre_ready, j + 1)
                        nc.scalar.activation(g[:, p, :], pre[:, p, 0:F], ACT.Silu).then_inc(g_ready, 1)
                    else:
                        act.wait_ge(gu_ps, j + 1)
                        for q in range(2):
                            ins = nc.scalar.activation(g[:, p, q * N:(q + 1) * N], mem.ps[:, GU[0] + q, :], ACT.Gelu)
                            ins.then_inc(g_ready, 1)

            def keep_rows(j, s):
                act.wait_ge(xT_ps, j + 1)
                if not fixed(j) or j >= 2:
                    act.wait_ge(gu_ps, j - 1)
                if not fixed(j) or j >= 4:
                    act.wait_ge(added, 16 * j - 48)
                nc.scalar.activation(meta[:, s, 0:NE + 1], xg[:, s, D:C_ID], ACT.Copy).then_inc(xT_kept, 1)
                nc.scalar.activation(xgT[:, s % 2, :, :].rearrange("p k t -> p (k t)"),
                                     mem.ps[:, XT, 0:D], ACT.Copy).then_inc(xT_kept, 1)

            keep_rows(0, 0)
            steps(body, nc.scalar)

        @block.vector
        def _(dve):
            if layer == 0:
                dve.wait_ge(mem.experts_in, 64)

            def keep_token(j, s):
                dve.wait_ge(loaded_value(j, s)[0], loaded_value(j, s)[1])
                if not fixed(j) or j >= 4:
                    dve.wait_ge(added, 16 * j - 48)
                nc.vector.tensor_copy(meta[:, s, NE + 1:NE + 2].bitcast(I32),
                                      xg[:, s, C_ID:C_ID + 1].bitcast(I32)).then_inc(meta_kept, 1)

            fill = {}

            def loaded_value(j, s):
                if fixed(j):
                    return loaded[s], 16 * (j // 4 + 1)
                return loaded[s], fill[s]

            def body(j, s, r=None, u=None):
                p = s % 2
                if r is not None:
                    fill[(s + 1) % 4] = 16 * (r + (u + 1) // 4 + 1)
                if not fixed(j) or j < n_tiles - 1:
                    keep_token(j + 1, (s + 1) % 4)
                if not fixed(j) or j < n_tiles:
                    dve.wait_ge(gu_ps, j + 1)
                    if not fixed(j) or j >= 2:
                        dve.wait_ge(hT_ps, j - 1)
                    if layer == 0:
                        e = nc.vector.value_load(mem.tab[0:1, 0, bass.ds(j, 1)], min_val=0, max_val=NE)
                        nc.vector.tensor_tensor(
                            pre[:, p, :], mem.ps[:, GU[p], :],
                            mem.b1[:, bass.ds(e, 1), :].rearrange("p o f -> p (o f)"), ALU.add).then_inc(pre_ready, 1)
                        dve.wait_ge(g_ready, j + 1)
                        nc.vector.tensor_tensor(hact[:, p, :], g[:, p, :], pre[:, p, F:2 * F],
                                                ALU.mult).then_inc(hact_ready, 1)
                    else:
                        dve.wait_ge(g_ready, 2 * j + 2)
                        nc.vector.tensor_tensor(hact[:, p, :], g[:, p, :],
                                                mem.ps[:, GU[1]:GU[1] + 2, :].rearrange("p a b -> p (a b)"),
                                                ALU.mult).then_inc(hact_ready, 1)
                if not fixed(j) or j >= 1:
                    v = (s - 1) % 4
                    e = nc.vector.value_load(mem.tab[0:1, 0, bass.ds(j - 1, 1)], min_val=0, max_val=NE)
                    dve.wait_ge(y_ps, j + Y1)
                    dve.wait_ge(xT_kept, 2 * j)
                    if not fixed(j) or j >= 5:
                        dve.wait_ge(added, 16 * j - 64)
                    src = mem.ps[:, Y, 0:D]
                    if layer == 0:
                        nc.vector.tensor_tensor(y0[:, 1 - p, :], src,
                                                mem.b2[:, bass.ds(e, 1), :].rearrange("p o f -> p (o f)"),
                                                ALU.add).then_inc(y_step, 1)
                        dve.wait_ge(y_step, j)
                        src = y0[:, 1 - p, :]
                    nc.vector.tensor_scalar(y[:, v, :], src, meta[:, v, bass.ds(e, 1)], None,
                                            ALU.mult).then_inc(y_ready, 1)

            keep_token(0, 0)
            steps(body, nc.vector)

        @block.tensor
        def _(pe):
            if layer == 0:
                pe.wait_ge(mem.experts_in, 64)

            fill = {}

            def turn_rows(j, s):
                pe.wait_ge(loaded[s], 16 * (j // 4 + 1) if fixed(j) else fill[s])
                if not fixed(j) or j >= 1:
                    pe.wait_ge(xT_kept, 2 * j)
                for k in range(KD):
                    ins = nc.tensor.transpose(mem.ps[:, XT, k * P:(k + 1) * P], xg[:, s, k * P:(k + 1) * P], mem.ident)
                ins.then_inc(xT_ps, 1)

            def body(j, s, r=None, u=None):
                p = s % 2
                if r is not None:
                    fill[(s + 1) % 4] = 16 * (r + (u + 1) // 4 + 1)
                if not fixed(j) or j < n_tiles - 1:
                    turn_rows(j + 1, (s + 1) % 4)
                if not fixed(j) or j < n_tiles:
                    pe.wait_ge(xT_kept, 2 * j + 2)
                    if layer == 0:
                        e = nc.tensor.value_load(mem.tab[0:1, 0, bass.ds(j, 1)], min_val=0, max_val=NE)
                        if not fixed(j) or j >= 2:
                            pe.wait_ge(pre_ready, j - 1)
                        w = mem.w1[:, bass.ds(e, 1), :].rearrange("p o (k f) -> p (o k) f", k=KD)
                        for k in range(KD):
                            ins = nc.tensor.matmul(mem.ps[:, GU[p], :], xgT[:, p, k, :], w[:, k, :],
                                                   start=(k == 0), stop=(k == KD - 1))
                    else:
                        o = nc.tensor.value_load(mem.tab[0:1, 2, bass.ds(j, 1)], min_val=0, max_val=1)
                        come = nc.tensor.value_load(mem.tab[0:1, 1, bass.ds(j, 1)], min_val=32, max_val=32 * NE)
                        pe.wait_ge(w_loaded, come)
                        if not fixed(j) or j >= 1:
                            pe.wait_ge(hact_ready, j)
                        w = mem.ring_gu[:, bass.ds(o, 1), :].rearrange("p o (k f) -> p (o k) f", k=KD)
                        for q in range(4):
                            for k in range(KD):
                                ins = nc.tensor.matmul(mem.ps[:, GU[0] + q, :], xgT[:, p, k, :],
                                                       w[:, k, q * N:(q + 1) * N], start=(k == 0), stop=(k == KD - 1))
                    ins.then_inc(gu_ps, 1)
                if not fixed(j) or j >= 1:
                    pe.wait_ge(hact_ready, j)
                    copies = max(1, FT // 4)
                    if not fixed(j) or j >= 2:
                        pe.wait_ge(hT_kept, copies * (j - 1))
                    for c in range(FT):
                        ins = nc.tensor.transpose(mem.ps[:, HT + c // 4, (c % 4) * P:(c % 4 + 1) * P],
                                                  hact[:, 1 - p, c * P:(c + 1) * P], mem.ident)
                    ins.then_inc(hT_ps, 1)
                    tab = 0 if layer == 0 else 2
                    e = nc.tensor.value_load(mem.tab[0:1, tab, bass.ds(j - 1, 1)], min_val=0, max_val=NE if layer == 0 else 1)
                    pe.wait_ge(hT_kept, copies * j)
                    if not fixed(j) or j >= 2:
                        pe.wait_ge(y_step if layer == 0 else y_ready, j - 1)
                    w2 = (mem.w2 if layer == 0 else mem.ring_dn)[:, bass.ds(e, 1), :]
                    w2 = w2.rearrange("p o (c n) -> p (o c) n", c=FT)
                    for c in range(FT):
                        ins = nc.tensor.matmul(mem.ps[:, Y, 0:D], hT[:, 1 - p, c, :], w2[:, c, :],
                                               start=(c == 0), stop=(c == FT - 1))
                    ins.then_inc(y_ps, 1)

            turn_rows(0, 0)
            steps(body, nc.tensor)



def stage_chebyshev(nc, mem, io, sem):
    a = Arena(mem.arena, 0)
    feat = a.take(7 * T).rearrange("p (b t) -> p b t", b=7)
    kq = a.take(KD * T).rearrange("p (o t) -> p o t", o=KD)
    kv = a.take(2 * M * B * P).rearrange("p (o m b c) -> p o m b c", o=2, m=M, b=B)
    w_in = a.take(KD * 3 * D).rearrange("p (k n) -> p k n", k=KD)
    mem.w_out = a.take(KD * D).rearrange("p (k n) -> p k n", k=KD)
    V1 = mem.xw
    BUF = {2: 0, 3: 1, 4: 2, 5: 3, 6: 4, 7: 5, 8: 6, 9: 4, 10: 5}

    w_ready, step, stats_done, means_done = (sem("e_" + n) for n in ("w", "step", "stats", "means"))
    var_ready, sd_ready, xn_ready, turned, xT_ready = (sem("e_" + n) for n in ("var", "sd", "xn", "turned", "xT"))
    kv_ps, kv_taken, q_ps, q_raw, q_taken, x_ready = (sem("e_" + n) for n in ("kv_ps", "kv_taken", "q_ps", "q_raw", "q_taken", "x"))
    square, f_step, f_ready, used, kv_kept, o_kept = (
        sem("e_" + n) for n in ("square", "f_step", "f", "used", "kv_kept", "o_kept"))

    def wait_used(engine, ps, m):
        if m in (9, 10):
            engine.wait_ge(used, 11 * ps + m - 3 + 1)
        elif ps:
            last = {6: 9, 7: 10}.get(m, m)
            engine.wait_ge(used, 11 * (ps - 1) + last + 1)

    with nc.Block() as block:
        @block.sync
        def _(sp):
            sp.dma_start(w_in, io["w_in"]).then_inc(w_ready, 16)
            sp.dma_start(mem.w_out, io["w_out"]).then_inc(w_ready, 16)
            sp.dma_start(mem.beta[:, :, :], io["beta"]).then_inc(w_ready, 16)
            sp.wait_ge(w_ready, 48)

        @block.scalar
        def _(act):
            norm_root(nc, act, mem, var_ready, sd_ready)
            keep_turned(nc, act, mem, turned, xT_ready)
            for i in range(NT):
                act.wait_ge(kv_ps, i + 1)
                nc.scalar.activation(V1[:, i, 0:D], mem.ps[:, i % 8, D:2 * D], ACT.Copy).then_inc(kv_taken, 1)
            for ps in range(4):
                if ps:
                    act.wait_ge(f_ready, 9 * ps)
                for m in (2, 4, 6, 8, 10):
                    half = m // 2
                    if half == 1:
                        if ps == 0:
                            act.wait_ge(x_ready, NT)
                        elif ps == 2:
                            act.wait_ge(x_ready, NT + 8)
                        src = kq[:, ps % 2, :]
                    else:
                        act.wait_ge(f_ready, 9 * ps + half - 1)
                        src = feat[:, BUF[half], :]
                    wait_used(act, ps, m)
                    nc.scalar.activation(feat[:, BUF[m], :], src, ACT.Square).then_inc(square, 1)

        @block.vector
        def _(dve):
            link = step_counter(dve, step)
            norm_stats(nc, dve, link, mem, stats_done, means_done, lambda i: None, var_ready, sd_ready)
            norm_apply(nc, mem, xn_ready)
            dve.wait_ge(w_ready, 48)
            for i in range(NT):
                dve.wait_ge(kv_taken, i + 1)
                k_dst = kq[:, :, i * P:(i + 1) * P]
                nc.vector.tensor_scalar(k_dst, mem.ps[:, i % 8, 0:D].rearrange("p (o d) -> p o d", o=2), 0.25, 1.0,
                                        ALU.mult, ALU.min).then_inc(q_raw, 1)
                dve.wait_ge(q_raw, i + 1)
                nc.vector.tensor_scalar(k_dst, k_dst, -1.0, None, ALU.max).then_inc(x_ready, 1)

            def scale_sum(ps, m):
                dve.wait_ge(used, 11 * ps + m + 1)
                bank = m % 8
                nc.vector.scalar_tensor_tensor(
                    kv[:, ps, m, :, :], mem.ps[:, bank, 0:B * P].rearrange("p (b c) -> p b c", b=B),
                    mem.beta[:, ps, m:m + 1], mem.const[:, None, K_BLOCK:K_BLOCK + P].broadcast_to([P, B, P]),
                    ALU.mult, ALU.mult).then_inc(kv_kept, 1)

            for ps in range(4):
                if ps == 2:
                    dve.wait_ge(used, 22)
                    for n in range(8):
                        dve.wait_ge(q_ps, n + 1)
                        dst = kq[:, n // 4, (n % 4) * N:(n % 4 + 1) * N]
                        nc.vector.tensor_scalar(dst, mem.ps[:, n, :], 0.25, 1.0, ALU.mult, ALU.min).then_inc(q_raw, 1)
                        dve.wait_ge(q_raw, NT + n + 1)
                        nc.vector.tensor_scalar(dst, dst, -1.0, None, ALU.max).then_inc(x_ready, 1)
                x = kq[:, ps % 2, :]
                for m in range(2, M):
                    dst = feat[:, BUF[m], :]
                    if m % 2 == 0:
                        dve.wait_ge(square, 5 * ps + m // 2)
                        nc.vector.tensor_scalar(dst, dst, 2.0, -1.0, ALU.mult, ALU.add).then_inc(f_ready, 1)
                    else:
                        lo, hi = m // 2, m // 2 + 1
                        wait_used(dve, ps, m)
                        if m == 3:
                            dve.wait_ge(x_ready, NT + 8 * (ps // 2))
                        dve.wait_ge(f_ready, 9 * ps + hi - 1)
                        lo_f = x if lo == 1 else feat[:, BUF[lo], :]
                        nc.vector.tensor_tensor(dst, lo_f, feat[:, BUF[hi], :], ALU.mult).then_inc(f_step, 1)
                        dve.wait_ge(f_step, 4 * ps + m // 2)
                        nc.vector.scalar_tensor_tensor(dst, dst, 2.0, x, ALU.mult, ALU.subtract).then_inc(f_ready, 1)
                    if ps < 2 and m >= 3:
                        scale_sum(ps, m - 3)
                if ps < 2:
                    for m in range(M - 3, M):
                        scale_sum(ps, m)
            for n in range(8):
                dve.wait_ge(used, 22 + 11 * (n // 4) + 11)
                nc.vector.tensor_copy(mem.xT[:, n // 4, (n % 4) * N:(n % 4 + 1) * N], mem.ps[:, n, :]).then_inc(o_kept, 1)

        @block.tensor
        def _(pe):
            transpose_rows(nc, pe, mem, lambda i, k: mem.xw[:, i, k * P:(k + 1) * P],
                           lambda i: pe.wait_ge(xn_ready, i + 1), turned)
            pe.wait_ge(xT_ready, 8)
            pe.wait_ge(w_ready, 48)
            for i in range(NT):
                if i >= 8:
                    pe.wait_ge(kv_taken, i - 7)
                    pe.wait_ge(x_ready, i - 7)
                for k in range(KD):
                    ins = nc.tensor.matmul(mem.ps[:, i % 8, :], mem.xT[:, k, i * P:(i + 1) * P], w_in[:, k, D:3 * D],
                                           start=(k == 0), stop=(k == KD - 1))
                ins.then_inc(kv_ps, 1)
            pe.wait_ge(kv_taken, NT)
            pe.wait_ge(x_ready, NT)
            for ps in range(2):
                for m in range(M):
                    n = 11 * ps + m
                    if m >= 8:
                        pe.wait_ge(kv_kept, n - 7)
                    elif ps == 1:
                        pe.wait_ge(kv_kept, m + 8 + 1 if m < 3 else m + 1)
                    if m >= 2:
                        pe.wait_ge(f_ready, 9 * ps + m - 1)
                    for i in range(NT):
                        lhs = mem.ones[:, 0:P] if m == 0 else (kq[:, ps, i * P:(i + 1) * P] if m == 1 else
                                                               feat[:, BUF[m], i * P:(i + 1) * P])
                        b = i // QT
                        ins = nc.tensor.matmul(mem.ps[:, m % 8, b * P:(b + 1) * P], lhs, V1[:, i, ps * P:(ps + 1) * P],
                                               start=(i % QT == 0), stop=(i % QT == QT - 1))
                    ins.then_inc(used, 1)
            pe.wait_ge(kv_kept, 22)
            for n in range(8):
                o, c = n // 4, n % 4
                for k in range(KD):
                    ins = nc.tensor.matmul(mem.ps[:, n, :], w_in[:, k, o * P:(o + 1) * P], mem.xT[:, k, c * N:(c + 1) * N],
                                           start=(k == 0), stop=(k == KD - 1))
                ins.then_inc(q_ps, 1)
            pe.wait_ge(x_ready, NT + 8)
            for ps in range(2, 4):
                o = ps - 2
                for m in range(M):
                    if m >= 2:
                        pe.wait_ge(f_ready, 9 * ps + m - 1)
                    for c in range(4):
                        rhs = (mem.ones[:, 0:N] if m == 0 else kq[:, o, c * N:(c + 1) * N] if m == 1 else
                               feat[:, BUF[m], c * N:(c + 1) * N])
                        ins = nc.tensor.matmul(mem.ps[:, 4 * o + c, :], kv[:, o, m, c // 2, :], rhs,
                                               start=(m == 0), stop=(m == M - 1))
                    ins.then_inc(used, 1)
            pe.wait_ge(o_kept, 8)



class Memory:
    pass


def build_tower(nc, io, out):
    with ExitStack() as ctx:
        def sb(name, shape, dt=F32):
            return ctx.enter_context(nc.sbuf_tensor(name, shape, dt))[(slice(None),) * len(shape)]

        def sem(name):
            return ctx.enter_context(nc.semaphore(name))

        mem = Memory()
        mem.ps = ctx.enter_context(nc.psum_tensor("banks", [P, 8, N], F32))[:, :, :]
        mem.h = sb("h", [P, NT, D])
        mem.xw = sb("xw", [P, NT, ROW])
        mem.xT = sb("xT", [P, KD, T])
        mem.arena = sb("arena", [P, ARENA])
        mem.const = sb("const", [P, K_ALL])
        mem.ident = mem.const[:, K_IDENT:K_IDENT + P]
        mem.ident_bf = sb("ident_bf", [P, P], BF16)
        mem.zero_bf = sb("zero_bf", [P, P], BF16)
        mem.ones_bf = sb("ones_bf", [P, P], BF16)
        mem.tri_bf = sb("tri_bf", [P, P], BF16)
        mem.ones = sb("ones", [P, N])
        mem.ids = sb("ids", [P, NT], I32)
        mem.bo = sb("bo", [P, D])
        wo = sb("wo_sb", [P, KD, D])
        mem.wo = wo[:, :, :]
        mem.gate = sb("gate", [P, KD, NE])
        mem.gate_b = sb("gate_b", [P, NE])
        mem.beta = sb("beta", [P, 2, M])
        mem.bn = sb("bn", [P, NT, 6])
        mem.mv = sb("mv", [P, NT, 2])
        mem.ve, mem.r2, mem.sd, mem.rstd = (sb(n, [P, NT]) for n in ("ve", "r2", "sd", "rstd"))
        mem.lg = sb("lg", [P, NT * NE])
        mem.s16 = sb("s16", [P, NT])
        mem.rank = sb("rank", [P, NT * NE])
        mem.mask = sb("mask", [P, 3, NT * NE])
        mem.mask_bf = sb("mask_bf", [P, NT * NE], BF16)
        mem.small = sb("small", [P, 6, NE])
        mem.slots = sb("slots", [P, TOP_K, NT], I32)
        mem.tf = sb("tf", [P, 2, NRT])
        mem.tab = sb("tab", [P, 4, NT + NRT], I32)
        mem.places = sb("places", [P, 2, NE], I32)
        mem.MX = sb("MX", [P, 2, HG, 4, 2])
        mem.NM = sb("NM", [P, 2, 16])
        mem.mr = sb("mr", [P, 2, 16])
        mem.MP = sb("MP", [P, 2, P], BF16)
        mem.mTs = sb("mTs", [48, 2, P], BF16)
        mem.den = sb("den", [P, 16])

        a = Arena(mem.arena, 0)
        mem.QO = a.take(3 * HG * S // 2).bitcast(BF16).rearrange("p (s h t) -> p s h t", s=3, h=HG)
        mem.e = a.take(4 * 2 * N).rearrange("p (s n) -> p s n", s=4)
        mem.po = a.take(2 * N).rearrange("p (s n) -> p s n", s=2)
        mem.V_at = a.at
        mem.KO = a.take(3 * HG * S // 2).bitcast(BF16).rearrange("p (s h t) -> p s h t", s=3, h=HG)
        mem.V = a.take(NIT * QT * HG * DH).rearrange("p (i c x) -> p i c x", i=NIT, c=QT)
        mem.vst = a.take(3 * QT * HG * 32).rearrange("p (s c h x) -> p s c h x", s=3, c=QT, h=HG)
        mem.ao = mem.xT[:, :, :].rearrange("p k (i q x) -> p (k i) q x", i=NIT // KD // 2, q=QT)
        a = Arena(mem.arena, 0)
        mem.w1 = a.take((NE + 1) * KD * 2 * F0).rearrange("p (e n) -> p e n", e=NE + 1)
        mem.w2 = a.take((NE + 1) * F0 // P * D).rearrange("p (e n) -> p e n", e=NE + 1)
        mem.b1 = a.take((NE + 1) * 2 * F0).rearrange("p (e n) -> p e n", e=NE + 1)
        mem.b2 = a.take((NE + 1) * D).rearrange("p (e n) -> p e n", e=NE + 1)
        mem.tiles0_at = a.at
        mem.aoT_at = a.at
        mem.ring_at = ARENA - 2 * (KD * 2 * F1 + F1 // P * D)
        a = Arena(mem.arena, mem.ring_at)
        mem.ring_gu = a.take(2 * KD * 2 * F1).rearrange("p (s n) -> p s n", s=2)
        mem.ring_dn = a.take(2 * F1 // P * D).rearrange("p (s n) -> p s n", s=2)

        def dram(name, shape, dt=F32):
            return nc.dram_tensor(name, shape, dt, kind="Internal").ap()

        mem.qk_dram = dram("qk_parts", [2, 3, B * D, S], BF16)
        mem.row_dram = dram("max_rows", [2, 48, P], BF16)
        mem.rows0 = dram("rows0", [(NT + NRT) * P, ROW])
        mem.rows1 = dram("rows1", [NRT * P, ROW])
        mem.acc = (dram("acc0", [T + TRASH, D]), out)
        mem.pads_in, mem.experts_in = sem("pads_in"), sem("experts_in")

        stage_embed_qkv(nc, mem, io, sem)
        stage_attention(nc, mem, sem)
        stage_router(nc, mem, io, sem, 0)
        stage_experts(nc, mem, io, sem, 0)
        stage_chebyshev(nc, mem, io, sem)
        stage_router(nc, mem, io, sem, 1)
        stage_experts(nc, mem, io, sem, 1)


def constants():
    p = np.arange(P)
    c = np.zeros((P, K_ALL), np.float32)
    c[:, K_IDENT:K_IDENT + P] = np.eye(P)
    c[:, K_TRI:K_TRI + P] = p[:, None] < p[None, :]
    c[:, K_BLOCK:K_BLOCK + P] = p[:, None] // DH == p[None, :] // DH
    e = np.arange(NE)
    c[:, K_LT:K_LT + NE * NE] = (e[None, :] < e[:, None]).reshape(1, -1)
    c[:, K_J128:K_J128 + NT] = P * np.arange(NT)
    c[:, K_J:K_J + NRT] = np.arange(NRT)
    c[:, K_PAD + C_ID] = (T + p).astype(np.int32).view(np.float32)
    c[:, K_TOK:K_TOK + NT] = P * np.arange(NT)[None, :] + p[:, None]
    return c


def kernel(**inputs):
    import concourse.bacc as bacc
    from concourse.bass_utils import run_bass_kernel_spmd

    x = {k: np.asarray(v) for k, v in inputs.items()}

    def halves(w):
        return w.reshape(-1, P, w.shape[-1]).transpose(1, 0, 2)

    def experts(w):
        return w.reshape(w.shape[0], -1, P, w.shape[-1]).transpose(0, 2, 1, 3).reshape(w.shape[0], P, -1)

    cat = np.concatenate
    arrays = {
        "ids": x["x"].reshape(NT, P).T,
        "tok": cat([x["L0_tok_weight"], x["L0_tok_scales"]], 1),
        "const": constants(),
        "wq": halves(x["L0_attn_Wq"].T), "wk": halves(x["L0_attn_Wk"].T), "wv": halves(x["L0_attn_Wv"].T),
        "wo": halves(x["L0_attn_Wo"].T), "bo": x["L0_attn_bo"],
        "gate0": halves(x["L0_ffn_gate_w"]), "gate_b": x["L0_ffn_gate_b"],
        "w1": experts(cat([x["L0_ffn_rw1"], x["L0_ffn_sw1"]])),
        "w2": experts(cat([x["L0_ffn_rw2"], x["L0_ffn_sw2"]])),
        "b1": cat([x["L0_ffn_rb1"], x["L0_ffn_sb1"]]),
        "b2": cat([x["L0_ffn_rb2"], x["L0_ffn_sb2"]]),
        "w_in": halves(x["L1_attn_w_in"].T), "w_out": halves(x["L1_attn_w_out"].T),
        "beta": np.repeat(x["L1_attn_beta"], DH, axis=0).reshape(2, P, M).transpose(1, 0, 2),
        "gate1": halves(x["L1_ffn_gate_w"].T),
        "gu": experts(x["L1_ffn_gate_up_w"].transpose(0, 2, 1)),
        "dn": experts(x["L1_ffn_down_w"].transpose(0, 2, 1)),
    }
    nc = bacc.Bacc("TRN2", target_bir_lowering=False, num_devices=1)
    io, feeds = {}, {}
    for name, a in arrays.items():
        a = np.ascontiguousarray(a)
        feeds["in_" + name] = a
        io[name] = nc.dram_tensor("in_" + name, a.shape, mybir.dt.from_np(a.dtype), kind="ExternalInput").ap()
    out = nc.dram_tensor("out_rows", (T + TRASH, D), F32, kind="ExternalOutput").ap()
    build_tower(nc, io, out)
    r = run_bass_kernel_spmd(nc, [feeds], core_ids=[0])
    return r.results[0]["out_rows"][0:T].reshape(B, S, D)
```

```python
from contextlib import ExitStack

import numpy as np
import concourse.bass as bass
from concourse import mybir

F32 = mybir.dt.float32
BF16 = mybir.dt.bfloat16
I32 = mybir.dt.int32
U32 = mybir.dt.uint32
ALU = mybir.AluOpType
ACT = mybir.ActivationFunctionType
AX = mybir.AxisListType

P = 128
B, S, D = 2, 1024, 256
T = B * S
NT = T // P
KD = D // P
H, DH = 16, 16
HG = 4
NG = H // HG
NIT = B * NG
QT = S // P
N = 512
NE = 8
TOP_K = 2
NRT = (TOP_K * T) // P + NE - 1
F0, F1 = 256, 1024
M = 11
VOCAB = 50257
LN_EPS = 1e-5
DEN_EPS = 1e-8

HEAD = 5
N_WORDS = -(-NRT // 4)
assert (NRT - 2 - HEAD) % 4 == 0 and NE < 16

C_W = D
C_ID = D + NE
ROW = C_ID + 1
TRASH = P

Q_PARTS = (0, 0, 1, 1, 0, 2)
K_PARTS = (0, 1, 0, 1, 2, 0)
KROWS = 16 * len(Q_PARTS)
KMAX = KROWS + 3

K_IDENT = 0
K_TRI = K_IDENT + P
K_BLOCK = K_TRI + P
K_LT = K_BLOCK + P
K_J128 = K_LT + NE * NE
K_J = K_J128 + NT
K_PAD = K_J + NRT
K_TOK = K_PAD + ROW
K_ALL = K_TOK + NT

ARENA = 35840


class Arena:

    def __init__(self, tensor, at):
        self.tensor, self.at = tensor, at

    def take(self, words, parts=P):
        piece = self.tensor[0:parts, self.at:self.at + words]
        self.at += words
        assert self.at <= ARENA, self.at
        return piece


def step_counter(engine, sem, start=0):
    count = [start]

    def link(ins):
        ins.then_inc(sem, 1)
        count[0] += 1
        engine.wait_ge(sem, count[0])

    return link



def norm_stats(nc, dve, link, mem, stats_done, means_done, ready, var_ready, sd_ready):
    for i in range(NT):
        ready(i)
        nc.vector.bn_stats(mem.bn[:, i, :], mem.h[:, i, :]).then_inc(stats_done, 1)
    for i in range(NT):
        dve.wait_ge(stats_done, i + 1)
        nc.vector.bn_aggr(mem.mv[:, i, :], mem.bn[:, i, :]).then_inc(means_done, 1)
    dve.wait_ge(means_done, NT)
    link(nc.vector.tensor_scalar(mem.ve[:, :], mem.mv[:, :, 1], LN_EPS, None, ALU.add))
    nc.vector.tensor_copy(mem.r2[:, :], mem.ve[:, :]).then_inc(var_ready, 1)
    dve.wait_ge(sd_ready, 1)
    link(nc.vector.reciprocal(mem.rstd[:, :], mem.sd[:, :]))
    link(nc.vector.tensor_tensor(mem.r2[:, :], mem.rstd[:, :], mem.rstd[:, :], ALU.mult))
    link(nc.vector.tensor_tensor(mem.r2[:, :], mem.r2[:, :], mem.ve[:, :], ALU.mult))
    link(nc.vector.tensor_scalar(mem.r2[:, :], mem.r2[:, :], -0.5, 1.5, ALU.mult, ALU.add))
    link(nc.vector.tensor_tensor(mem.rstd[:, :], mem.rstd[:, :], mem.r2[:, :], ALU.mult))


def norm_root(nc, act, mem, var_ready, sd_ready):
    act.wait_ge(var_ready, 1)
    nc.scalar.activation(mem.sd[:, :], mem.r2[:, :], ACT.Sqrt).then_inc(sd_ready, 1)


def norm_apply(nc, mem, xn_ready):
    for i in range(NT):
        nc.vector.tensor_scalar(mem.xw[:, i, 0:D], mem.h[:, i, :], mem.mv[:, i, 0:1], mem.rstd[:, i:i + 1],
                                ALU.subtract, ALU.mult).then_inc(xn_ready, 1)


def transpose_rows(nc, pe, mem, source, ready, turned):
    for i in range(NT):
        ready(i)
        for k in range(KD):
            ins = nc.tensor.transpose(mem.ps[:, 2 * (i // 4) + k, (i % 4) * P:(i % 4 + 1) * P],
                                      source(i, k), mem.ident)
            if i % 4 == 3:
                ins.then_inc(turned, 1)


def keep_turned(nc, act, mem, turned, xT_ready):
    for c in range(NT // 4):
        for k in range(KD):
            act.wait_ge(turned, 2 * c + k + 1)
            nc.scalar.activation(mem.xT[:, k, c * N:(c + 1) * N], mem.ps[:, 2 * c + k, :],
                                 ACT.Copy).then_inc(xT_ready, 1)



def stage_embed_qkv(nc, mem, io, sem):
    a = Arena(mem.arena, 0)
    emb = a.take(NT * (D + 2)).rearrange("p (i c) -> p i c", i=NT)
    parts = a.take(4 * 3 * N // 2).bitcast(BF16).rearrange("p (s a n) -> p s a n", s=4, a=3)
    rest = a.take(2 * N).rearrange("p (s n) -> p s n", s=2)
    wqk = a.take(2 * KD * D).rearrange("p (w k n) -> p w k n", w=2, k=KD)
    wv = a.take(KD * D).rearrange("p (k n) -> p k n", k=KD)
    sc2 = a.take(NT * 2).rearrange("p (i g) -> p i g", i=NT)
    assert a.at <= mem.V_at

    ids_in, w_in, const_in = sem("ids_in"), sem("w_in"), sem("const_in")
    gathered = [sem(f"gathered{c}") for c in range(4)]
    step, var_ready, sd_ready = sem("a_step"), sem("a_var"), sem("a_sd")
    xn_ready, turned, xT_ready = sem("a_xn"), sem("a_turned"), sem("a_xT")
    qk_ps, v_ps, part1, rest_ok, part2, part3 = (sem("a_" + n) for n in ("qk_ps", "v_ps", "part1", "rest", "part2", "part3"))
    filled = sem("a_filled")
    v_kept, h_ready, stats_done, means_done = sem("a_v_kept"), sem("a_h"), sem("a_stats"), sem("a_means")
    stored = [sem(f"a_stored{i}") for i in range(4)]
    NP = 16

    with nc.Block() as block:
        @block.sync
        def _(sp):
            sp.dma_start(mem.ids[:, :], io["ids"]).then_inc(ids_in, 16)
            sp.dma_start(mem.const[:, :], io["const"]).then_inc(const_in, 16)
            sp.dma_start(wqk[:, 0, :, :], io["wq"]).then_inc(w_in, 16)
            sp.dma_start(wqk[:, 1, :, :], io["wk"]).then_inc(w_in, 16)
            sp.dma_start(wv, io["wv"]).then_inc(w_in, 16)
            sp.dma_start(mem.wo, io["wo"]).then_inc(w_in, 16)
            sp.dma_start(mem.bo, io["bo"].partition_broadcast(P)).then_inc(w_in, 16)
            sp.wait_ge(const_in, 16)
            pad = mem.const[:, K_PAD:K_PAD + ROW]
            for rows in mem.rows:
                sp.dma_start(rows.rearrange("(j p) c -> p j c", p=P),
                             pad[:, None, :].broadcast_to([P, NRT, ROW])).then_inc(mem.pads_in, 16)
            for n in range(NP):
                c, w, o = n // 4, (n // 2) % 2, n % 2
                sp.wait_ge(part3, n + 1)
                b, t0 = c // 2, (c % 2) * N
                dst = mem.qk_dram[w, :, b * D + o * P:b * D + (o + 1) * P, t0:t0 + N]
                sp.dma_start(dst.rearrange("a p t -> p a t"), parts[:, n % 4, :, :]).then_inc(stored[n % 4], 16)
            for i in range(4):
                sp.wait_ge(stored[i], 16 * NP // 4)
            sp.wait_ge(w_in, 16 * 5)
            sp.wait_ge(mem.pads_in, 32)

        @block.gpsimd
        def _(pool):
            nc.gpsimd.memset(mem.KO[KROWS:KMAX, :, :, :], 1.0).then_inc(filled, 1)
            pool.wait_ge(filled, 1)
            nc.gpsimd.memset(mem.vst[:, :, :, :, DH:DH + 1], 1.0).then_inc(filled, 1)
            pool.wait_ge(filled, 2)
            nc.gpsimd.memset(mem.vst[:, :, :, :, DH + 1:32], 0.0).then_inc(filled, 1)
            pool.wait_ge(filled, 3)
            nc.gpsimd.memset(mem.MP[:, :, :], 0.0).then_inc(filled, 1)
            pool.wait_ge(ids_in, 16)
            for i in range(NT):
                nc.gpsimd.indirect_dma_start(
                    out=emb[:, i, :], out_offset=None, in_=io["tok"],
                    in_offset=bass.IndirectOffsetOnAxis(ap=mem.ids[:, i:i + 1].bitcast(U32), axis=0),
                    bounds_check=VOCAB - 1, oob_is_err=False).then_inc(gathered[i // 4], 16)

        @block.vector
        def _(dve):
            link = step_counter(dve, step)
            dve.wait_ge(const_in, 16)
            nc.vector.tensor_copy(mem.ident_bf[:, :], mem.ident)
            nc.vector.memset(mem.ones_bf[:, :], 1.0)
            nc.vector.memset(mem.zero_bf[:, :], 0.0)
            nc.vector.memset(mem.ones[:, :], 1.0)
            nc.vector.tensor_copy(mem.tri_bf[:, :], mem.const[:, K_TRI:K_TRI + P])
            for c in range(4):
                g = slice(4 * c, 4 * c + 4)
                dve.wait_ge(gathered[c], 64)
                nc.vector.tensor_scalar(sc2[:, g, :], emb[:, g, D:D + 2], 1e-8, 2.0, ALU.max, ALU.mult).then_inc(h_ready, 1)
                nc.vector.tensor_scalar(emb[:, g, 0:D], emb[:, g, 0:D], 0.0, 0.5, ALU.is_ge, ALU.subtract).then_inc(h_ready, 1)
                dve.wait_ge(h_ready, 3 * c + 2)
                nc.vector.tensor_tensor(
                    mem.h[:, g, :].rearrange("p i (g c) -> p i g c", g=2),
                    emb[:, g, 0:D].rearrange("p i (g c) -> p i g c", g=2),
                    sc2[:, g, :, None].broadcast_to([P, 4, 2, P]), ALU.mult).then_inc(h_ready, 1)

            def tile_of_h(i):
                if i % 4 == 0:
                    dve.wait_ge(h_ready, 3 * (i // 4) + 3)

            norm_stats(nc, dve, link, mem, stats_done, means_done, tile_of_h, var_ready, sd_ready)
            norm_apply(nc, mem, xn_ready)

            def third_part(n):
                dve.wait_ge(part2, n + 1)
                nc.vector.tensor_tensor(parts[:, n % 4, 2, :], rest[:, n % 2, :], parts[:, n % 4, 1, :],
                                        ALU.subtract).then_inc(part3, 1)

            for n in range(NP):
                dve.wait_ge(part1, n + 1)
                if n >= 2:
                    dve.wait_ge(part3, n - 1)
                nc.vector.scalar_tensor_tensor(rest[:, n % 2, :], mem.ps[:, n % 4, :], 0.25 if (n // 2) % 2 == 0 else 1.0,
                                               parts[:, n % 4, 0, :], ALU.mult, ALU.subtract).then_inc(rest_ok, 1)
                if n >= 1:
                    third_part(n - 1)
                if n % 2 == 1:
                    j = n // 2
                    dve.wait_ge(v_ps, j + 1)
                    b, c0 = j // 4, 2 * (j % 4)
                    for g in range(NG):
                        nc.vector.tensor_copy(
                            mem.V[:, b * NG + g, c0:c0 + 2, :],
                            mem.ps[:, 4 + j % 4, :].rearrange("p (c x) -> p c x", c=2)[:, :, g * 64:(g + 1) * 64],
                        ).then_inc(v_kept, 1)
            third_part(NP - 1)

        @block.scalar
        def _(act):
            norm_root(nc, act, mem, var_ready, sd_ready)
            keep_turned(nc, act, mem, turned, xT_ready)

            def second_part(n):
                act.wait_ge(rest_ok, n + 1)
                nc.scalar.activation(parts[:, n % 4, 1, :], rest[:, n % 2, :], ACT.Copy).then_inc(part2, 1)

            for n in range(NP):
                act.wait_ge(qk_ps, n + 1)
                if n >= 4:
                    act.wait_ge(stored[n % 4], 16 * (n // 4))
                nc.scalar.activation(parts[:, n % 4, 0, :], mem.ps[:, n % 4, :], ACT.Copy,
                                     scale=0.25 if (n // 2) % 2 == 0 else 1.0).then_inc(part1, 1)
                if n >= 1:
                    second_part(n - 1)
            second_part(NP - 1)

        @block.tensor
        def _(pe):
            pe.wait_ge(const_in, 16)
            transpose_rows(nc, pe, mem, lambda i, k: mem.xw[:, i, k * P:(k + 1) * P],
                           lambda i: pe.wait_ge(xn_ready, i + 1), turned)
            pe.wait_ge(xT_ready, 8)
            pe.wait_ge(w_in, 16 * 5)
            for n in range(NP):
                c, w, o = n // 4, (n // 2) % 2, n % 2
                if n >= 4:
                    pe.wait_ge(rest_ok, n - 3)
                for k in range(KD):
                    ins = nc.tensor.matmul(mem.ps[:, n % 4, :], wqk[:, w, k, o * P:(o + 1) * P],
                                           mem.xT[:, k, c * N:(c + 1) * N], start=(k == 0), stop=(k == KD - 1))
                ins.then_inc(qk_ps, 1)
                if n % 2 == 1:
                    j = n // 2
                    if j >= 4:
                        pe.wait_ge(v_kept, NG * (j - 3))
                    for i in (2 * j, 2 * j + 1):
                        for k in range(KD):
                            ins = nc.tensor.matmul(mem.ps[:, 4 + j % 4, (i % 2) * D:(i % 2 + 1) * D],
                                                   mem.xT[:, k, i * P:(i + 1) * P], wv[:, k, :],
                                                   start=(k == 0), stop=(k == KD - 1))
                    ins.then_inc(v_ps, 1)



def stage_attention(nc, mem, io, sem):
    qk_in = [sem(f"b_qk_in{s}") for s in range(3)]
    row_out = sem("b_row_out")
    row_in = [sem(f"b_row_in{q}") for q in range(2)]
    st_ready, exp_done, pv_done = (sem("b_" + n) for n in ("st", "exp", "pv"))
    ms_ready, ms_free, mp_step, mt_ready, mt_kept = (sem("b_" + n) for n in ("ms", "ms_free", "mp", "mt", "mt_kept"))
    v_staged, po_ready, outT_ready, norm_step, norm_done = (
        sem("b_" + n) for n in ("v_staged", "po", "outT", "norm_step", "norm"))
    UH = 2 * QT
    MH = HG * 4
    QO, KO = mem.QO, mem.KO
    assert MH == UH

    def pair_of(U):
        b = 2 * ((2 * U) % 3)
        return slice(b, b + 2)

    def unit_mod(s, qb, u):
        return 2 * UH * s + UH * qb + u

    def halves(it):
        return ((it, 0), (it, 1))

    def iterations(body, engine):
        body(0, 0)
        with engine.Fori(0, 2) as r:
            for s in (1, 2, 3):
                body(3 * r + s, s % 3)
        body(NIT - 1, (NIT - 1) % 3, last=True)

    def first_pair(n):
        return slice(2 * (n % 3), 2 * (n % 3) + 2)

    with nc.Block() as block:
        @block.sync
        def _(sp):
            def load(it):
                for w, X, PARTS in ((0, QO, Q_PARTS), (1, KO, K_PARTS)):
                    for j, part in enumerate(PARTS):
                        src = mem.qk_dram[w, part, it * 64:(it + 1) * 64, :].rearrange("(h d) t -> d h t", h=HG)
                        sp.dma_start(X[16 * j:16 * j + 16, it % 3, :, :], src).then_inc(qk_in[it % 3], 16)

            def max_rows(G):
                it, qb = G // 2, G % 2
                sp.wait_ge(mt_kept, G + 1)
                if G >= 2:
                    sp.wait_ge(row_in[qb], 16 * (G // 2))
                sp.dma_start(mem.row_dram[qb], mem.mTs[0:48, qb, :]).then_inc(row_out, 16)
                sp.wait_ge(row_out, 16 * (G + 1))
                sp.dma_start(QO[KROWS:KMAX, it % 3, :, qb * N:(qb + 1) * N],
                             mem.row_dram[qb].rearrange("(a h q) p -> a h (q p)", a=3, h=HG)).then_inc(row_in[qb], 16)

            load(0)
            load(1)
            sp.dma_start(mem.w1, io["w1"].rearrange("e p n -> p e n")).then_inc(mem.experts_in, 16)
            max_rows(0)
            max_rows(1)
            for it in range(NIT):
                if it + 2 < NIT:
                    if it >= 1:
                        sp.wait_ge(pv_done, 2 * UH * it)
                    load(it + 2)
                for G in (2 * it + 2, 2 * it + 3):
                    if G < 2 * NIT:
                        max_rows(G)

        @block.gpsimd
        def _(pool):
            def max_parts(G, qb):
                pool.wait_ge(ms_free, MH * (G + 1))
                if not (type(G) is int and G < 2):
                    pool.wait_ge(mt_ready, G - 1)
                nm = mem.NM[:, qb, :]
                mp = mem.MP[:, qb:qb + 1, 0:48].rearrange("p o (a c) -> p o a c", a=3)
                nc.gpsimd.tensor_copy(mp[:, 0, 0, :], nm).then_inc(mp_step, 1)
                pool.wait_ge(mp_step, 4 * G + 1)
                nc.gpsimd.tensor_tensor(mem.mr[:, qb, :], nm, mp[:, 0, 0, :], ALU.subtract).then_inc(mp_step, 1)
                pool.wait_ge(mp_step, 4 * G + 2)
                nc.gpsimd.tensor_copy(mp[:, 0, 1, :], mem.mr[:, qb, :]).then_inc(mp_step, 1)
                pool.wait_ge(mp_step, 4 * G + 3)
                nc.gpsimd.tensor_tensor(mp[:, 0, 2, :], mem.mr[:, qb, :], mp[:, 0, 1, :],
                                        ALU.subtract).then_inc(mp_step, 1)

            def stage_v(it, slot):
                nc.gpsimd.tensor_copy(mem.vst[:, slot, :, :, 0:DH],
                                      mem.V[:, bass.ds(it, 1), :, :].rearrange("p o c (h d) -> p (o c) h d", h=HG),
                                      ).then_inc(v_staged, 1)

            def body(it, s, last=False):
                if not last:
                    pool.wait_ge(pv_done, UH * (2 * it + 1))
                    stage_v(it + 1, (s + 1) % 3)
                    max_parts(2 * it + 2, 0)
                    max_parts(2 * it + 3, 1)

            stage_v(0, 0)
            max_parts(0, 0)
            max_parts(1, 1)
            nc.gpsimd.tensor_tensor(mem.h[:, :, :], mem.h[:, :, :],
                                    mem.bo[:, None, :].broadcast_to([P, NT, D]), ALU.add)
            for it in range(NIT):
                body(it, it % 3, last=(it == NIT - 1))

        @block.scalar
        def _(act):
            def keep_rows(G, qb, bank):
                act.wait_ge(mt_ready, G + 1)
                if not (type(G) is int and G < 2):
                    act.wait_ge(row_out, 16 * (G - 1))
                nc.scalar.activation(mem.mTs[0:48, qb, :],
                                     mem.ps[0:48, bank, 0:64].bitcast(BF16), ACT.Copy).then_inc(mt_kept, 1)

            def keep_out(half, qb):
                act.wait_ge(pv_done, UH * (half + 1))
                if not (type(half) is int and half < 2):
                    act.wait_ge(outT_ready, half - 1)
                nc.scalar.activation(mem.po[:, qb, :], mem.ps[:, 6 + qb, :], ACT.Copy).then_inc(po_ready, 1)

            def body(it, s, last=False):
                for qb in (0, 1):
                    for u in range(UH):
                        U = 2 * UH * it + UH * qb + u
                        act.wait_ge(st_ready, U + 1)
                        if not (type(it) is int and U < 4):
                            act.wait_ge(pv_done, U - 3)
                        nc.scalar.activation(mem.e[:, u % 4, :], mem.ps[:, pair_of(unit_mod(s, qb, u)), :],
                                             ACT.Exp).then_inc(exp_done, 1)
                        if u == 1 and not (type(it) is int and it == 0 and qb == 0):
                            keep_out(2 * it + qb - 1, 1 - qb)
                        if u == 7:
                            if not (last and qb == 1) and not (type(it) is int and it == 0 and qb == 0):
                                keep_rows(2 * it + qb + 1, 1 - qb, 7 - qb)

            keep_rows(0, 0, 6)
            keep_rows(1, 1, 7)
            iterations(body, nc.scalar)
            keep_out(2 * NIT - 1, 1)

        @block.vector
        def _(dve):
            def row_max(G, qb, mb, pair):
                if mb == 0 and not (type(G) is int and G < 2):
                    dve.wait_ge(mp_step, 4 * (G - 1))
                dve.wait_ge(ms_ready, MH * G + mb + 1)
                nc.vector.tensor_reduce(mem.NM[:, qb, mb:mb + 1], mem.ps[:, pair, :],
                                        AX.XY, ALU.max, negate=True).then_inc(ms_free, 1)

            def normalise(half, it, qb):
                dve.wait_ge(outT_ready, half + 1)
                if not (type(half) is int and half < 1):
                    dve.wait_ge(norm_done, half)
                o = mem.ps[:, 6 + qb, :].rearrange("p (q h c) -> p q h c", q=4, h=HG)
                nc.vector.tensor_scalar(mem.den[:, :].rearrange("p (q h) -> p q h", q=4), o[:, :, :, DH],
                                        DEN_EPS, None, ALU.add).then_inc(norm_step, 1)
                dve.wait_ge(norm_step, 2 * half + 1)
                nc.vector.reciprocal(mem.den[:, :], mem.den[:, :]).then_inc(norm_step, 1)
                dve.wait_ge(norm_step, 2 * half + 2)
                nc.vector.tensor_tensor(
                    mem.ao[:, bass.ds(it // 2, 1), 4 * qb:4 * qb + 4, bass.ds((it % 2) * 64, 64)].rearrange(
                        "p o q (h d) -> p (o q) h d", h=HG),
                    o[:, :, :, 0:DH],
                    mem.den[:, :].rearrange("p (q h) -> p q h", q=4)[:, :, :, None].broadcast_to([P, 4, HG, DH]),
                    ALU.mult).then_inc(norm_done, 1)

            def body(it, s, last=False):
                for qb in (0, 1):
                    first = type(it) is int and it == 0 and qb == 0
                    for u in range(UH):
                        if not last:
                            row_max(2 * it + 2 + qb, qb, u, pair_of(unit_mod(s, qb, u)))
                        if u == 12 and not first:
                            normalise(2 * it + qb - 1, it if qb == 1 else it - 1, 1 - qb)

            for G in (0, 1):
                for mb in range(MH):
                    row_max(G, G, mb, first_pair(MH * G + mb))
            iterations(body, nc.vector)
            normalise(2 * NIT - 1, NIT - 1, 1)

        @block.tensor
        def _(pe):
            def score_block(qb, s, mb, pair):
                hh, qt = mb // 4, mb % 4
                q0 = qb * N + qt * P
                for kh in range(2):
                    ins = nc.tensor.matmul(mem.ps[:, pair.start + kh, :], QO[0:KROWS, s, hh, q0:q0 + P],
                                           KO[0:KROWS, s, hh, kh * N:(kh + 1) * N], start=True, stop=True)
                ins.then_inc(ms_ready, 1)

            def turn_max(G, qb, bank):
                pe.wait_ge(mp_step, 4 * G + 4)
                nc.tensor.transpose(mem.ps[:, bank, 0:64].bitcast(BF16), mem.MP[:, qb, :],
                                    mem.ident_bf[:, :]).then_inc(mt_ready, 1)

            def turn_out(half, G, qb):
                pe.wait_ge(po_ready, half + 1)
                if G is not None:
                    pe.wait_ge(mt_kept, G + 1)
                for q in range(4):
                    ins = nc.tensor.transpose(mem.ps[:, 6 + qb, q * P:(q + 1) * P],
                                              mem.po[:, qb, q * P:(q + 1) * P], mem.ident)
                ins.then_inc(outT_ready, 1)

            def scores_t(it, s, qb, u, last=False):
                U = 2 * UH * it + UH * qb + u
                if u == 0:
                    pe.wait_ge(row_in[qb], 16 * (it + 1))
                if type(it) is int and U == 0:
                    pe.wait_ge(ms_free, 2 * MH - 1)
                elif not (last and UH * qb + u >= 3):
                    pe.wait_ge(ms_free, U + 2 * MH - 2)
                kc, pair = u // 2, u % 2
                bank = pair_of(unit_mod(s, qb, u)).start
                for j in range(2):
                    hh = 2 * pair + j
                    ins = nc.tensor.matmul(mem.ps[:, bank + j, :], KO[0:KMAX, s, hh, kc * P:(kc + 1) * P],
                                           QO[0:KMAX, s, hh, qb * N:(qb + 1) * N], start=True, stop=True)
                ins.then_inc(st_ready, 1)

            def times_v(it, s, qb, u):
                U = 2 * UH * it + UH * qb + u
                pe.wait_ge(exp_done, U + 1)
                kc, pair = u // 2, u % 2
                for j in range(2):
                    hh = 2 * pair + j
                    ins = nc.tensor.matmul(mem.ps[32 * hh:32 * hh + 32, 6 + qb, :], mem.vst[:, s, kc, hh, :],
                                           mem.e[:, u % 4, j * N:(j + 1) * N], start=(kc == 0), stop=(kc == QT - 1))
                ins.then_inc(pv_done, 1)

            def body(it, s, last=False):
                fixed0 = type(it) is int and it == 0
                for qb in (0, 1):
                    first = fixed0 and qb == 0
                    for u in range(UH):
                        if u < UH - 1:
                            scores_t(it, s, qb, u + 1, last)
                        elif qb == 0:
                            scores_t(it, s, 1, 0, last)
                        elif not last:
                            scores_t(it + 1, (s + 1) % 3, 0, 0)
                        if not last:
                            if qb == 0 and u == 0:
                                pe.wait_ge(qk_in[(s + 1) % 3], slot_value(it, s))
                            pe.wait_ge(exp_done, 2 * UH * it + UH * qb + u + 1)
                            score_block(qb, (s + 1) % 3, u, pair_of(unit_mod(s, qb, u)))
                        if u == 0:
                            if qb == 0:
                                pe.wait_ge(v_staged, it + 1)
                            if fixed0:
                                pe.wait_ge(mt_kept, qb + 1)
                            else:
                                pe.wait_ge(norm_done, 2 * it + qb - 1)
                        if u == 5 and not first and not (last and qb == 1):
                            pe.wait_ge(po_ready, 2 * it + qb)
                            turn_max(2 * it + qb + 1, 1 - qb, 7 - qb)
                        if u == 9 and not first:
                            turn_out(2 * it + qb - 1, None if (last and qb == 1) else 2 * it + qb + 1, 1 - qb)
                        times_v(it, s, qb, u)

            def slot_value(it, s):
                if type(it) is int:
                    return 192 * ((it + 1) // 3 + 1)
                return slot_fill[s]

            slot_fill = {}
            pe.wait_ge(qk_in[0], 192)
            for G in (0, 1):
                for mb in range(MH):
                    n = MH * G + mb
                    if n >= 3:
                        pe.wait_ge(ms_free, n - 2)
                    score_block(G, 0, mb, first_pair(n))
                    if n == MH + MH // 2:
                        turn_max(0, 0, 6)
            turn_max(1, 1, 7)
            scores_t(0, 0, 0, 0)
            body(0, 0)
            with nc.tensor.Fori(0, 2) as r:
                for s in (1, 2, 3):
                    slot_fill[s % 3] = 192 * (r + ((s + 1) // 3) + 1)
                    body(3 * r + s, s % 3)
            body(NIT - 1, (NIT - 1) % 3, last=True)
            turn_out(2 * NIT - 1, None, 1)



def project_and_add(nc, pe, mem, aT, w, start, done):
    for i in range(NT):
        start(i)
        for k in range(KD):
            ins = nc.tensor.matmul(mem.ps[:, i // 2, (i % 2) * D:(i % 2 + 1) * D], aT[:, k, i * P:(i + 1) * P],
                                   w[:, k, :], start=(k == 0), stop=(k == KD - 1))
        ins.then_inc(done, 1)


def add_projection(nc, dve, mem, projected, h_ready):
    for i in range(NT):
        dve.wait_ge(projected, 2 * (i // 2) + 2)
        nc.vector.tensor_tensor(mem.h[:, i, :], mem.ps[:, i // 2, (i % 2) * D:(i % 2 + 1) * D],
                                mem.h[:, i, :], ALU.add).then_inc(h_ready, 1)


def stage_router(nc, mem, io, sem, layer):
    t = f"c{layer}_"
    if layer == 0:
        a = Arena(mem.arena, mem.layer0_at)
        aT = a.take(KD * T).rearrange("p (k t) -> p k t", k=KD)
        w_out = mem.wo
        gs = a.take(2 * F0 // P * N).rearrange("p (s f t) -> p s f t", s=2, f=F0 // P)
        hs = a.take(2 * F0 // P * N).rearrange("p (s f t) -> p s f t", s=2, f=F0 // P)
    else:
        a = Arena(mem.arena, 0)
        aT, w_out = mem.xT, mem.w_out
    rows = mem.rows[layer]
    cmp = a.take(2 * NT * NE * NE).rearrange("p (s n) -> p s n", s=2)
    assert a.at <= (mem.w1_at if layer == 0 else mem.ring_at)
    acc, gate, gate_in = mem.acc[layer], mem.gate, sem(t + "gate_in")
    projected, h_ready = sem(t + "projected"), sem(t + "h")
    step, stats_done, means_done = (sem(t + n) for n in ("step", "stats", "means"))
    var_ready, sd_ready, xn_ready, turned, xT_ready = (sem(t + n) for n in ("var", "sd", "xn", "turned", "xT"))
    logits, shifted, exped, mask_ready, counted, slots_ready, sent = (
        sem(t + n) for n in ("logits", "shifted", "exped", "mask", "counted", "slots", "sent"))
    if layer == 0:
        turned0, kept0 = sem(t + "turned0"), sem(t + "kept0")
        s_up, s_gate, s_act, s_down, s_added, s_bias = (
            sem(t + n) for n in ("s_up", "s_gate", "s_act", "s_down", "s_added", "s_bias"))
    else:
        places_ready = sem(t + "places")
    NC = T // N
    S_UP, S_Y = 4, (3, 0)

    with nc.Block() as block:
        @block.sync
        def _(sp):
            sp.dma_start(gate[:, :, :], io[f"gate{layer}"]).then_inc(gate_in, 16)
            if layer == 0:
                sp.dma_start(mem.gate_b[:, :], io["gate_b"].partition_broadcast(P)).then_inc(gate_in, 16)
                sp.dma_start(mem.w2, io["w2"].rearrange("e p n -> p e n")).then_inc(mem.experts_in, 16)
                sp.dma_start(mem.b1_shared[:, :], io["b1_shared"]).then_inc(mem.experts_in, 16)
                sp.dma_start(mem.b2, io["b2"].partition_broadcast(P)).then_inc(mem.experts_in, 16)
                sp.dma_start(mem.b1, io["b1"].partition_broadcast(P)).then_inc(mem.experts_in, 16)
            for c in range(NC):
                if layer == 0:
                    sp.wait_ge(s_added, 2 * c + 2)
                else:
                    sp.wait_ge(h_ready, 4 * c + 4)
                sp.dma_start(acc[c * N:(c + 1) * N, :].rearrange("(i p) c -> p i c", p=P),
                             mem.h[:, 4 * c:4 * c + 4, :]).then_inc(mem.acc_in[layer], 16)
            sp.dma_start(acc[T:T + TRASH, :], mem.h[:, 0, :]).then_inc(mem.acc_in[layer], 16)
            if layer == 1:
                sp.wait_ge(places_ready, 1)
                for o in range(2):
                    load_experts(nc, sp, mem, io, o)
            sp.wait_ge(gate_in, 32 if layer == 0 else 16)

        @block.gpsimd
        def _(pool):
            if layer == 0:
                pool.wait_ge(xn_ready, NT)
                pool.wait_ge(mem.experts_in, 16 * 5)
                nc.gpsimd.tensor_tensor(mem.h[:, :, :], mem.h[:, :, :],
                                        mem.b2[:, NE:NE + 1, :].broadcast_to([P, NT, D]), ALU.add).then_inc(s_bias, 1)
            pool.wait_ge(slots_ready, 1)
            for k in range(TOP_K):
                for i in range(NT):
                    nc.gpsimd.indirect_dma_start(
                        out=rows, out_offset=bass.IndirectOffsetOnAxis(ap=mem.slots[:, k, i:i + 1].bitcast(U32), axis=0),
                        in_=mem.xw[:, i, :], in_offset=None,
                        bounds_check=NRT * P - 1, oob_is_err=False).then_inc(sent, 16)
            pool.wait_ge(sent, 16 * TOP_K * NT)

        @block.scalar
        def _(act):
            if layer == 0:
                for c in range(NT // 4):
                    for k in range(KD):
                        act.wait_ge(turned0, 2 * c + k + 1)
                        nc.scalar.activation(aT[:, k, c * N:(c + 1) * N], mem.ps[:, 2 * c + k, :],
                                             ACT.Copy).then_inc(kept0, 1)
            norm_root(nc, act, mem, var_ready, sd_ready)
            keep_turned(nc, act, mem, turned, xT_ready)
            act.wait_ge(shifted, 1)
            nc.scalar.activation(mem.lg[:, :], mem.lg[:, :], ACT.Exp).then_inc(exped, 1)
            if layer == 0:
                act.wait_ge(mem.experts_in, 16 * 5)
                for c in range(NC):
                    act.wait_ge(s_up, c + 1)
                    if c >= 2:
                        act.wait_ge(s_act, 2 * c - 2)
                    for f in range(F0 // P):
                        nc.scalar.activation(gs[:, c % 2, f, :], mem.ps[:, S_UP + f, :], ACT.Silu,
                                             bias=mem.b1_shared[:, f:f + 1]).then_inc(s_gate, 1)

        @block.vector
        def _(dve):
            link = step_counter(dve, step)
            const = mem.const
            add_projection(nc, dve, mem, projected, h_ready)
            norm_stats(nc, dve, link, mem, stats_done, means_done, lambda i: dve.wait_ge(h_ready, i + 1),
                       var_ready, sd_ready)
            norm_apply(nc, mem, xn_ready)
            tok = mem.xw[:, :, :].rearrange("p i c -> p (i c)").bitcast(I32).rearrange("p (i c) -> p i c", i=NT)
            nc.vector.tensor_copy(tok[:, :, C_ID], const[:, K_TOK:K_TOK + NT])

            lg = mem.lg[:, :].rearrange("p (i e) -> p i e", i=NT)
            dve.wait_ge(gate_in, 32 if layer == 0 else 16)
            dve.wait_ge(logits, 1)
            l_ps = mem.ps[:, 0, 0:NT * NE].rearrange("p (i e) -> p i e", i=NT)
            if layer == 0:
                link(nc.vector.tensor_tensor(lg, l_ps, mem.gate_b[:, None, :].broadcast_to([P, NT, NE]), ALU.add))
            else:
                link(nc.vector.tensor_copy(lg, l_ps))
            link(nc.vector.tensor_reduce(mem.s16[:, :], lg, AX.X, ALU.max))
            link(nc.vector.tensor_tensor(lg, lg, mem.s16[:, :, None].broadcast_to([P, NT, NE]), ALU.subtract))
            nc.vector.memset(mem.r2[:, :], 0.0).then_inc(shifted, 1)
            dve.wait_ge(exped, 1)
            link(nc.vector.tensor_reduce(mem.s16[:, :], lg, AX.X, ALU.add))
            link(nc.vector.reciprocal(mem.s16[:, :], mem.s16[:, :]))
            link(nc.vector.tensor_tensor(lg, lg, mem.s16[:, :, None].broadcast_to([P, NT, NE]), ALU.mult))

            over_e = lg[:, :, None, :].broadcast_to([P, NT, NE, NE])
            own = lg[:, :, :, None].broadcast_to([P, NT, NE, NE])
            gt = cmp[:, 0, :].rearrange("p (i e f) -> p i e f", i=NT, e=NE)
            eq = cmp[:, 1, :].rearrange("p (i e f) -> p i e f", i=NT, e=NE)
            lower = const[:, K_LT:K_LT + NE * NE].rearrange("p (e f) -> p e f", e=NE)
            link(nc.vector.tensor_tensor(gt, over_e, own, ALU.is_gt))
            link(nc.vector.tensor_tensor(eq, over_e, own, ALU.is_equal))
            link(nc.vector.tensor_tensor(eq, eq, lower[:, None, :, :].broadcast_to([P, NT, NE, NE]), ALU.mult))
            link(nc.vector.tensor_tensor(gt, gt, eq, ALU.add))
            rank = mem.rank[:, :].rearrange("p (i e) -> p i e", i=NT)
            link(nc.vector.tensor_reduce(rank, gt, AX.X, ALU.add))
            mask = mem.mask[:, 2, :].rearrange("p (i e) -> p i e", i=NT)
            link(nc.vector.tensor_scalar(mem.mask_bf[:, :], mem.rank[:, :], float(TOP_K), None, ALU.is_lt))
            nc.vector.tensor_scalar(mem.mask[:, 2, :], mem.rank[:, :], float(TOP_K), None, ALU.is_lt).then_inc(mask_ready, 1)
            for k in range(TOP_K):
                link(nc.vector.tensor_scalar(mem.mask[:, k, :], mem.rank[:, :], float(k), None, ALU.is_equal))
            cw = mem.xw[:, :, C_W:C_W + NE]
            dve.wait_ge(mask_ready, 1)
            link(nc.vector.tensor_tensor(cw, lg, mask, ALU.mult))
            if layer == 1:
                link(nc.vector.tensor_reduce(mem.s16[:, :], cw, AX.X, ALU.add))
                link(nc.vector.reciprocal(mem.s16[:, :], mem.s16[:, :]))
                link(nc.vector.tensor_tensor(cw, cw, mem.s16[:, :, None].broadcast_to([P, NT, NE]), ALU.mult))

            dve.wait_ge(counted, 1)
            j128 = const[:, K_J128:K_J128 + NT]
            c128 = cmp[:, 0, 0:NE * NT].rearrange("p (e j) -> p e j", e=NE)
            n_of = mem.ps[:, 2, 0:NE]
            small = mem.small
            tiles, base, has, order = small[:, 0, :], small[:, 1, :], small[:, 2, :], small[:, 3, :]
            link(nc.vector.tensor_copy(small[:, 4, :], n_of))
            link(nc.vector.tensor_tensor(c128, small[:, 4, :, None].broadcast_to([P, NE, NT]),
                                         j128[:, None, :].broadcast_to([P, NE, NT]), ALU.is_gt))
            link(nc.vector.tensor_reduce(tiles, c128, AX.X, ALU.add))
            ee = cmp[:, 1, 0:NE * NE].rearrange("p (e f) -> p e f", e=NE)
            link(nc.vector.tensor_tensor(ee, tiles[:, None, :].broadcast_to([P, NE, NE]), lower, ALU.mult))
            link(nc.vector.tensor_reduce(base, ee, AX.X, ALU.add))

            slotm = mem.rank[:, :].rearrange("p (i e) -> p i e", i=NT)
            link(nc.vector.scalar_tensor_tensor(slotm, base[:, None, :].broadcast_to([P, NT, NE]), float(P),
                                                mem.ps[:, 1, 0:NT * NE].rearrange("p (i e) -> p i e", i=NT),
                                                ALU.mult, ALU.add))
            for k in range(TOP_K):
                sel = mem.mask[:, k, :]
                link(nc.vector.tensor_tensor(sel, sel, mem.rank[:, :], ALU.mult))
                link(nc.vector.tensor_reduce(mem.s16[:, :], sel.rearrange("p (i e) -> p i e", i=NT), AX.X, ALU.add))
                link(nc.vector.tensor_copy(mem.slots[:, k, :], mem.s16[:, :]))
            nc.vector.memset(mem.r2[:, :], 0.0).then_inc(slots_ready, 1)

            jj = const[:, K_J:K_J + NRT]
            ge = cmp[:, 0, 0:NRT * NE].rearrange("p (j e) -> p j e", j=NRT)
            tf, words = mem.tf[:, :, 1:1 + NRT], mem.words

            def pack(k):
                of = lambda i: mem.tf[:, k, i:i + 4 * N_WORDS - 3:4]
                link(nc.vector.scalar_tensor_tensor(words[:, k, :], of(5), 16.0, of(4), ALU.mult, ALU.add))
                for i in (3, 2, 1, 0):
                    link(nc.vector.scalar_tensor_tensor(words[:, k, :], words[:, k, :], 16.0, of(i), ALU.mult, ALU.add))
                link(nc.vector.tensor_copy(mem.tab[:, k, :], words[:, k, :]))

            link(nc.vector.memset(mem.tf[:, :, :], 0.0))
            link(nc.vector.tensor_tensor(ge, jj[:, :, None].broadcast_to([P, NRT, NE]),
                                         base[:, None, :].broadcast_to([P, NRT, NE]), ALU.is_ge))
            link(nc.vector.tensor_reduce(tf[:, 0, :], ge, AX.X, ALU.add))
            link(nc.vector.tensor_scalar(tf[:, 0, :], tf[:, 0, :], -1.0, None, ALU.add))
            pack(0)
            if layer == 1:
                link(nc.vector.tensor_scalar(has, tiles, 0.0, None, ALU.is_gt))
                link(nc.vector.tensor_tensor(ge, ge, has[:, None, :].broadcast_to([P, NRT, NE]), ALU.mult))
                link(nc.vector.tensor_reduce(tf[:, 1, :], ge, AX.X, ALU.add))
                pack(1)
                link(nc.vector.tensor_tensor(ee, has[:, None, :].broadcast_to([P, NE, NE]), lower, ALU.mult))
                link(nc.vector.tensor_reduce(order, ee, AX.X, ALU.add))
                place = const[:, K_J:K_J + NE]
                at = cmp[:, 0, 0:NE * NE].rearrange("p (o e) -> p o e", o=NE)
                link(nc.vector.tensor_tensor(at, place[:, :, None].broadcast_to([P, NE, NE]),
                                             order[:, None, :].broadcast_to([P, NE, NE]), ALU.is_equal))
                link(nc.vector.tensor_tensor(at, at, has[:, None, :].broadcast_to([P, NE, NE]), ALU.mult))
                link(nc.vector.tensor_tensor(ee, at, place[:, None, :].broadcast_to([P, NE, NE]), ALU.mult))
                link(nc.vector.tensor_reduce(small[:, 4, :], ee, AX.X, ALU.add))
                link(nc.vector.tensor_copy(mem.places[:, 0, :], small[:, 4, :]))
                n_has, last_at = mem.n_has[:, 0:1], mem.n_has[:, 1:2]
                link(nc.vector.tensor_tensor(small[:, 5, :], has, base, ALU.mult))
                link(nc.vector.tensor_reduce(last_at, small[:, 5, :], AX.X, ALU.max))
                link(nc.vector.tensor_scalar(last_at, last_at, 1.0, None, ALU.add))
                link(nc.vector.tensor_reduce(n_has, has, AX.X, ALU.add))
                link(nc.vector.tensor_scalar(small[:, 5, :], base, -float(NRT), None, ALU.add))
                link(nc.vector.tensor_tensor(ee, at, small[:, 5, None, :].broadcast_to([P, NE, NE]), ALU.mult))
                link(nc.vector.tensor_reduce(small[:, 4, :], ee, AX.X, ALU.add))
                link(nc.vector.tensor_scalar(mem.places[:, 1, :], small[:, 4, :], float(NRT + 1), last_at,
                                             ALU.add, ALU.min))
                link(nc.vector.tensor_scalar(mem.places[:, 3, :], place, n_has, None, ALU.min))
                link(nc.vector.tensor_scalar(mem.places[:, 2, :], mem.places[:, 3, :], 1, None, ALU.bitwise_and))
                nc.vector.memset(mem.r2[:, :], 0.0).then_inc(places_ready, 1)
            else:
                for c in range(NC + 1):
                    for f in range(F0 // P):
                        if c < NC:
                            if f == 0 and c >= 2:
                                dve.wait_ge(s_down, 2 * c - 2)
                            dve.wait_ge(s_gate, 2 * c + f + 1)
                            nc.vector.scalar_tensor_tensor(hs[:, c % 2, f, :], mem.ps[:, S_UP + 2 + f, :],
                                                           mem.b1_shared[:, 2 + f:3 + f], gs[:, c % 2, f, :],
                                                           ALU.add, ALU.mult).then_inc(s_act, 1)
                    for n in range(2 * c - 2, 2 * c) if c else ():
                        if n == 0:
                            dve.wait_ge(s_bias, 1)
                        dve.wait_ge(s_down, n + 1)
                        nc.vector.tensor_tensor(
                            mem.h[:, 2 * n:2 * n + 2, :], mem.ps[:, S_Y[n % 2], :].rearrange("p (i c) -> p i c", i=2),
                            mem.h[:, 2 * n:2 * n + 2, :], ALU.add).then_inc(s_added, 1)

        @block.tensor
        def _(pe):
            if layer == 0:
                def attended(i, k):
                    return mem.ao[:, (i // QT) * KD + k, i % QT, :]

                transpose_rows(nc, pe, mem, attended, lambda i: None, turned0)
                pe.wait_ge(kept0, 8)
            project_and_add(nc, pe, mem, aT, w_out, lambda i: None, projected)
            transpose_rows(nc, pe, mem, lambda i, k: mem.xw[:, i, k * P:(k + 1) * P],
                           lambda i: pe.wait_ge(xn_ready, i + 1), turned)
            pe.wait_ge(xT_ready, 8)
            pe.wait_ge(gate_in, 32 if layer == 0 else 16)
            for i in range(NT):
                for k in range(KD):
                    ins = nc.tensor.matmul(mem.ps[:, 0, i * NE:(i + 1) * NE], mem.xT[:, k, i * P:(i + 1) * P],
                                           gate[:, k, :], start=(k == 0), stop=(k == KD - 1))
            ins.then_inc(logits, 1)
            def shared_up(c):
                if c >= 1:
                    pe.wait_ge(s_act, 2 * c)
                for f in range(2 * F0 // P):
                    for k in range(KD):
                        n0 = k * 2 * F0 + f * P
                        ins = nc.tensor.matmul(mem.ps[:, S_UP + f, :], mem.w1[:, NE, n0:n0 + P],
                                               mem.xT[:, k, c * N:(c + 1) * N], start=(k == 0), stop=(k == KD - 1))
                ins.then_inc(s_up, 1)

            if layer == 0:
                pe.wait_ge(mem.experts_in, 16 * 5)
                shared_up(0)
            pe.wait_ge(mask_ready, 1)
            nc.tensor.matmul(mem.ps[:, 1, 0:NT * NE], mem.zero_bf, mem.mask_bf, start=True, stop=False)
            for d in range(1, NT):
                nc.tensor.matmul(mem.ps[:, 1, d * NE:NT * NE], mem.ones_bf[:, :], mem.mask_bf[:, 0:(NT - d) * NE],
                                 start=False, stop=False, skip_group_check=True)
            nc.tensor.matmul(mem.ps[:, 1, 0:NT * NE], mem.tri_bf, mem.mask_bf, start=False, stop=True)
            for i in range(NT):
                ins = nc.tensor.matmul(mem.ps[:, 2, 0:NE], mem.ones_bf[:, :], mem.mask_bf[:, i * NE:(i + 1) * NE],
                                       start=(i == 0), stop=(i == NT - 1))
            ins.then_inc(counted, 1)
            if layer == 0:
                for n in range(2 * NC):
                    c = n // 2
                    if n % 2 == 0 and c + 1 < NC:
                        shared_up(c + 1)
                    pe.wait_ge(s_act, 2 * c + 2)
                    if n >= 2:
                        pe.wait_ge(s_added, n - 1)
                    for i in range(2):
                        t0 = (n % 2) * 2 * P + i * P
                        for f in range(F0 // P):
                            ins = nc.tensor.matmul(mem.ps[:, S_Y[n % 2], i * D:(i + 1) * D], hs[:, c % 2, f, t0:t0 + P],
                                                   mem.w2[:, NE, f * D:(f + 1) * D],
                                                   start=(f == 0), stop=(f == F0 // P - 1))
                    ins.then_inc(s_down, 1)



def load_experts(nc, engine, mem, io, o):
    e = nc.sync.value_load(mem.places[0:1, 0, o:o + 1], min_val=0, max_val=NE - 1)
    slot = nc.sync.value_load(mem.places[0:1, 2, o:o + 1], min_val=0, max_val=1)
    if o >= 2:
        first = nc.sync.value_load(mem.places[0:1, 1, o - 1:o], min_val=1, max_val=NRT + 1)
        engine.wait_ge(mem.tiles_done, first)
    engine.dma_start(mem.ring_gu[:, bass.ds(slot, 1), :].rearrange("p o n -> p (o n)"),
                     io["gu"][bass.ds(e, 1), :, :].rearrange("o p n -> (o p) n")).then_inc(mem.w_loaded, 16)
    engine.dma_start(mem.ring_dn[:, bass.ds(slot, 1), :].rearrange("p o n -> p (o n)"),
                     io["dn"][bass.ds(e, 1), :, :].rearrange("o p n -> (o p) n")).then_inc(mem.w_loaded, 16)
    engine.wait_ge(mem.w_loaded, 32 * (o + 1))


def stage_experts(nc, mem, io, sem, layer):
    t = f"d{layer}_"
    if layer == 0:
        F = F0
        a = Arena(mem.arena, mem.layer0_at)
    else:
        F = F1
        a = Arena(mem.arena, 0)
    n_tiles, rows = NRT, mem.rows[layer]
    FT = F // P
    copies = max(1, FT // 4)
    acc = mem.acc[layer]
    xg = a.take(4 * ROW).rearrange("p (s c) -> p s c", s=4)
    meta = a.take(4 * (ROW - D)).rearrange("p (s c) -> p s c", s=4)
    xgT = a.take(2 * D).rearrange("p (s k t) -> p s k t", s=2, k=KD)
    pre = a.take(2 * 2 * F0).rearrange("p (s f) -> p s f", s=2)
    g = a.take(2 * F).rearrange("p (s f) -> p s f", s=2)
    hact = a.take(2 * F).rearrange("p (s f) -> p s f", s=2)
    hT = a.take(2 * F).rearrange("p (s c t) -> p s c t", s=2, c=FT)
    y0 = a.take(2 * D).rearrange("p (s c) -> p s c", s=2)
    y = a.take(4 * D).rearrange("p (s c) -> p s c", s=4)
    assert a.at <= (mem.w1_at if layer == 0 else mem.ring_at)
    XT, GU = 0, (1, 2) if layer == 0 else (1, 3)
    HT, Y = (3, 4) if layer == 0 else (5, 7)

    loaded = [sem(f"{t}loaded{s}") for s in range(4)]
    xT_ps, xT_kept, gu_ps, g_ready, hact_ready, hT_ps, hT_kept, y_ps, y_ready, added, meta_kept, may_add = (
        sem(t + n) for n in ("xT_ps", "xT_kept", "gu", "g", "hact", "hT_ps", "hT_kept", "y_ps", "y", "added",
                             "meta", "may_add"))
    if layer == 0:
        pre_ready, y_step, h_back = sem(t + "pre"), sem(t + "y_step"), sem(t + "h_back")
    mem.tiles_done = y_ps
    Y1 = 1

    LAG = 2 if layer == 0 else 1

    def steps(body, engine, row=None):
        def number_of(word, at):
            least, most = (0, NE - 1) if row == 0 else (1, NE)
            return lambda i: nc.s_assert_within(engine.snap((word // 16 ** (at + i + 1)) % 16), least, most,
                                                skip_runtime_bounds_check_because="the router packs these numbers")

        def load_word(g):
            if row is None:
                return 0
            return engine.value_load(mem.tab[0:1, row, bass.ds(g, 1)], min_val=0, max_val=2 ** 24 - 1)

        word = load_word(0)
        for j in range(HEAD):
            body(j, j % 4, number_of(word, j))
        with engine.Fori(0, (n_tiles - 2 - HEAD) // 4) as r:
            word = load_word(r + 1)
            for u in range(HEAD, HEAD + 4):
                body(4 * r + u, u % 4, number_of(word, u - 4), r, u)
        word = load_word(N_WORDS - 1)
        for j in range(n_tiles - 2, n_tiles + LAG):
            body(j, j % 4, number_of(word, j - 4 * (N_WORDS - 1)))

    def fixed(j):
        return type(j) is int

    with nc.Block() as block:
        def load(engine, j, s):
            row0 = j * P + 4 * P if fixed(j) else engine.snap(j * P + 4 * P)
            engine.wait_ge(meta_kept, 2 * j + 2)
            engine.dma_start(xg[:, s, :], rows[bass.ds(row0, P), :]).then_inc(loaded[s], 16)

        def first_loads(engine):
            for j in range(4):
                engine.dma_start(xg[:, j, :], rows[j * P:(j + 1) * P, :]).then_inc(loaded[j], 16)

        def run_loads(engine):
            first_loads(engine)
            for j in range(HEAD):
                load(engine, j, j % 4)
            n_loop = (n_tiles - 4 - HEAD) // 4
            with engine.Fori(0, n_loop) as r:
                for u in range(HEAD, HEAD + 4):
                    load(engine, 4 * r + u, u % 4)
            for j in range(4 * n_loop + HEAD, n_tiles - 4):
                load(engine, j, j % 4)

        @block.sync
        def _(sp):
            sp.sem_inc(y_ps, Y1)
            if layer == 1:
                for o in range(2, NE):
                    load_experts(nc, sp, mem, io, o)
            else:
                run_loads(sp)
                sp.wait_ge(added, 16 * n_tiles)
                sp.dma_start(mem.h[:, :, :], acc[0:T, :].rearrange("(i p) c -> p i c", p=P)).then_inc(h_back, 16)
                sp.wait_ge(h_back, 16)

        @block.gpsimd
        def _(pool):
            def body(j, s, loads):
                if loads:
                    load(nc.gpsimd, j, s)
                if not fixed(j) or j >= LAG:
                    pool.wait_ge(y_ready, j - LAG + 1)
                    if not fixed(j) or j > LAG:
                        pool.wait_ge(added, 16 * j - 16 * LAG)
                    pool.sem_inc(may_add, 1)
                    nc.gpsimd.indirect_dma_start(
                        out=acc, out_offset=bass.IndirectOffsetOnAxis(
                            ap=meta[:, (s - LAG) % 4, NE:NE + 1].bitcast(U32), axis=0),
                        in_=y[:, (s - LAG) % 4, :], in_offset=None, compute_op=ALU.add).then_inc(added, 16)

            if layer == 1:
                first_loads(nc.gpsimd)
            pool.wait_ge(mem.acc_in[layer], 16 * (T // N + 1))
            for j in range(HEAD):
                body(j, j % 4, layer == 1)
            n_loop = (n_tiles - 4 - HEAD) // 4
            with nc.gpsimd.Fori(0, n_loop) as r:
                for u in range(HEAD, HEAD + 4):
                    body(4 * r + u, u % 4, layer == 1)
            for j in range(4 * n_loop + HEAD, n_tiles + LAG):
                body(j, j % 4, layer == 1 and j + 4 < n_tiles)
            pool.wait_ge(added, 16 * n_tiles)

        @block.scalar
        def _(act):
            def body(j, s, of, r=None, u=None):
                p = s % 2
                if not fixed(j) or j < n_tiles - 1:
                    keep_rows(j + 1, (s + 1) % 4)
                if not fixed(j) or 1 <= j <= n_tiles:
                    for q in range(copies):
                        act.wait_ge(hT_ps, copies * (j - 1) + q + 1)
                        if q == 0 and (not fixed(j) or j >= 3):
                            act.wait_ge(y_ps, j - 2 + Y1)
                        w = min(4, FT)
                        nc.scalar.activation(
                            hT[:, 1 - p, 4 * q:4 * q + w, :].rearrange("p c t -> p (c t)"),
                            mem.ps[:, HT + q, 0:w * P], ACT.Copy).then_inc(hT_kept, 1)
                if not fixed(j) or j < n_tiles:
                    if not fixed(j) or j >= 2:
                        act.wait_ge(hact_ready, j - 1)
                    if layer == 0:
                        act.wait_ge(pre_ready, j + 1)
                        nc.scalar.activation(g[:, p, :], pre[:, p, 0:F], ACT.Silu).then_inc(g_ready, 1)
                    else:
                        act.wait_ge(gu_ps, j + 1)
                        for q in range(2):
                            ins = nc.scalar.activation(g[:, p, q * N:(q + 1) * N], mem.ps[:, GU[0] + q, :], ACT.Gelu)
                            ins.then_inc(g_ready, 1)

            def keep_rows(j, s):
                act.wait_ge(xT_ps, j + 1)
                if not fixed(j) or j >= 2:
                    act.wait_ge(gu_ps, j - 1)
                nc.scalar.activation(xgT[:, s % 2, :, :].rearrange("p k t -> p (k t)"),
                                     mem.ps[:, XT, 0:D], ACT.Copy).then_inc(xT_kept, 1)

            keep_rows(0, 0)
            steps(body, nc.scalar)

        @block.vector
        def _(dve):
            if layer == 0:
                dve.wait_ge(mem.experts_in, 16 * 5)

            def keep_meta(j, s):
                dve.wait_ge(xT_ps, j + 1)
                if not fixed(j) or j >= 4:
                    dve.wait_ge(added, 16 * j - 48)
                nc.vector.tensor_copy(meta[:, s, 0:NE], xg[:, s, C_W:C_ID]).then_inc(meta_kept, 1)
                nc.vector.tensor_copy(meta[:, s, NE:NE + 1].bitcast(I32),
                                      xg[:, s, C_ID:C_ID + 1].bitcast(I32)).then_inc(meta_kept, 1)

            def body(j, s, of, r=None, u=None):
                p = s % 2
                if not fixed(j) or j < n_tiles:
                    dve.wait_ge(gu_ps, j + 1)
                    if not fixed(j) or j >= 2:
                        dve.wait_ge(hT_ps, copies * (j - 1))
                    if layer == 0:
                        nc.vector.tensor_tensor(
                            pre[:, p, :], mem.ps[:, GU[p], :],
                            mem.b1[:, bass.ds(of(0), 1), :].rearrange("p o f -> p (o f)"), ALU.add).then_inc(pre_ready, 1)
                        dve.wait_ge(g_ready, j + 1)
                        nc.vector.tensor_tensor(hact[:, p, :], g[:, p, :], pre[:, p, F:2 * F],
                                                ALU.mult).then_inc(hact_ready, 1)
                    else:
                        dve.wait_ge(g_ready, 2 * j + 2)
                        nc.vector.tensor_tensor(hact[:, p, :], g[:, p, :],
                                                mem.ps[:, GU[1]:GU[1] + 2, :].rearrange("p a b -> p (a b)"),
                                                ALU.mult).then_inc(hact_ready, 1)
                if not fixed(j) or j >= LAG:
                    v, e = (s - LAG) % 4, of(-LAG)
                    dve.wait_ge(y_ps, j - LAG + 1 + Y1)
                    dve.wait_ge(meta_kept, 2 * j - 2 * LAG + 2)
                    if not fixed(j) or j >= LAG + 4:
                        dve.wait_ge(added, 16 * j - 16 * (LAG + 3))
                    src = mem.ps[:, Y, 0:D]
                    if layer == 0:
                        nc.vector.tensor_tensor(y0[:, v % 2, :], src,
                                                mem.b2[:, bass.ds(e, 1), :].rearrange("p o f -> p (o f)"),
                                                ALU.add).then_inc(y_step, 1)
                        dve.wait_ge(y_step, j - LAG + 1)
                        src = y0[:, v % 2, :]
                    nc.vector.tensor_scalar(y[:, v, :], src, meta[:, v, bass.ds(e, 1)], None,
                                            ALU.mult).then_inc(y_ready, 1)
                if not fixed(j) or j < n_tiles:
                    keep_meta(j, s)

            steps(body, nc.vector, 0)

        @block.tensor
        def _(pe):
            if layer == 0:
                pe.wait_ge(mem.experts_in, 16 * 5)

            fill = {}

            def turn_rows(j, s):
                pe.wait_ge(loaded[s], 16 * (j // 4 + 1) if fixed(j) else fill[s])
                if not fixed(j) or j >= 1:
                    pe.wait_ge(xT_kept, j)
                for k in range(KD):
                    ins = nc.tensor.transpose(mem.ps[:, XT, k * P:(k + 1) * P], xg[:, s, k * P:(k + 1) * P], mem.ident)
                ins.then_inc(xT_ps, 1)

            def first_product(j, p, of):
                pe.wait_ge(xT_kept, j + 1)
                if layer == 0:
                    if not fixed(j) or j >= 2:
                        pe.wait_ge(pre_ready, j - 1)
                    w = mem.w1[:, bass.ds(of(0), 1), :].rearrange("p o (k f) -> p (o k) f", k=KD)
                    for k in range(KD):
                        ins = nc.tensor.matmul(mem.ps[:, GU[p], :], xgT[:, p, k, :], w[:, k, :],
                                               start=(k == 0), stop=(k == KD - 1))
                else:
                    pe.wait_ge(mem.w_loaded, 32 * of(0))
                    if not fixed(j) or j >= 1:
                        pe.wait_ge(hact_ready, j)
                    buffer = nc.tensor.snap((of(0) + 1) % 2)
                    w = mem.ring_gu[:, bass.ds(buffer, 1), :].rearrange("p o (k f) -> p (o k) f", k=KD)
                    for q in range(4):
                        for k in range(KD):
                            ins = nc.tensor.matmul(mem.ps[:, GU[0] + q, :], xgT[:, p, k, :],
                                                   w[:, k, q * N:(q + 1) * N], start=(k == 0), stop=(k == KD - 1))
                ins.then_inc(gu_ps, 1)

            def turn_activations(j, p):
                pe.wait_ge(hact_ready, j + 1)
                if not fixed(j) or j >= 1:
                    pe.wait_ge(hT_kept, copies * j)
                for c in range(FT):
                    ins = nc.tensor.transpose(mem.ps[:, HT + c // 4, (c % 4) * P:(c % 4 + 1) * P],
                                              hact[:, p, c * P:(c + 1) * P], mem.ident)
                    if c % 4 == 3 or c == FT - 1:
                        ins.then_inc(hT_ps, 1)

            def second_product(j, p, e):
                pe.wait_ge(hT_kept, copies * (j + 1))
                if not fixed(j) or j >= 1:
                    pe.wait_ge(y_step if layer == 0 else y_ready, j)
                if layer == 0:
                    w2 = mem.w2[:, bass.ds(e, 1), :]
                else:
                    w2 = mem.ring_dn[:, bass.ds(nc.tensor.snap((e + 1) % 2), 1), :]
                w2 = w2.rearrange("p o (c n) -> p (o c) n", c=FT)
                for c in range(FT):
                    ins = nc.tensor.matmul(mem.ps[:, Y, 0:D], hT[:, p, c, :], w2[:, c, :],
                                           start=(c == 0), stop=(c == FT - 1))
                ins.then_inc(y_ps, 1)

            def body(j, s, of, r=None, u=None):
                if r is not None:
                    fill[(s + 1) % 4] = 16 * (r + (u + 1) // 4 + 1)
                if not fixed(j) or j < n_tiles - 1:
                    turn_rows(j + 1, (s + 1) % 4)
                turn = not fixed(j) or 1 <= j <= n_tiles
                if layer == 1 and turn:
                    turn_activations(j - 1, (s - 1) % 2)
                if not fixed(j) or j < n_tiles:
                    first_product(j, s % 2, of)
                if layer == 0 and turn:
                    turn_activations(j - 1, (s - 1) % 2)
                if not fixed(j) or j >= LAG:
                    second_product(j - LAG, (s - LAG) % 2, of(-LAG))

            turn_rows(0, 0)
            steps(body, nc.tensor, layer)



def stage_chebyshev(nc, mem, io, sem):
    a = Arena(mem.arena, 0)
    feat = a.take(7 * T).rearrange("p (b t) -> p b t", b=7)
    kq = a.take(KD * T).rearrange("p (o t) -> p o t", o=KD)
    kv = a.take(2 * M * B * P).rearrange("p (o m b c) -> p o m b c", o=2, m=M, b=B)
    w_in = a.take(KD * 3 * D).rearrange("p (k n) -> p k n", k=KD)
    mem.w_out = a.take(KD * D).rearrange("p (k n) -> p k n", k=KD)
    V1 = mem.xw
    BUF = {2: 0, 3: 1, 4: 2, 5: 3, 6: 4, 7: 5, 8: 6, 9: 4, 10: 5}

    w_ready, step, stats_done, means_done = (sem("e_" + n) for n in ("w", "step", "stats", "means"))
    var_ready, sd_ready, xn_ready, turned, xT_ready = (sem("e_" + n) for n in ("var", "sd", "xn", "turned", "xT"))
    kv_ps, kv_taken, q_ps, q_raw, q_taken, x_ready = (sem("e_" + n) for n in ("kv_ps", "kv_taken", "q_ps", "q_raw", "q_taken", "x"))
    square, f_step, f_ready, used, kv_kept, o_kept = (
        sem("e_" + n) for n in ("square", "f_step", "f", "used", "kv_kept", "o_kept"))

    def wait_used(engine, ps, m):
        if m in (9, 10):
            engine.wait_ge(used, 11 * ps + m - 3 + 1)
        elif ps:
            last = {6: 9, 7: 10}.get(m, m)
            engine.wait_ge(used, 11 * (ps - 1) + last + 1)

    with nc.Block() as block:
        @block.sync
        def _(sp):
            sp.dma_start(w_in, io["w_in"]).then_inc(w_ready, 16)
            sp.dma_start(mem.w_out, io["w_out"]).then_inc(w_ready, 16)
            sp.dma_start(mem.beta[:, :, :], io["beta"]).then_inc(w_ready, 16)
            sp.wait_ge(w_ready, 48)

        @block.scalar
        def _(act):
            norm_root(nc, act, mem, var_ready, sd_ready)
            keep_turned(nc, act, mem, turned, xT_ready)
            for i in range(NT):
                act.wait_ge(kv_ps, i + 1)
                nc.scalar.activation(V1[:, i, 0:D], mem.ps[:, i % 8, D:2 * D], ACT.Copy).then_inc(kv_taken, 1)
            for ps in range(4):
                if ps:
                    act.wait_ge(f_ready, 9 * ps)
                for m in (2, 4, 6, 8, 10):
                    half = m // 2
                    if half == 1:
                        if ps == 0:
                            act.wait_ge(x_ready, NT)
                        elif ps == 2:
                            act.wait_ge(x_ready, NT + 8)
                        src = kq[:, ps % 2, :]
                    else:
                        act.wait_ge(f_ready, 9 * ps + half - 1)
                        src = feat[:, BUF[half], :]
                    wait_used(act, ps, m)
                    nc.scalar.activation(feat[:, BUF[m], :], src, ACT.Square).then_inc(square, 1)

        @block.vector
        def _(dve):
            link = step_counter(dve, step)
            norm_stats(nc, dve, link, mem, stats_done, means_done, lambda i: None, var_ready, sd_ready)
            norm_apply(nc, mem, xn_ready)
            dve.wait_ge(w_ready, 48)
            for i in range(NT):
                dve.wait_ge(kv_taken, i + 1)
                k_dst = kq[:, :, i * P:(i + 1) * P]
                nc.vector.tensor_scalar(k_dst, mem.ps[:, i % 8, 0:D].rearrange("p (o d) -> p o d", o=2), 0.25, 1.0,
                                        ALU.mult, ALU.min).then_inc(q_raw, 1)
                dve.wait_ge(q_raw, i + 1)
                nc.vector.tensor_scalar(k_dst, k_dst, -1.0, None, ALU.max).then_inc(x_ready, 1)

            def scale_sum(ps, m):
                dve.wait_ge(used, 11 * ps + m + 1)
                bank = m % 8
                nc.vector.scalar_tensor_tensor(
                    kv[:, ps, m, :, :], mem.ps[:, bank, 0:B * P].rearrange("p (b c) -> p b c", b=B),
                    mem.beta[:, ps, m:m + 1], mem.const[:, None, K_BLOCK:K_BLOCK + P].broadcast_to([P, B, P]),
                    ALU.mult, ALU.mult).then_inc(kv_kept, 1)

            for ps in range(4):
                if ps == 2:
                    dve.wait_ge(used, 22)
                    for n in range(8):
                        dve.wait_ge(q_ps, n + 1)
                        dst = kq[:, n // 4, (n % 4) * N:(n % 4 + 1) * N]
                        nc.vector.tensor_scalar(dst, mem.ps[:, n, :], 0.25, 1.0, ALU.mult, ALU.min).then_inc(q_raw, 1)
                        dve.wait_ge(q_raw, NT + n + 1)
                        nc.vector.tensor_scalar(dst, dst, -1.0, None, ALU.max).then_inc(x_ready, 1)
                x = kq[:, ps % 2, :]
                for m in range(2, M):
                    dst = feat[:, BUF[m], :]
                    if m % 2 == 0:
                        dve.wait_ge(square, 5 * ps + m // 2)
                        nc.vector.tensor_scalar(dst, dst, 2.0, -1.0, ALU.mult, ALU.add).then_inc(f_ready, 1)
                    else:
                        lo, hi = m // 2, m // 2 + 1
                        wait_used(dve, ps, m)
                        if m == 3:
                            dve.wait_ge(x_ready, NT + 8 * (ps // 2))
                        dve.wait_ge(f_ready, 9 * ps + hi - 1)
                        lo_f = x if lo == 1 else feat[:, BUF[lo], :]
                        nc.vector.tensor_tensor(dst, lo_f, feat[:, BUF[hi], :], ALU.mult).then_inc(f_step, 1)
                        dve.wait_ge(f_step, 4 * ps + m // 2)
                        nc.vector.scalar_tensor_tensor(dst, dst, 2.0, x, ALU.mult, ALU.subtract).then_inc(f_ready, 1)
                    if ps < 2 and m >= 3:
                        scale_sum(ps, m - 3)
                if ps < 2:
                    for m in range(M - 3, M):
                        scale_sum(ps, m)
            for n in range(8):
                dve.wait_ge(used, 22 + 11 * (n // 4) + 11)
                nc.vector.tensor_copy(mem.xT[:, n // 4, (n % 4) * N:(n % 4 + 1) * N], mem.ps[:, n, :]).then_inc(o_kept, 1)

        @block.tensor
        def _(pe):
            transpose_rows(nc, pe, mem, lambda i, k: mem.xw[:, i, k * P:(k + 1) * P],
                           lambda i: pe.wait_ge(xn_ready, i + 1), turned)
            pe.wait_ge(xT_ready, 8)
            pe.wait_ge(w_ready, 48)
            for i in range(NT):
                if i >= 8:
                    pe.wait_ge(kv_taken, i - 7)
                    pe.wait_ge(x_ready, i - 7)
                for k in range(KD):
                    ins = nc.tensor.matmul(mem.ps[:, i % 8, :], mem.xT[:, k, i * P:(i + 1) * P], w_in[:, k, D:3 * D],
                                           start=(k == 0), stop=(k == KD - 1))
                ins.then_inc(kv_ps, 1)
            pe.wait_ge(kv_taken, NT)
            pe.wait_ge(x_ready, NT)
            for ps in range(2):
                for m in range(M):
                    n = 11 * ps + m
                    if m >= 8:
                        pe.wait_ge(kv_kept, n - 7)
                    elif ps == 1:
                        pe.wait_ge(kv_kept, m + 8 + 1 if m < 3 else m + 1)
                    if m >= 2:
                        pe.wait_ge(f_ready, 9 * ps + m - 1)
                    for i in range(NT):
                        lhs = mem.ones[:, 0:P] if m == 0 else (kq[:, ps, i * P:(i + 1) * P] if m == 1 else
                                                               feat[:, BUF[m], i * P:(i + 1) * P])
                        b = i // QT
                        ins = nc.tensor.matmul(mem.ps[:, m % 8, b * P:(b + 1) * P], lhs, V1[:, i, ps * P:(ps + 1) * P],
                                               start=(i % QT == 0), stop=(i % QT == QT - 1))
                    ins.then_inc(used, 1)
            pe.wait_ge(kv_kept, 22)
            for n in range(8):
                o, c = n // 4, n % 4
                for k in range(KD):
                    ins = nc.tensor.matmul(mem.ps[:, n, :], w_in[:, k, o * P:(o + 1) * P], mem.xT[:, k, c * N:(c + 1) * N],
                                           start=(k == 0), stop=(k == KD - 1))
                ins.then_inc(q_ps, 1)
            pe.wait_ge(x_ready, NT + 8)
            for ps in range(2, 4):
                o = ps - 2
                for m in range(M):
                    if m >= 2:
                        pe.wait_ge(f_ready, 9 * ps + m - 1)
                    for c in range(4):
                        rhs = (mem.ones[:, 0:N] if m == 0 else kq[:, o, c * N:(c + 1) * N] if m == 1 else
                               feat[:, BUF[m], c * N:(c + 1) * N])
                        ins = nc.tensor.matmul(mem.ps[:, 4 * o + c, :], kv[:, o, m, c // 2, :], rhs,
                                               start=(m == 0), stop=(m == M - 1))
                    ins.then_inc(used, 1)
            pe.wait_ge(o_kept, 8)



class Memory:
    pass


def build_tower(nc, io, out):
    with ExitStack() as ctx:
        def sb(name, shape, dt=F32):
            return ctx.enter_context(nc.sbuf_tensor(name, shape, dt))[(slice(None),) * len(shape)]

        def sem(name):
            return ctx.enter_context(nc.semaphore(name))

        mem = Memory()
        mem.ps = ctx.enter_context(nc.psum_tensor("banks", [P, 8, N], F32))[:, :, :]
        mem.h = sb("h", [P, NT, D])
        mem.xw = sb("xw", [P, NT, ROW])
        mem.xT = sb("xT", [P, KD, T])
        mem.arena = sb("arena", [P, ARENA])
        mem.const = sb("const", [P, K_ALL])
        mem.ident = mem.const[:, K_IDENT:K_IDENT + P]
        mem.ident_bf = sb("ident_bf", [P, P], BF16)
        mem.zero_bf = sb("zero_bf", [P, P], BF16)
        mem.ones_bf = sb("ones_bf", [P, P], BF16)
        mem.tri_bf = sb("tri_bf", [P, P], BF16)
        mem.ones = sb("ones", [P, N])
        mem.ids = sb("ids", [P, NT], I32)
        mem.bo = sb("bo", [P, D])
        wo = sb("wo_sb", [P, KD, D])
        mem.wo = wo[:, :, :]
        mem.gate = sb("gate", [P, KD, NE])
        mem.gate_b = sb("gate_b", [P, NE])
        mem.beta = sb("beta", [P, 2, M])
        mem.bn = sb("bn", [P, NT, 6])
        mem.mv = sb("mv", [P, NT, 2])
        mem.ve, mem.r2, mem.sd, mem.rstd = (sb(n, [P, NT]) for n in ("ve", "r2", "sd", "rstd"))
        mem.lg = sb("lg", [P, NT * NE])
        mem.s16 = sb("s16", [P, NT])
        mem.rank = sb("rank", [P, NT * NE])
        mem.mask = sb("mask", [P, 3, NT * NE])
        mem.mask_bf = sb("mask_bf", [P, NT * NE], BF16)
        mem.small = sb("small", [P, 6, NE])
        mem.slots = sb("slots", [P, TOP_K, NT], I32)
        mem.tf = sb("tf", [P, 2, 4 * N_WORDS + 2])
        mem.words = sb("words", [P, 2, N_WORDS])
        mem.tab = sb("tab", [P, 2, N_WORDS], I32)
        mem.places = sb("places", [P, 4, NE], I32)
        mem.n_has = sb("n_has", [P, 2])
        mem.b1_shared = sb("b1_shared", [P, 2 * F0 // P])
        mem.NM = sb("NM", [P, 2, 16])
        mem.mr = sb("mr", [P, 2, 16])
        mem.MP = sb("MP", [P, 2, P], BF16)
        mem.mTs = sb("mTs", [48, 2, P], BF16)
        mem.den = sb("den", [P, 16])

        a = Arena(mem.arena, 0)
        mem.QO = a.take(3 * HG * S // 2).bitcast(BF16).rearrange("p (s h t) -> p s h t", s=3, h=HG)
        mem.e = a.take(4 * 2 * N).rearrange("p (s n) -> p s n", s=4)
        mem.po = a.take(2 * N).rearrange("p (s n) -> p s n", s=2)
        mem.V_at = a.at
        mem.KO = a.take(3 * HG * S // 2).bitcast(BF16).rearrange("p (s h t) -> p s h t", s=3, h=HG)
        mem.V = a.take(NIT * QT * HG * DH).rearrange("p (i c x) -> p i c x", i=NIT, c=QT)
        mem.vst = a.take(3 * QT * HG * 32).rearrange("p (s c h x) -> p s c h x", s=3, c=QT, h=HG)
        mem.ao = mem.xT[:, :, :].rearrange("p k (i q x) -> p (k i) q x", i=NIT // KD // 2, q=QT)
        assert a.at <= ARENA - (NE + 1) * KD * 2 * F0
        a = Arena(mem.arena, 0)
        mem.w2 = a.take((NE + 1) * F0 // P * D).rearrange("p (e n) -> p e n", e=NE + 1)
        mem.b1 = a.take(NE * 2 * F0).rearrange("p (e n) -> p e n", e=NE)
        mem.b2 = a.take((NE + 1) * D).rearrange("p (e n) -> p e n", e=NE + 1)
        mem.layer0_at = a.at
        mem.w1_at = ARENA - (NE + 1) * KD * 2 * F0
        mem.w1 = Arena(mem.arena, mem.w1_at).take((NE + 1) * KD * 2 * F0).rearrange("p (e n) -> p e n", e=NE + 1)
        mem.ring_at = ARENA - 2 * (KD * 2 * F1 + F1 // P * D)
        a = Arena(mem.arena, mem.ring_at)
        mem.ring_gu = a.take(2 * KD * 2 * F1).rearrange("p (s n) -> p s n", s=2)
        mem.ring_dn = a.take(2 * F1 // P * D).rearrange("p (s n) -> p s n", s=2)

        def dram(name, shape, dt=F32):
            return nc.dram_tensor(name, shape, dt, kind="Internal").ap()

        mem.qk_dram = dram("qk_parts", [2, 3, B * D, S], BF16)
        mem.row_dram = dram("max_rows", [2, 48, P], BF16)
        mem.rows = [dram(f"rows{i}", [NRT * P, ROW]) for i in range(2)]
        mem.acc = (dram("acc0", [T + TRASH, D]), out)
        mem.pads_in, mem.experts_in, mem.w_loaded = sem("pads_in"), sem("experts_in"), sem("w_loaded")
        mem.acc_in = [sem(f"acc{i}_in") for i in range(2)]

        stage_embed_qkv(nc, mem, io, sem)
        stage_attention(nc, mem, io, sem)
        stage_router(nc, mem, io, sem, 0)
        stage_experts(nc, mem, io, sem, 0)
        stage_chebyshev(nc, mem, io, sem)
        stage_router(nc, mem, io, sem, 1)
        stage_experts(nc, mem, io, sem, 1)


def constants():
    p = np.arange(P)
    c = np.zeros((P, K_ALL), np.float32)
    c[:, K_IDENT:K_IDENT + P] = np.eye(P)
    c[:, K_TRI:K_TRI + P] = p[:, None] < p[None, :]
    c[:, K_BLOCK:K_BLOCK + P] = p[:, None] // DH == p[None, :] // DH
    e = np.arange(NE)
    c[:, K_LT:K_LT + NE * NE] = (e[None, :] < e[:, None]).reshape(1, -1)
    c[:, K_J128:K_J128 + NT] = P * np.arange(NT)
    c[:, K_J:K_J + NRT] = np.arange(NRT)
    c[:, K_PAD + C_ID] = (T + p).astype(np.int32).view(np.float32)
    c[:, K_TOK:K_TOK + NT] = P * np.arange(NT)[None, :] + p[:, None]
    return c


def kernel(**inputs):
    import concourse.bacc as bacc
    from concourse.bass_utils import run_bass_kernel_spmd

    x = {k: np.asarray(v) for k, v in inputs.items()}

    def halves(w):
        return w.reshape(-1, P, w.shape[-1]).transpose(1, 0, 2)

    def experts(w):
        return w.reshape(w.shape[0], -1, P, w.shape[-1]).transpose(0, 2, 1, 3).reshape(w.shape[0], P, -1)

    cat = np.concatenate
    arrays = {
        "ids": x["x"].reshape(NT, P).T,
        "tok": cat([x["L0_tok_weight"], x["L0_tok_scales"]], 1),
        "const": constants(),
        "wq": halves(x["L0_attn_Wq"].T), "wk": halves(x["L0_attn_Wk"].T), "wv": halves(x["L0_attn_Wv"].T),
        "wo": halves(x["L0_attn_Wo"].T), "bo": x["L0_attn_bo"],
        "gate0": halves(x["L0_ffn_gate_w"]), "gate_b": x["L0_ffn_gate_b"],
        "w1": experts(cat([x["L0_ffn_rw1"], x["L0_ffn_sw1"]])),
        "w2": experts(cat([x["L0_ffn_rw2"], x["L0_ffn_sw2"]])),
        "b1": x["L0_ffn_rb1"], "b1_shared": x["L0_ffn_sb1"].reshape(-1, P).T,
        "b2": cat([x["L0_ffn_rb2"], x["L0_ffn_sb2"]]),
        "w_in": halves(x["L1_attn_w_in"].T), "w_out": halves(x["L1_attn_w_out"].T),
        "beta": np.repeat(x["L1_attn_beta"], DH, axis=0).reshape(2, P, M).transpose(1, 0, 2),
        "gate1": halves(x["L1_ffn_gate_w"].T),
        "gu": experts(x["L1_ffn_gate_up_w"].transpose(0, 2, 1)),
        "dn": experts(x["L1_ffn_down_w"].transpose(0, 2, 1)),
    }
    nc = bacc.Bacc("TRN2", target_bir_lowering=False, num_devices=1)
    io, feeds = {}, {}
    for name, a in arrays.items():
        a = np.ascontiguousarray(a)
        feeds["in_" + name] = a
        io[name] = nc.dram_tensor("in_" + name, a.shape, mybir.dt.from_np(a.dtype), kind="ExternalInput").ap()
    out = nc.dram_tensor("out_rows", (T + TRASH, D), F32, kind="ExternalOutput").ap()
    build_tower(nc, io, out)
    r = run_bass_kernel_spmd(nc, [feeds], core_ids=[0])
    return r.results[0]["out_rows"][0:T].reshape(B, S, D)
```

```python
from contextlib import ExitStack

import numpy as np
import concourse.bass as bass
from concourse import mybir

F32 = mybir.dt.float32
BF16 = mybir.dt.bfloat16
I32 = mybir.dt.int32
U32 = mybir.dt.uint32
ALU = mybir.AluOpType
ACT = mybir.ActivationFunctionType
AX = mybir.AxisListType

P = 128
B, S, D = 2, 1024, 256
T = B * S
NT = T // P
KD = D // P
H, DH = 16, 16
HG = 4
NG = H // HG
NIT = B * NG
QT = S // P
N = 512
NE = 8
TOP_K = 2
NRT = (TOP_K * T) // P + NE - 1
F0, F1 = 256, 1024
M = 11
VOCAB = 50257
LN_EPS = 1e-5
DEN_EPS = 1e-8

HEAD = 5
N_WORDS = -(-NRT // 4)
assert (NRT - 2 - HEAD) % 4 == 0 and NE < 16

C_W = D
C_ID = D + NE
ROW = C_ID + 1
TRASH = P

Q_PARTS = (0, 0, 1, 1, 0, 2)
K_PARTS = (0, 1, 0, 1, 2, 0)
KROWS = 16 * len(Q_PARTS)
KMAX = KROWS + 3

K_IDENT = 0
K_TRI = K_IDENT + P
K_BLOCK = K_TRI + P
K_LT = K_BLOCK + P
K_J128 = K_LT + NE * NE
K_J = K_J128 + NT
K_PAD = K_J + NRT
K_TOK = K_PAD + ROW
K_MINUS = K_TOK + NT
K_ALL = K_MINUS + 1

ARENA = 35840


class Arena:

    def __init__(self, tensor, at):
        self.tensor, self.at = tensor, at

    def take(self, words, parts=P):
        piece = self.tensor[0:parts, self.at:self.at + words]
        self.at += words
        assert self.at <= ARENA, self.at
        return piece


def step_counter(engine, sem, start=0):
    count = [start]

    def link(ins):
        ins.then_inc(sem, 1)
        count[0] += 1
        engine.wait_ge(sem, count[0])

    return link



def norm_rows(nc, dve, link, mem, prepare, follow, stats_done, means_done, var_ready, sd_ready, xn_ready):
    def statistics(c):
        prepare(c)
        for i in range(4 * c, 4 * c + 4):
            nc.vector.bn_stats(mem.bn[:, i, :], mem.h[:, i, :]).then_inc(stats_done, 1)
        for i in range(4 * c, 4 * c + 4):
            dve.wait_ge(stats_done, i + 1)
            nc.vector.bn_aggr(mem.mv[:, i, :], mem.bn[:, i, :]).then_inc(means_done, 1)
        dve.wait_ge(means_done, 4 * c + 4)
        nc.vector.tensor_scalar(mem.ve[:, 4 * c:4 * c + 4], mem.mv[:, 4 * c:4 * c + 4, 1], LN_EPS, None,
                                ALU.add).then_inc(var_ready, 1)

    def finish(c):
        g = slice(4 * c, 4 * c + 4)
        dve.wait_ge(sd_ready, c + 1)
        link(nc.vector.reciprocal(mem.rstd[:, g], mem.sd[:, g]))
        link(nc.vector.tensor_tensor(mem.r2[:, g], mem.rstd[:, g], mem.rstd[:, g], ALU.mult))
        link(nc.vector.tensor_tensor(mem.r2[:, g], mem.r2[:, g], mem.ve[:, g], ALU.mult))
        link(nc.vector.tensor_scalar(mem.r2[:, g], mem.r2[:, g], -0.5, 1.5, ALU.mult, ALU.add))
        link(nc.vector.tensor_tensor(mem.rstd[:, g], mem.rstd[:, g], mem.r2[:, g], ALU.mult))
        for i in range(4 * c, 4 * c + 4):
            nc.vector.tensor_scalar(mem.xw[:, i, 0:D], mem.h[:, i, :], mem.mv[:, i, 0:1], mem.rstd[:, i:i + 1],
                                    ALU.subtract, ALU.mult).then_inc(xn_ready, 1)

    statistics(0)
    for c in range(NT // 4):
        if c + 1 < NT // 4:
            statistics(c + 1)
        finish(c)
        follow(c)


def norm_root(nc, act, mem, c, var_ready, sd_ready):
    act.wait_ge(var_ready, c + 1)
    nc.scalar.activation(mem.sd[:, 4 * c:4 * c + 4], mem.ve[:, 4 * c:4 * c + 4], ACT.Sqrt).then_inc(sd_ready, 1)


def transpose_rows(nc, pe, mem, source, ready, turned, groups=range(NT // 4), bank=lambda c: 2 * c):
    for c in groups:
        for i in range(4 * c, 4 * c + 4):
            ready(i)
            for k in range(KD):
                ins = nc.tensor.transpose(mem.ps[:, bank(c) + k, (i % 4) * P:(i % 4 + 1) * P],
                                          source(i, k), mem.ident)
                if i % 4 == 3:
                    ins.then_inc(turned, 1)


def keep_turned(nc, act, mem, c, turned, xT_ready, to=None, bank=lambda c: 2 * c):
    to = mem.xT if to is None else to
    for k in range(KD):
        act.wait_ge(turned, 2 * c + k + 1)
        nc.scalar.activation(to[:, k, c * N:(c + 1) * N], mem.ps[:, bank(c) + k, :], ACT.Copy).then_inc(xT_ready, 1)


def root_and_keep(nc, act, mem, var_ready, sd_ready, turned, xT_ready):
    norm_root(nc, act, mem, 0, var_ready, sd_ready)
    for c in range(NT // 4):
        if c + 1 < NT // 4:
            norm_root(nc, act, mem, c + 1, var_ready, sd_ready)
        keep_turned(nc, act, mem, c, turned, xT_ready)



def load_operands(sp, mem, it, which=range(2 * len(Q_PARTS))):
    for n in which:
        w, j = n // len(Q_PARTS), n % len(Q_PARTS)
        X, part = (mem.QO, Q_PARTS[j]) if w == 0 else (mem.KO, K_PARTS[j])
        src = mem.qk_dram[w, part, it * 64:(it + 1) * 64, :].rearrange("(h d) t -> d h t", h=HG)
        sp.dma_start(X[16 * j:16 * j + 16, it % 3, :, :], src).then_inc(mem.qk_in[it % 3], 16)


def stage_embed_qkv(nc, mem, io, sem):
    a = Arena(mem.arena, mem.free_at)
    emb = a.take(NT * (D + 2)).rearrange("p (i c) -> p i c", i=NT)
    parts = a.take(4 * 3 * N // 2).bitcast(BF16).rearrange("p (s a n) -> p s a n", s=4, a=3)
    rest = a.take(2 * N).rearrange("p (s n) -> p s n", s=2)
    wqk = a.take(2 * KD * D).rearrange("p (w k n) -> p w k n", w=2, k=KD)
    wv = a.take(KD * D).rearrange("p (k n) -> p k n", k=KD)
    sc2 = a.take(NT * 2).rearrange("p (i g) -> p i g", i=NT)
    ids_in, w_in, const_in = sem("ids_in"), sem("w_in"), sem("const_in")
    gathered = [sem(f"gathered{c}") for c in range(4)]
    step, var_ready, sd_ready = sem("a_step"), sem("a_var"), sem("a_sd")
    xn_ready, turned, xT_ready = sem("a_xn"), sem("a_turned"), sem("a_xT")
    qk_ps, v_ps, part1, rest_ok, part2, part3 = (sem("a_" + n) for n in ("qk_ps", "v_ps", "part1", "rest", "part2", "part3"))
    filled = sem("a_filled")
    v_kept, h_ready, stats_done, means_done = sem("a_v_kept"), sem("a_h"), sem("a_stats"), sem("a_means")
    stored = [sem(f"a_stored{i}") for i in range(4)]
    NP = 16

    with nc.Block() as block:
        @block.sync
        def _(sp):
            sp.dma_start(mem.ids[:, :], io["ids"]).then_inc(ids_in, 16)
            sp.dma_start(mem.const[:, :], io["const"]).then_inc(const_in, 16)
            sp.dma_start(wqk[:, 0, :, :], io["wq"]).then_inc(w_in, 16)
            sp.dma_start(wqk[:, 1, :, :], io["wk"]).then_inc(w_in, 16)
            sp.dma_start(wv, io["wv"]).then_inc(w_in, 16)
            sp.dma_start(mem.wo, io["wo"]).then_inc(w_in, 16)
            sp.dma_start(mem.bo, io["bo"].partition_broadcast(P)).then_inc(w_in, 16)
            for n in range(NP):
                c, w, o = n // 4, (n // 2) % 2, n % 2
                sp.wait_ge(part3, n + 1)
                b, t0 = c // 2, (c % 2) * N
                dst = mem.qk_dram[w, :, b * D + o * P:b * D + (o + 1) * P, t0:t0 + N]
                sp.dma_start(dst.rearrange("a p t -> p a t"), parts[:, n % 4, :, :]).then_inc(stored[n % 4], 16)
                if n >= NP // 2:
                    if n == NP // 2:
                        for i in range(4):
                            sp.wait_ge(stored[i], 16 * NP // 8 + (16 if i == n % 4 else 0))
                    first = 3 * (n - NP // 2)
                    load_operands(sp, mem, first // 12, range(first % 12, first % 12 + 3))
            for i in range(4):
                sp.wait_ge(stored[i], 16 * NP // 4)
            sp.wait_ge(w_in, 16 * 5)
            sp.wait_ge(const_in, 16)

        @block.gpsimd
        def _(pool):
            pool.wait_ge(ids_in, 16)
            for i in range(NT):
                nc.gpsimd.indirect_dma_start(
                    out=emb[:, i, :], out_offset=None, in_=io["tok"],
                    in_offset=bass.IndirectOffsetOnAxis(ap=mem.ids[:, i:i + 1].bitcast(U32), axis=0),
                    bounds_check=VOCAB - 1, oob_is_err=False).then_inc(gathered[i // 4], 16)
            nc.gpsimd.memset(mem.KO[KROWS:KMAX, :, :, :], 1.0).then_inc(filled, 1)
            pool.wait_ge(filled, 1)
            nc.gpsimd.memset(mem.vst[:, :, :, :, DH:DH + 1], 1.0).then_inc(filled, 1)
            pool.wait_ge(filled, 2)
            nc.gpsimd.memset(mem.vst[:, :, :, :, DH + 1:32], 0.0).then_inc(filled, 1)
            pool.wait_ge(filled, 3)
            nc.gpsimd.memset(mem.MP[:, :, :], 0.0).then_inc(filled, 1)

        @block.vector
        def _(dve):
            link = step_counter(dve, step)
            dve.wait_ge(const_in, 16)
            nc.vector.tensor_copy(mem.ident_bf[:, :], mem.ident)
            nc.vector.memset(mem.ones_bf[:, :], 1.0)
            nc.vector.memset(mem.zero_bf[:, :], 0.0)
            nc.vector.memset(mem.ones[:, :], 1.0)
            nc.vector.tensor_copy(mem.tri_bf[:, :], mem.const[:, K_TRI:K_TRI + P])

            def embed(c):
                g = slice(4 * c, 4 * c + 4)
                dve.wait_ge(gathered[c], 64)
                nc.vector.tensor_scalar(sc2[:, g, :], emb[:, g, D:D + 2], 1e-8, 2.0, ALU.max, ALU.mult).then_inc(h_ready, 1)
                nc.vector.tensor_scalar(emb[:, g, 0:D], emb[:, g, 0:D], 0.0, 0.5, ALU.is_ge, ALU.subtract).then_inc(h_ready, 1)
                dve.wait_ge(h_ready, 3 * c + 2)
                nc.vector.tensor_tensor(
                    mem.h[:, g, :].rearrange("p i (g c) -> p i g c", g=2),
                    emb[:, g, 0:D].rearrange("p i (g c) -> p i g c", g=2),
                    sc2[:, g, :, None].broadcast_to([P, 4, 2, P]), ALU.mult).then_inc(h_ready, 1)
                dve.wait_ge(h_ready, 3 * c + 3)

            def third_part(n):
                dve.wait_ge(part2, n + 1)
                nc.vector.tensor_tensor(parts[:, n % 4, 2, :], rest[:, n % 2, :], parts[:, n % 4, 1, :],
                                        ALU.subtract).then_inc(part3, 1)

            def split(n):
                dve.wait_ge(part1, n + 1)
                if n >= 2:
                    dve.wait_ge(part3, n - 1)
                nc.vector.scalar_tensor_tensor(rest[:, n % 2, :], mem.ps[:, n % 4, :], 0.25 if (n // 2) % 2 == 0 else 1.0,
                                               parts[:, n % 4, 0, :], ALU.mult, ALU.subtract).then_inc(rest_ok, 1)
                if n >= 1:
                    third_part(n - 1)
                if n % 2 == 1:
                    j = n // 2
                    dve.wait_ge(v_ps, j + 1)
                    b, c0 = j // 4, 2 * (j % 4)
                    for g in range(NG):
                        nc.vector.tensor_copy(
                            mem.V[:, b * NG + g, c0:c0 + 2, :],
                            mem.ps[:, 4 + j % 2, :].rearrange("p (c x) -> p c x", c=2)[:, :, g * 64:(g + 1) * 64],
                        ).then_inc(v_kept, 1)

            def follow(c):
                for n in range(4 * c - 4, 4 * c) if c else ():
                    split(n)

            norm_rows(nc, dve, link, mem, embed, follow, stats_done, means_done, var_ready, sd_ready, xn_ready)
            for n in range(NP - 4, NP):
                split(n)
            third_part(NP - 1)

        @block.scalar
        def _(act):
            def second_part(n):
                act.wait_ge(rest_ok, n + 1)
                nc.scalar.activation(parts[:, n % 4, 1, :], rest[:, n % 2, :], ACT.Copy).then_inc(part2, 1)

            def first_and_second(n):
                act.wait_ge(qk_ps, n + 1)
                if n >= 4:
                    act.wait_ge(stored[n % 4], 16 * (n // 4))
                nc.scalar.activation(parts[:, n % 4, 0, :], mem.ps[:, n % 4, :], ACT.Copy,
                                     scale=0.25 if (n // 2) % 2 == 0 else 1.0).then_inc(part1, 1)
                if n >= 1:
                    second_part(n - 1)

            norm_root(nc, act, mem, 0, var_ready, sd_ready)
            norm_root(nc, act, mem, 1, var_ready, sd_ready)
            for c in range(4):
                keep_turned(nc, act, mem, c, turned, xT_ready, bank=lambda c: 6)
                if 1 <= c < 3:
                    norm_root(nc, act, mem, c + 1, var_ready, sd_ready)
                for n in range(4 * c - 4, 4 * c) if c else ():
                    first_and_second(n)
            for n in range(NP - 4, NP):
                first_and_second(n)
            second_part(NP - 1)

        @block.tensor
        def _(pe):
            def turn(c):
                if c >= 1:
                    pe.wait_ge(xT_ready, 2 * c)
                transpose_rows(nc, pe, mem, lambda i, k: mem.xw[:, i, k * P:(k + 1) * P],
                               lambda i: pe.wait_ge(xn_ready, i + 1), turned, groups=(c,), bank=lambda c: 6)

            pe.wait_ge(const_in, 16)
            turn(0)
            for n in range(NP):
                c, w, o = n // 4, (n // 2) % 2, n % 2
                if n % 4 == 0:
                    if c + 1 < 4:
                        turn(c + 1)
                    if c == 0:
                        pe.wait_ge(w_in, 16 * 5)
                    pe.wait_ge(xT_ready, 2 * c + 2)
                if n >= 4:
                    pe.wait_ge(rest_ok, n - 3)
                for k in range(KD):
                    ins = nc.tensor.matmul(mem.ps[:, n % 4, :], wqk[:, w, k, o * P:(o + 1) * P],
                                           mem.xT[:, k, c * N:(c + 1) * N], start=(k == 0), stop=(k == KD - 1))
                ins.then_inc(qk_ps, 1)
                if n % 2 == 1:
                    j = n // 2
                    if j >= 2:
                        pe.wait_ge(v_kept, NG * (j - 1))
                    for i in (2 * j, 2 * j + 1):
                        for k in range(KD):
                            ins = nc.tensor.matmul(mem.ps[:, 4 + j % 2, (i % 2) * D:(i % 2 + 1) * D],
                                                   mem.xT[:, k, i * P:(i + 1) * P], wv[:, k, :],
                                                   start=(k == 0), stop=(k == KD - 1))
                    ins.then_inc(v_ps, 1)



def stage_attention(nc, mem, io, sem):
    qk_in = mem.qk_in
    row_out = sem("b_row_out")
    row_in = [sem(f"b_row_in{q}") for q in range(2)]
    st_ready, exp_done, pv_done = (sem("b_" + n) for n in ("st", "exp", "pv"))
    ms_ready, ms_free, mp_step, mt_ready, mt_kept = (sem("b_" + n) for n in ("ms", "ms_free", "mp", "mt", "mt_kept"))
    v_staged, po_ready, outT_ready, norm_step, norm_done = (
        sem("b_" + n) for n in ("v_staged", "po", "outT", "norm_step", "norm"))
    UH = 2 * QT
    MH = HG * 4
    QO, KO = mem.QO, mem.KO
    assert MH == UH

    def pair_of(U):
        b = 2 * ((2 * U) % 3)
        return slice(b, b + 2)

    def unit_mod(s, qb, u):
        return 2 * UH * s + UH * qb + u

    def halves(it):
        return ((it, 0), (it, 1))

    def iterations(body, engine):
        body(0, 0)
        with engine.Fori(0, 2) as r:
            for s in (1, 2, 3):
                body(3 * r + s, s % 3)
        body(NIT - 1, (NIT - 1) % 3, last=True)

    def first_pair(n):
        return slice(2 * (n % 3), 2 * (n % 3) + 2)

    with nc.Block() as block:
        @block.sync
        def _(sp):
            def max_rows(G):
                it, qb = G // 2, G % 2
                sp.wait_ge(mt_kept, G + 1)
                if G >= 2:
                    sp.wait_ge(row_in[qb], 16 * (G // 2))
                sp.dma_start(mem.row_dram[qb], mem.mTs[0:48, qb, :]).then_inc(row_out, 16)
                sp.wait_ge(row_out, 16 * (G + 1))
                sp.dma_start(QO[KROWS:KMAX, it % 3, :, qb * N:(qb + 1) * N],
                             mem.row_dram[qb].rearrange("(a h q) p -> a h (q p)", a=3, h=HG)).then_inc(row_in[qb], 16)

            sp.dma_start(mem.w1, io["w1"].rearrange("e p n -> p e n")).then_inc(mem.experts_in, 16)
            max_rows(0)
            max_rows(1)
            for it in range(NIT):
                if it + 2 < NIT:
                    if it >= 1:
                        sp.wait_ge(pv_done, 2 * UH * it)
                    load_operands(sp, mem, it + 2)
                if it < 2:
                    sp.dma_start(mem.rows[it].rearrange("(j p) c -> p j c", p=P),
                                 mem.const[:, None, K_PAD:K_PAD + ROW].broadcast_to([P, NRT, ROW])).then_inc(mem.pads_in, 16)
                for G in (2 * it + 2, 2 * it + 3):
                    if G < 2 * NIT:
                        max_rows(G)

        @block.gpsimd
        def _(pool):
            def max_parts(G, qb):
                pool.wait_ge(ms_free, MH * (G + 1))
                if not (type(G) is int and G < 2):
                    pool.wait_ge(mt_ready, G - 1)
                nm = mem.NM[:, qb, :]
                mp = mem.MP[:, qb:qb + 1, 0:48].rearrange("p o (a c) -> p o a c", a=3)
                nc.gpsimd.tensor_copy(mp[:, 0, 0, :], nm).then_inc(mp_step, 1)
                pool.wait_ge(mp_step, 4 * G + 1)
                nc.gpsimd.tensor_tensor(mem.mr[:, qb, :], nm, mp[:, 0, 0, :], ALU.subtract).then_inc(mp_step, 1)
                pool.wait_ge(mp_step, 4 * G + 2)
                nc.gpsimd.tensor_copy(mp[:, 0, 1, :], mem.mr[:, qb, :]).then_inc(mp_step, 1)
                pool.wait_ge(mp_step, 4 * G + 3)
                nc.gpsimd.tensor_tensor(mp[:, 0, 2, :], mem.mr[:, qb, :], mp[:, 0, 1, :],
                                        ALU.subtract).then_inc(mp_step, 1)

            def stage_v(it, slot):
                nc.gpsimd.tensor_copy(mem.vst[:, slot, :, :, 0:DH],
                                      mem.V[:, bass.ds(it, 1), :, :].rearrange("p o c (h d) -> p (o c) h d", h=HG),
                                      ).then_inc(v_staged, 1)

            def body(it, s, last=False):
                if not last:
                    pool.wait_ge(pv_done, UH * (2 * it + 1))
                    stage_v(it + 1, (s + 1) % 3)
                    max_parts(2 * it + 2, 0)
                    max_parts(2 * it + 3, 1)

            stage_v(0, 0)
            max_parts(0, 0)
            max_parts(1, 1)
            nc.gpsimd.tensor_tensor(mem.h[:, :, :], mem.h[:, :, :],
                                    mem.bo[:, None, :].broadcast_to([P, NT, D]), ALU.add)
            for it in range(NIT):
                body(it, it % 3, last=(it == NIT - 1))

        @block.scalar
        def _(act):
            def keep_rows(G, qb, bank):
                act.wait_ge(mt_ready, G + 1)
                if not (type(G) is int and G < 2):
                    act.wait_ge(row_out, 16 * (G - 1))
                nc.scalar.activation(mem.mTs[0:48, qb, :],
                                     mem.ps[0:48, bank, 0:64].bitcast(BF16), ACT.Copy).then_inc(mt_kept, 1)

            def keep_out(half, qb):
                act.wait_ge(pv_done, UH * (half + 1))
                if not (type(half) is int and half < 2):
                    act.wait_ge(outT_ready, half - 1)
                nc.scalar.activation(mem.po[:, qb, :], mem.ps[:, 6 + qb, :], ACT.Copy).then_inc(po_ready, 1)

            def body(it, s, last=False):
                for qb in (0, 1):
                    for u in range(UH):
                        U = 2 * UH * it + UH * qb + u
                        act.wait_ge(st_ready, U + 1)
                        if not (type(it) is int and U < 4):
                            act.wait_ge(pv_done, U - 3)
                        nc.scalar.activation(mem.e[:, u % 4, :], mem.ps[:, pair_of(unit_mod(s, qb, u)), :],
                                             ACT.Exp).then_inc(exp_done, 1)
                        if u == 1 and not (type(it) is int and it == 0 and qb == 0):
                            keep_out(2 * it + qb - 1, 1 - qb)
                        if u == 7:
                            if not (last and qb == 1) and not (type(it) is int and it == 0 and qb == 0):
                                keep_rows(2 * it + qb + 1, 1 - qb, 7 - qb)

            keep_rows(0, 0, 6)
            keep_rows(1, 1, 7)
            iterations(body, nc.scalar)
            keep_out(2 * NIT - 1, 1)

        @block.vector
        def _(dve):
            def row_max(G, qb, mb, pair):
                if mb == 0 and not (type(G) is int and G < 2):
                    dve.wait_ge(mp_step, 4 * (G - 1))
                dve.wait_ge(ms_ready, MH * G + mb + 1)
                nc.vector.tensor_reduce(mem.NM[:, qb, mb:mb + 1], mem.ps[:, pair, :],
                                        AX.XY, ALU.max, negate=True).then_inc(ms_free, 1)

            def normalise(half, it, qb):
                dve.wait_ge(outT_ready, half + 1)
                if not (type(half) is int and half < 1):
                    dve.wait_ge(norm_done, half)
                o = mem.ps[:, 6 + qb, :].rearrange("p (q h c) -> p q h c", q=4, h=HG)
                nc.vector.tensor_scalar(mem.den[:, :].rearrange("p (q h) -> p q h", q=4), o[:, :, :, DH],
                                        DEN_EPS, None, ALU.add).then_inc(norm_step, 1)
                dve.wait_ge(norm_step, 2 * half + 1)
                nc.vector.reciprocal(mem.den[:, :], mem.den[:, :]).then_inc(norm_step, 1)
                dve.wait_ge(norm_step, 2 * half + 2)
                nc.vector.tensor_tensor(
                    mem.ao[:, bass.ds(it // 2, 1), 4 * qb:4 * qb + 4, bass.ds((it % 2) * 64, 64)].rearrange(
                        "p o q (h d) -> p (o q) h d", h=HG),
                    o[:, :, :, 0:DH],
                    mem.den[:, :].rearrange("p (q h) -> p q h", q=4)[:, :, :, None].broadcast_to([P, 4, HG, DH]),
                    ALU.mult).then_inc(norm_done, 1)

            def body(it, s, last=False):
                for qb in (0, 1):
                    first = type(it) is int and it == 0 and qb == 0
                    for u in range(UH):
                        if not last:
                            row_max(2 * it + 2 + qb, qb, u, pair_of(unit_mod(s, qb, u)))
                        if u == 12 and not first:
                            normalise(2 * it + qb - 1, it if qb == 1 else it - 1, 1 - qb)

            for G in (0, 1):
                for mb in range(MH):
                    row_max(G, G, mb, first_pair(MH * G + mb))
            iterations(body, nc.vector)
            normalise(2 * NIT - 1, NIT - 1, 1)

        @block.tensor
        def _(pe):
            def score_block(qb, s, mb, pair):
                hh, qt = mb // 4, mb % 4
                q0 = qb * N + qt * P
                for kh in range(2):
                    ins = nc.tensor.matmul(mem.ps[:, pair.start + kh, :], QO[0:KROWS, s, hh, q0:q0 + P],
                                           KO[0:KROWS, s, hh, kh * N:(kh + 1) * N], start=True, stop=True)
                ins.then_inc(ms_ready, 1)

            def turn_max(G, qb, bank):
                pe.wait_ge(mp_step, 4 * G + 4)
                nc.tensor.transpose(mem.ps[:, bank, 0:64].bitcast(BF16), mem.MP[:, qb, :],
                                    mem.ident_bf[:, :]).then_inc(mt_ready, 1)

            def turn_out(half, G, qb):
                pe.wait_ge(po_ready, half + 1)
                if G is not None:
                    pe.wait_ge(mt_kept, G + 1)
                for q in range(4):
                    ins = nc.tensor.transpose(mem.ps[:, 6 + qb, q * P:(q + 1) * P],
                                              mem.po[:, qb, q * P:(q + 1) * P], mem.ident)
                ins.then_inc(outT_ready, 1)

            def scores_t(it, s, qb, u, last=False):
                U = 2 * UH * it + UH * qb + u
                if u == 0:
                    pe.wait_ge(row_in[qb], 16 * (it + 1))
                if type(it) is int and U == 0:
                    pe.wait_ge(ms_free, 2 * MH - 1)
                elif not (last and UH * qb + u >= 3):
                    pe.wait_ge(ms_free, U + 2 * MH - 2)
                kc, pair = u // 2, u % 2
                bank = pair_of(unit_mod(s, qb, u)).start
                for j in range(2):
                    hh = 2 * pair + j
                    ins = nc.tensor.matmul(mem.ps[:, bank + j, :], KO[0:KMAX, s, hh, kc * P:(kc + 1) * P],
                                           QO[0:KMAX, s, hh, qb * N:(qb + 1) * N], start=True, stop=True)
                ins.then_inc(st_ready, 1)

            def times_v(it, s, qb, u):
                U = 2 * UH * it + UH * qb + u
                pe.wait_ge(exp_done, U + 1)
                kc, pair = u // 2, u % 2
                for j in range(2):
                    hh = 2 * pair + j
                    ins = nc.tensor.matmul(mem.ps[32 * hh:32 * hh + 32, 6 + qb, :], mem.vst[:, s, kc, hh, :],
                                           mem.e[:, u % 4, j * N:(j + 1) * N], start=(kc == 0), stop=(kc == QT - 1))
                ins.then_inc(pv_done, 1)

            def body(it, s, last=False):
                fixed0 = type(it) is int and it == 0
                for qb in (0, 1):
                    first = fixed0 and qb == 0
                    for u in range(UH):
                        if u < UH - 1:
                            scores_t(it, s, qb, u + 1, last)
                        elif qb == 0:
                            scores_t(it, s, 1, 0, last)
                        elif not last:
                            scores_t(it + 1, (s + 1) % 3, 0, 0)
                        if not last:
                            if qb == 0 and u == 0:
                                pe.wait_ge(qk_in[(s + 1) % 3], slot_value(it, s))
                            pe.wait_ge(exp_done, 2 * UH * it + UH * qb + u + 1)
                            score_block(qb, (s + 1) % 3, u, pair_of(unit_mod(s, qb, u)))
                        if u == 0:
                            if qb == 0:
                                pe.wait_ge(v_staged, it + 1)
                            if fixed0:
                                pe.wait_ge(mt_kept, qb + 1)
                            else:
                                pe.wait_ge(norm_done, 2 * it + qb - 1)
                        if u == 5 and not first and not (last and qb == 1):
                            pe.wait_ge(po_ready, 2 * it + qb)
                            turn_max(2 * it + qb + 1, 1 - qb, 7 - qb)
                        if u == 9 and not first:
                            turn_out(2 * it + qb - 1, None if (last and qb == 1) else 2 * it + qb + 1, 1 - qb)
                        times_v(it, s, qb, u)

            def slot_value(it, s):
                if type(it) is int:
                    return 192 * ((it + 1) // 3 + 1)
                return slot_fill[s]

            slot_fill = {}
            pe.wait_ge(qk_in[0], 192)
            for G in (0, 1):
                for mb in range(MH):
                    n = MH * G + mb
                    if n >= 3:
                        pe.wait_ge(ms_free, n - 2)
                    score_block(G, 0, mb, first_pair(n))
                    if n == MH + MH // 2:
                        turn_max(0, 0, 6)
            turn_max(1, 1, 7)
            scores_t(0, 0, 0, 0)
            body(0, 0)
            with nc.tensor.Fori(0, 2) as r:
                for s in (1, 2, 3):
                    slot_fill[s % 3] = 192 * (r + ((s + 1) // 3) + 1)
                    body(3 * r + s, s % 3)
            body(NIT - 1, (NIT - 1) % 3, last=True)
            turn_out(2 * NIT - 1, None, 1)



def project_and_add(nc, pe, mem, aT, w, start, done):
    for i in range(NT):
        start(i)
        for k in range(KD):
            ins = nc.tensor.matmul(mem.ps[:, i // 2, (i % 2) * D:(i % 2 + 1) * D], aT[:, k, i * P:(i + 1) * P],
                                   w[:, k, :], start=(k == 0), stop=(k == KD - 1))
        ins.then_inc(done, 1)


def add_projection(nc, dve, mem, projected, h_ready, c):
    for i in range(4 * c, 4 * c + 4):
        dve.wait_ge(projected, 2 * (i // 2) + 2)
        nc.vector.tensor_tensor(mem.h[:, i, :], mem.ps[:, i // 2, (i % 2) * D:(i % 2 + 1) * D],
                                mem.h[:, i, :], ALU.add).then_inc(h_ready, 1)
    dve.wait_ge(h_ready, 4 * c + 4)


def stage_router(nc, mem, io, sem, layer):
    t = f"c{layer}_"
    if layer == 0:
        a = Arena(mem.arena, mem.layer0_at)
        aT = a.take(KD * T).rearrange("p (k t) -> p k t", k=KD)
        w_out = mem.wo
        gs = a.take(2 * F0 // P * N).rearrange("p (s f t) -> p s f t", s=2, f=F0 // P)
        hs = a.take(2 * F0 // P * N).rearrange("p (s f t) -> p s f t", s=2, f=F0 // P)
    else:
        a = Arena(mem.arena, 0)
        aT, w_out = mem.xT, mem.w_out
    rows = mem.rows[layer]
    cmp = a.take(2 * NT * NE * NE).rearrange("p (s n) -> p s n", s=2)
    assert a.at <= (mem.w1_at if layer == 0 else mem.ring_at)
    acc, gate, gate_in = mem.acc[layer], mem.gate, sem(t + "gate_in")
    projected, h_ready = sem(t + "projected"), sem(t + "h")
    step, stats_done, means_done = (sem(t + n) for n in ("step", "stats", "means"))
    var_ready, sd_ready, xn_ready, turned, xT_ready = (sem(t + n) for n in ("var", "sd", "xn", "turned", "xT"))
    logits, shifted, exped, mask_ready, counted, slots_ready, sent = (
        sem(t + n) for n in ("logits", "shifted", "exped", "mask", "counted", "slots", "sent"))
    if layer == 0:
        turned0, kept0 = sem(t + "turned0"), sem(t + "kept0")
        s_up, s_gate, s_act, s_down, s_added, s_bias = (
            sem(t + n) for n in ("s_up", "s_gate", "s_act", "s_down", "s_added", "s_bias"))
    else:
        places_ready = sem(t + "places")
    NC = T // N
    S_UP, S_Y = 4, (3, 0)

    with nc.Block() as block:
        @block.sync
        def _(sp):
            sp.dma_start(gate[:, :, :], io[f"gate{layer}"]).then_inc(gate_in, 16)
            if layer == 0:
                sp.dma_start(mem.gate_b[:, :], io["gate_b"].partition_broadcast(P)).then_inc(gate_in, 16)
                sp.dma_start(mem.w2, io["w2"].rearrange("e p n -> p e n")).then_inc(mem.experts_in, 16)
                sp.dma_start(mem.b1_shared[:, :], io["b1_shared"]).then_inc(mem.experts_in, 16)
                sp.dma_start(mem.b2, io["b2"].partition_broadcast(P)).then_inc(mem.experts_in, 16)
                sp.dma_start(mem.b1, io["b1"].partition_broadcast(P)).then_inc(mem.experts_in, 16)
            for c in range(NC):
                if layer == 0:
                    sp.wait_ge(s_added, 2 * c + 2)
                else:
                    sp.wait_ge(h_ready, 4 * c + 4)
                sp.dma_start(acc[c * N:(c + 1) * N, :].rearrange("(i p) c -> p i c", p=P),
                             mem.h[:, 4 * c:4 * c + 4, :]).then_inc(mem.acc_in[layer], 16)
            sp.dma_start(acc[T:T + TRASH, :], mem.h[:, 0, :]).then_inc(mem.acc_in[layer], 16)
            if layer == 1:
                sp.wait_ge(places_ready, 1)
                for o in range(2):
                    load_experts(nc, sp, mem, io, o)
            sp.wait_ge(gate_in, 32 if layer == 0 else 16)

        @block.gpsimd
        def _(pool):
            pool.wait_ge(mem.pads_in, 32)
            if layer == 0:
                pool.wait_ge(xn_ready, NT)
                pool.wait_ge(mem.experts_in, 16 * 5)
                nc.gpsimd.tensor_tensor(mem.h[:, :, :], mem.h[:, :, :],
                                        mem.b2[:, NE:NE + 1, :].broadcast_to([P, NT, D]), ALU.add).then_inc(s_bias, 1)
            pool.wait_ge(slots_ready, 1)
            for k in range(TOP_K):
                for i in range(NT):
                    nc.gpsimd.indirect_dma_start(
                        out=rows, out_offset=bass.IndirectOffsetOnAxis(ap=mem.slots[:, k, i:i + 1].bitcast(U32), axis=0),
                        in_=mem.xw[:, i, :], in_offset=None,
                        bounds_check=NRT * P - 1, oob_is_err=False).then_inc(sent, 16)
            pool.wait_ge(sent, 16 * TOP_K * NT)

        @block.scalar
        def _(act):
            if layer == 0:
                for c in range(NT // 4):
                    keep_turned(nc, act, mem, c, turned0, kept0, to=aT)
            root_and_keep(nc, act, mem, var_ready, sd_ready, turned, xT_ready)
            act.wait_ge(shifted, 1)
            nc.scalar.activation(mem.lg[:, :], mem.lg[:, :], ACT.Exp).then_inc(exped, 1)
            if layer == 0:
                act.wait_ge(mem.experts_in, 16 * 5)
                for c in range(NC):
                    act.wait_ge(s_up, c + 1)
                    if c >= 2:
                        act.wait_ge(s_act, 2 * c - 2)
                    for f in range(F0 // P):
                        nc.scalar.activation(gs[:, c % 2, f, :], mem.ps[:, S_UP + f, :], ACT.Silu,
                                             bias=mem.b1_shared[:, f:f + 1]).then_inc(s_gate, 1)

        @block.vector
        def _(dve):
            link = step_counter(dve, step)
            const = mem.const
            norm_rows(nc, dve, link, mem, lambda c: add_projection(nc, dve, mem, projected, h_ready, c), lambda c: None,
                      stats_done, means_done, var_ready, sd_ready, xn_ready)
            tok = mem.xw[:, :, :].rearrange("p i c -> p (i c)").bitcast(I32).rearrange("p (i c) -> p i c", i=NT)
            nc.vector.tensor_copy(tok[:, :, C_ID], const[:, K_TOK:K_TOK + NT])

            lg = mem.lg[:, :].rearrange("p (i e) -> p i e", i=NT)
            dve.wait_ge(gate_in, 32 if layer == 0 else 16)
            dve.wait_ge(logits, 1)
            l_ps = mem.ps[:, 0, 0:NT * NE].rearrange("p (i e) -> p i e", i=NT)
            if layer == 0:
                link(nc.vector.tensor_tensor(lg, l_ps, mem.gate_b[:, None, :].broadcast_to([P, NT, NE]), ALU.add))
            else:
                link(nc.vector.tensor_copy(lg, l_ps))
            link(nc.vector.tensor_reduce(mem.s16[:, :], lg, AX.X, ALU.max))
            link(nc.vector.tensor_tensor(lg, lg, mem.s16[:, :, None].broadcast_to([P, NT, NE]), ALU.subtract))
            nc.vector.memset(mem.r2[:, :], 0.0).then_inc(shifted, 1)
            dve.wait_ge(exped, 1)
            link(nc.vector.tensor_reduce(mem.s16[:, :], lg, AX.X, ALU.add))
            link(nc.vector.reciprocal(mem.s16[:, :], mem.s16[:, :]))
            link(nc.vector.tensor_tensor(lg, lg, mem.s16[:, :, None].broadcast_to([P, NT, NE]), ALU.mult))

            over_e = lg[:, :, None, :].broadcast_to([P, NT, NE, NE])
            own = lg[:, :, :, None].broadcast_to([P, NT, NE, NE])
            gt = cmp[:, 0, :].rearrange("p (i e f) -> p i e f", i=NT, e=NE)
            eq = cmp[:, 1, :].rearrange("p (i e f) -> p i e f", i=NT, e=NE)
            lower = const[:, K_LT:K_LT + NE * NE].rearrange("p (e f) -> p e f", e=NE)
            link(nc.vector.tensor_tensor(gt, over_e, own, ALU.is_gt))
            link(nc.vector.tensor_tensor(eq, over_e, own, ALU.is_equal))
            link(nc.vector.tensor_tensor(eq, eq, lower[:, None, :, :].broadcast_to([P, NT, NE, NE]), ALU.mult))
            link(nc.vector.tensor_tensor(gt, gt, eq, ALU.add))
            rank = mem.rank[:, :].rearrange("p (i e) -> p i e", i=NT)
            link(nc.vector.tensor_reduce(rank, gt, AX.X, ALU.add))
            mask = mem.mask[:, 2, :].rearrange("p (i e) -> p i e", i=NT)
            link(nc.vector.tensor_scalar(mem.mask_bf[:, :], mem.rank[:, :], float(TOP_K), None, ALU.is_lt))
            nc.vector.tensor_scalar(mem.mask[:, 2, :], mem.rank[:, :], float(TOP_K), None, ALU.is_lt).then_inc(mask_ready, 1)
            for k in range(TOP_K):
                link(nc.vector.tensor_scalar(mem.mask[:, k, :], mem.rank[:, :], float(k), None, ALU.is_equal))
            cw = mem.xw[:, :, C_W:C_W + NE]
            dve.wait_ge(mask_ready, 1)
            link(nc.vector.tensor_tensor(cw, lg, mask, ALU.mult))
            if layer == 1:
                link(nc.vector.tensor_reduce(mem.s16[:, :], cw, AX.X, ALU.add))
                link(nc.vector.reciprocal(mem.s16[:, :], mem.s16[:, :]))
                link(nc.vector.tensor_tensor(cw, cw, mem.s16[:, :, None].broadcast_to([P, NT, NE]), ALU.mult))

            dve.wait_ge(counted, 1)
            j128 = const[:, K_J128:K_J128 + NT]
            c128 = cmp[:, 0, 0:NE * NT].rearrange("p (e j) -> p e j", e=NE)
            n_of = mem.ps[:, 2, 0:NE]
            small = mem.small
            tiles, base, has, order = small[:, 0, :], small[:, 1, :], small[:, 2, :], small[:, 3, :]
            link(nc.vector.tensor_copy(small[:, 4, :], n_of))
            link(nc.vector.tensor_tensor(c128, small[:, 4, :, None].broadcast_to([P, NE, NT]),
                                         j128[:, None, :].broadcast_to([P, NE, NT]), ALU.is_gt))
            link(nc.vector.tensor_reduce(tiles, c128, AX.X, ALU.add))
            ee = cmp[:, 1, 0:NE * NE].rearrange("p (e f) -> p e f", e=NE)
            link(nc.vector.tensor_tensor(ee, tiles[:, None, :].broadcast_to([P, NE, NE]), lower, ALU.mult))
            link(nc.vector.tensor_reduce(base, ee, AX.X, ALU.add))

            slotm = mem.rank[:, :].rearrange("p (i e) -> p i e", i=NT)
            link(nc.vector.scalar_tensor_tensor(slotm, base[:, None, :].broadcast_to([P, NT, NE]), float(P),
                                                mem.ps[:, 1, 0:NT * NE].rearrange("p (i e) -> p i e", i=NT),
                                                ALU.mult, ALU.add))
            for k in range(TOP_K):
                sel = mem.mask[:, k, :]
                link(nc.vector.tensor_tensor(sel, sel, mem.rank[:, :], ALU.mult))
                link(nc.vector.tensor_reduce(mem.s16[:, :], sel.rearrange("p (i e) -> p i e", i=NT), AX.X, ALU.add))
                link(nc.vector.tensor_copy(mem.slots[:, k, :], mem.s16[:, :]))
            nc.vector.memset(mem.r2[:, :], 0.0).then_inc(slots_ready, 1)

            jj = const[:, K_J:K_J + NRT]
            ge = cmp[:, 0, 0:NRT * NE].rearrange("p (j e) -> p j e", j=NRT)
            tf, words = mem.tf[:, :, 1:1 + NRT], mem.words

            def pack(k):
                of = lambda i: mem.tf[:, k, i:i + 4 * N_WORDS - 3:4]
                link(nc.vector.scalar_tensor_tensor(words[:, k, :], of(5), 16.0, of(4), ALU.mult, ALU.add))
                for i in (3, 2, 1, 0):
                    link(nc.vector.scalar_tensor_tensor(words[:, k, :], words[:, k, :], 16.0, of(i), ALU.mult, ALU.add))
                link(nc.vector.tensor_copy(mem.tab[:, k, :], words[:, k, :]))

            link(nc.vector.memset(mem.tf[:, :, :], 0.0))
            link(nc.vector.tensor_tensor(ge, jj[:, :, None].broadcast_to([P, NRT, NE]),
                                         base[:, None, :].broadcast_to([P, NRT, NE]), ALU.is_ge))
            link(nc.vector.tensor_reduce(tf[:, 0, :], ge, AX.X, ALU.add))
            link(nc.vector.tensor_scalar(tf[:, 0, :], tf[:, 0, :], -1.0, None, ALU.add))
            pack(0)
            if layer == 1:
                link(nc.vector.tensor_scalar(has, tiles, 0.0, None, ALU.is_gt))
                link(nc.vector.tensor_tensor(ge, ge, has[:, None, :].broadcast_to([P, NRT, NE]), ALU.mult))
                link(nc.vector.tensor_reduce(tf[:, 1, :], ge, AX.X, ALU.add))
                pack(1)
                link(nc.vector.tensor_tensor(ee, has[:, None, :].broadcast_to([P, NE, NE]), lower, ALU.mult))
                link(nc.vector.tensor_reduce(order, ee, AX.X, ALU.add))
                place = const[:, K_J:K_J + NE]
                at = cmp[:, 0, 0:NE * NE].rearrange("p (o e) -> p o e", o=NE)
                link(nc.vector.tensor_tensor(at, place[:, :, None].broadcast_to([P, NE, NE]),
                                             order[:, None, :].broadcast_to([P, NE, NE]), ALU.is_equal))
                link(nc.vector.tensor_tensor(at, at, has[:, None, :].broadcast_to([P, NE, NE]), ALU.mult))
                link(nc.vector.tensor_tensor(ee, at, place[:, None, :].broadcast_to([P, NE, NE]), ALU.mult))
                link(nc.vector.tensor_reduce(small[:, 4, :], ee, AX.X, ALU.add))
                link(nc.vector.tensor_copy(mem.places[:, 0, :], small[:, 4, :]))
                n_has, last_at = mem.n_has[:, 0:1], mem.n_has[:, 1:2]
                link(nc.vector.tensor_tensor(small[:, 5, :], has, base, ALU.mult))
                link(nc.vector.tensor_reduce(last_at, small[:, 5, :], AX.X, ALU.max))
                link(nc.vector.tensor_scalar(last_at, last_at, 1.0, None, ALU.add))
                link(nc.vector.tensor_reduce(n_has, has, AX.X, ALU.add))
                link(nc.vector.tensor_scalar(small[:, 5, :], base, -float(NRT), None, ALU.add))
                link(nc.vector.tensor_tensor(ee, at, small[:, 5, None, :].broadcast_to([P, NE, NE]), ALU.mult))
                link(nc.vector.tensor_reduce(small[:, 4, :], ee, AX.X, ALU.add))
                link(nc.vector.tensor_scalar(mem.places[:, 1, :], small[:, 4, :], float(NRT + 1), last_at,
                                             ALU.add, ALU.min))
                link(nc.vector.tensor_scalar(mem.places[:, 3, :], place, n_has, None, ALU.min))
                link(nc.vector.tensor_scalar(mem.places[:, 2, :], mem.places[:, 3, :], 1, None, ALU.bitwise_and))
                nc.vector.memset(mem.r2[:, :], 0.0).then_inc(places_ready, 1)
            else:
                for c in range(NC + 1):
                    for f in range(F0 // P):
                        if c < NC:
                            if f == 0 and c >= 2:
                                dve.wait_ge(s_down, 2 * c - 2)
                            dve.wait_ge(s_gate, 2 * c + f + 1)
                            nc.vector.scalar_tensor_tensor(hs[:, c % 2, f, :], mem.ps[:, S_UP + 2 + f, :],
                                                           mem.b1_shared[:, 2 + f:3 + f], gs[:, c % 2, f, :],
                                                           ALU.add, ALU.mult).then_inc(s_act, 1)
                    for n in range(2 * c - 2, 2 * c) if c else ():
                        if n == 0:
                            dve.wait_ge(s_bias, 1)
                        dve.wait_ge(s_down, n + 1)
                        nc.vector.tensor_tensor(
                            mem.h[:, 2 * n:2 * n + 2, :], mem.ps[:, S_Y[n % 2], :].rearrange("p (i c) -> p i c", i=2),
                            mem.h[:, 2 * n:2 * n + 2, :], ALU.add).then_inc(s_added, 1)

        @block.tensor
        def _(pe):
            if layer == 0:
                def attended(i, k):
                    return mem.ao[:, (i // QT) * KD + k, i % QT, :]

                transpose_rows(nc, pe, mem, attended, lambda i: None, turned0)
                pe.wait_ge(kept0, 8)
            project_and_add(nc, pe, mem, aT, w_out, lambda i: None, projected)
            transpose_rows(nc, pe, mem, lambda i, k: mem.xw[:, i, k * P:(k + 1) * P],
                           lambda i: pe.wait_ge(xn_ready, i + 1), turned)
            pe.wait_ge(xT_ready, 8)
            pe.wait_ge(gate_in, 32 if layer == 0 else 16)
            for i in range(NT):
                for k in range(KD):
                    ins = nc.tensor.matmul(mem.ps[:, 0, i * NE:(i + 1) * NE], mem.xT[:, k, i * P:(i + 1) * P],
                                           gate[:, k, :], start=(k == 0), stop=(k == KD - 1))
            ins.then_inc(logits, 1)
            def shared_up(c):
                if c >= 1:
                    pe.wait_ge(s_act, 2 * c)
                for f in range(2 * F0 // P):
                    for k in range(KD):
                        n0 = k * 2 * F0 + f * P
                        ins = nc.tensor.matmul(mem.ps[:, S_UP + f, :], mem.w1[:, NE, n0:n0 + P],
                                               mem.xT[:, k, c * N:(c + 1) * N], start=(k == 0), stop=(k == KD - 1))
                ins.then_inc(s_up, 1)

            if layer == 0:
                pe.wait_ge(mem.experts_in, 16 * 5)
                shared_up(0)
            pe.wait_ge(mask_ready, 1)
            nc.tensor.matmul(mem.ps[:, 1, 0:NT * NE], mem.zero_bf, mem.mask_bf, start=True, stop=False)
            for d in range(1, NT):
                nc.tensor.matmul(mem.ps[:, 1, d * NE:NT * NE], mem.ones_bf[:, :], mem.mask_bf[:, 0:(NT - d) * NE],
                                 start=False, stop=False, skip_group_check=True)
            nc.tensor.matmul(mem.ps[:, 1, 0:NT * NE], mem.tri_bf, mem.mask_bf, start=False, stop=True)
            for i in range(NT):
                ins = nc.tensor.matmul(mem.ps[:, 2, 0:NE], mem.ones_bf[:, :], mem.mask_bf[:, i * NE:(i + 1) * NE],
                                       start=(i == 0), stop=(i == NT - 1))
            ins.then_inc(counted, 1)
            if layer == 0:
                for n in range(2 * NC):
                    c = n // 2
                    if n % 2 == 0 and c + 1 < NC:
                        shared_up(c + 1)
                    pe.wait_ge(s_act, 2 * c + 2)
                    if n >= 2:
                        pe.wait_ge(s_added, n - 1)
                    for i in range(2):
                        t0 = (n % 2) * 2 * P + i * P
                        for f in range(F0 // P):
                            ins = nc.tensor.matmul(mem.ps[:, S_Y[n % 2], i * D:(i + 1) * D], hs[:, c % 2, f, t0:t0 + P],
                                                   mem.w2[:, NE, f * D:(f + 1) * D],
                                                   start=(f == 0), stop=(f == F0 // P - 1))
                    ins.then_inc(s_down, 1)



def load_experts(nc, engine, mem, io, o):
    e = nc.sync.value_load(mem.places[0:1, 0, o:o + 1], min_val=0, max_val=NE - 1)
    slot = nc.sync.value_load(mem.places[0:1, 2, o:o + 1], min_val=0, max_val=1)
    if o >= 2:
        first = nc.sync.value_load(mem.places[0:1, 1, o - 1:o], min_val=1, max_val=NRT + 1)
        engine.wait_ge(mem.tiles_done, first)
    engine.dma_start(mem.ring_gu[:, bass.ds(slot, 1), :].rearrange("p o n -> p (o n)"),
                     io["gu"][bass.ds(e, 1), :, :].rearrange("o p n -> (o p) n")).then_inc(mem.w_loaded, 16)
    engine.dma_start(mem.ring_dn[:, bass.ds(slot, 1), :].rearrange("p o n -> p (o n)"),
                     io["dn"][bass.ds(e, 1), :, :].rearrange("o p n -> (o p) n")).then_inc(mem.w_loaded, 16)
    engine.wait_ge(mem.w_loaded, 32 * (o + 1))


def stage_experts(nc, mem, io, sem, layer):
    t = f"d{layer}_"
    if layer == 0:
        F = F0
        a = Arena(mem.arena, mem.layer0_at)
    else:
        F = F1
        a = Arena(mem.arena, 0)
    n_tiles, rows = NRT, mem.rows[layer]
    FT = F // P
    copies = max(1, FT // 4)
    acc = mem.acc[layer]
    xg = a.take(4 * ROW).rearrange("p (s c) -> p s c", s=4)
    meta = a.take(4 * (ROW - D)).rearrange("p (s c) -> p s c", s=4)
    xgT = a.take(2 * D).rearrange("p (s k t) -> p s k t", s=2, k=KD)
    pre = a.take(2 * 2 * F0).rearrange("p (s f) -> p s f", s=2)
    g = a.take(2 * F).rearrange("p (s f) -> p s f", s=2)
    hact = a.take(2 * F).rearrange("p (s f) -> p s f", s=2)
    hT = a.take(2 * F).rearrange("p (s c t) -> p s c t", s=2, c=FT)
    y0 = a.take(2 * D).rearrange("p (s c) -> p s c", s=2)
    y = a.take(4 * D).rearrange("p (s c) -> p s c", s=4)
    assert a.at <= (mem.w1_at if layer == 0 else mem.ring_at)
    XT, GU = 0, (1, 2) if layer == 0 else (1, 3)
    HT, Y = (3, 4) if layer == 0 else (5, 7)

    loaded = [sem(f"{t}loaded{s}") for s in range(4)]
    xT_ps, xT_kept, gu_ps, g_ready, hact_ready, hT_ps, hT_kept, y_ps, y_ready, added, meta_kept, may_add = (
        sem(t + n) for n in ("xT_ps", "xT_kept", "gu", "g", "hact", "hT_ps", "hT_kept", "y_ps", "y", "added",
                             "meta", "may_add"))
    if layer == 0:
        pre_ready, y_step = sem(t + "pre"), sem(t + "y_step")
        mem.h_back = [sem(f"{t}h_back{c}") for c in range(T // N)]
    mem.tiles_done = y_ps
    Y1 = 1

    LAG = 2 if layer == 0 else 1

    def steps(body, engine, row=None):
        def number_of(word, at):
            least, most = (0, NE - 1) if row == 0 else (1, NE)
            return lambda i: nc.s_assert_within(engine.snap((word // 16 ** (at + i + 1)) % 16), least, most,
                                                skip_runtime_bounds_check_because="the router packs these numbers")

        def load_word(g):
            if row is None:
                return 0
            return engine.value_load(mem.tab[0:1, row, bass.ds(g, 1)], min_val=0, max_val=2 ** 24 - 1)

        word = load_word(0)
        for j in range(HEAD):
            body(j, j % 4, number_of(word, j))
        with engine.Fori(0, (n_tiles - 2 - HEAD) // 4) as r:
            word = load_word(r + 1)
            for u in range(HEAD, HEAD + 4):
                body(4 * r + u, u % 4, number_of(word, u - 4), r, u)
        word = load_word(N_WORDS - 1)
        for j in range(n_tiles - 2, n_tiles + LAG):
            body(j, j % 4, number_of(word, j - 4 * (N_WORDS - 1)))

    def fixed(j):
        return type(j) is int

    with nc.Block() as block:
        def load(engine, j, s):
            row0 = j * P + 4 * P if fixed(j) else engine.snap(j * P + 4 * P)
            engine.wait_ge(meta_kept, 2 * j + 2)
            engine.dma_start(xg[:, s, :], rows[bass.ds(row0, P), :]).then_inc(loaded[s], 16)

        def first_loads(engine):
            for j in range(4):
                engine.dma_start(xg[:, j, :], rows[j * P:(j + 1) * P, :]).then_inc(loaded[j], 16)

        def run_loads(engine):
            first_loads(engine)
            for j in range(HEAD):
                load(engine, j, j % 4)
            n_loop = (n_tiles - 4 - HEAD) // 4
            with engine.Fori(0, n_loop) as r:
                for u in range(HEAD, HEAD + 4):
                    load(engine, 4 * r + u, u % 4)
            for j in range(4 * n_loop + HEAD, n_tiles - 4):
                load(engine, j, j % 4)

        @block.sync
        def _(sp):
            sp.sem_inc(y_ps, Y1)
            if layer == 1:
                for o in range(2, NE):
                    load_experts(nc, sp, mem, io, o)
            else:
                run_loads(sp)
                sp.wait_ge(added, 16 * n_tiles)
                for c in range(T // N):
                    sp.dma_start(mem.h[:, 4 * c:4 * c + 4, :],
                                 acc[c * N:(c + 1) * N, :].rearrange("(i p) c -> p i c", p=P)).then_inc(mem.h_back[c], 16)

        @block.gpsimd
        def _(pool):
            def body(j, s, loads):
                if loads:
                    load(nc.gpsimd, j, s)
                if not fixed(j) or j >= LAG:
                    pool.wait_ge(y_ready, j - LAG + 1)
                    if not fixed(j) or j > LAG:
                        pool.wait_ge(added, 16 * j - 16 * LAG)
                    pool.sem_inc(may_add, 1)
                    nc.gpsimd.indirect_dma_start(
                        out=acc, out_offset=bass.IndirectOffsetOnAxis(
                            ap=meta[:, (s - LAG) % 4, NE:NE + 1].bitcast(U32), axis=0),
                        in_=y[:, (s - LAG) % 4, :], in_offset=None, compute_op=ALU.add).then_inc(added, 16)

            if layer == 1:
                first_loads(nc.gpsimd)
            pool.wait_ge(mem.acc_in[layer], 16 * (T // N + 1))
            for j in range(HEAD):
                body(j, j % 4, layer == 1)
            n_loop = (n_tiles - 4 - HEAD) // 4
            with nc.gpsimd.Fori(0, n_loop) as r:
                for u in range(HEAD, HEAD + 4):
                    body(4 * r + u, u % 4, layer == 1)
            for j in range(4 * n_loop + HEAD, n_tiles + LAG):
                body(j, j % 4, layer == 1 and j + 4 < n_tiles)
            pool.wait_ge(added, 16 * n_tiles)

        @block.scalar
        def _(act):
            def body(j, s, of, r=None, u=None):
                p = s % 2
                if not fixed(j) or j < n_tiles - 1:
                    keep_rows(j + 1, (s + 1) % 4)
                if not fixed(j) or 1 <= j <= n_tiles:
                    for q in range(copies):
                        act.wait_ge(hT_ps, copies * (j - 1) + q + 1)
                        if q == 0 and (not fixed(j) or j >= 3):
                            act.wait_ge(y_ps, j - 2 + Y1)
                        w = min(4, FT)
                        nc.scalar.activation(
                            hT[:, 1 - p, 4 * q:4 * q + w, :].rearrange("p c t -> p (c t)"),
                            mem.ps[:, HT + q, 0:w * P], ACT.Copy).then_inc(hT_kept, 1)
                if not fixed(j) or j < n_tiles:
                    if not fixed(j) or j >= 2:
                        act.wait_ge(hact_ready, j - 1)
                    if layer == 0:
                        act.wait_ge(pre_ready, j + 1)
                        nc.scalar.activation(g[:, p, :], pre[:, p, 0:F], ACT.Silu).then_inc(g_ready, 1)
                    else:
                        act.wait_ge(gu_ps, j + 1)
                        for q in range(2):
                            ins = nc.scalar.activation(g[:, p, q * N:(q + 1) * N], mem.ps[:, GU[0] + q, :], ACT.Gelu)
                            ins.then_inc(g_ready, 1)

            def keep_rows(j, s):
                act.wait_ge(xT_ps, j + 1)
                if not fixed(j) or j >= 2:
                    act.wait_ge(gu_ps, j - 1)
                nc.scalar.activation(xgT[:, s % 2, :, :].rearrange("p k t -> p (k t)"),
                                     mem.ps[:, XT, 0:D], ACT.Copy).then_inc(xT_kept, 1)

            keep_rows(0, 0)
            steps(body, nc.scalar)

        @block.vector
        def _(dve):
            if layer == 0:
                dve.wait_ge(mem.experts_in, 16 * 5)

            def keep_meta(j, s):
                dve.wait_ge(xT_ps, j + 1)
                if not fixed(j) or j >= 4:
                    dve.wait_ge(added, 16 * j - 48)
                nc.vector.tensor_copy(meta[:, s, 0:NE], xg[:, s, C_W:C_ID]).then_inc(meta_kept, 1)
                nc.vector.tensor_copy(meta[:, s, NE:NE + 1].bitcast(I32),
                                      xg[:, s, C_ID:C_ID + 1].bitcast(I32)).then_inc(meta_kept, 1)

            def body(j, s, of, r=None, u=None):
                p = s % 2
                if not fixed(j) or j < n_tiles:
                    dve.wait_ge(gu_ps, j + 1)
                    if not fixed(j) or j >= 2:
                        dve.wait_ge(hT_ps, copies * (j - 1))
                    if layer == 0:
                        nc.vector.tensor_tensor(
                            pre[:, p, :], mem.ps[:, GU[p], :],
                            mem.b1[:, bass.ds(of(0), 1), :].rearrange("p o f -> p (o f)"), ALU.add).then_inc(pre_ready, 1)
                        dve.wait_ge(g_ready, j + 1)
                        nc.vector.tensor_tensor(hact[:, p, :], g[:, p, :], pre[:, p, F:2 * F],
                                                ALU.mult).then_inc(hact_ready, 1)
                    else:
                        dve.wait_ge(g_ready, 2 * j + 2)
                        nc.vector.tensor_tensor(hact[:, p, :], g[:, p, :],
                                                mem.ps[:, GU[1]:GU[1] + 2, :].rearrange("p a b -> p (a b)"),
                                                ALU.mult).then_inc(hact_ready, 1)
                if not fixed(j) or j >= LAG:
                    v, e = (s - LAG) % 4, of(-LAG)
                    dve.wait_ge(y_ps, j - LAG + 1 + Y1)
                    dve.wait_ge(meta_kept, 2 * j - 2 * LAG + 2)
                    if not fixed(j) or j >= LAG + 4:
                        dve.wait_ge(added, 16 * j - 16 * (LAG + 3))
                    src = mem.ps[:, Y, 0:D]
                    if layer == 0:
                        nc.vector.tensor_tensor(y0[:, v % 2, :], src,
                                                mem.b2[:, bass.ds(e, 1), :].rearrange("p o f -> p (o f)"),
                                                ALU.add).then_inc(y_step, 1)
                        dve.wait_ge(y_step, j - LAG + 1)
                        src = y0[:, v % 2, :]
                    nc.vector.tensor_scalar(y[:, v, :], src, meta[:, v, bass.ds(e, 1)], None,
                                            ALU.mult).then_inc(y_ready, 1)
                if not fixed(j) or j < n_tiles:
                    keep_meta(j, s)

            steps(body, nc.vector, 0)

        @block.tensor
        def _(pe):
            if layer == 0:
                pe.wait_ge(mem.experts_in, 16 * 5)

            fill = {}

            def turn_rows(j, s):
                pe.wait_ge(loaded[s], 16 * (j // 4 + 1) if fixed(j) else fill[s])
                if not fixed(j) or j >= 1:
                    pe.wait_ge(xT_kept, j)
                for k in range(KD):
                    ins = nc.tensor.transpose(mem.ps[:, XT, k * P:(k + 1) * P], xg[:, s, k * P:(k + 1) * P], mem.ident)
                ins.then_inc(xT_ps, 1)

            def first_product(j, p, of):
                pe.wait_ge(xT_kept, j + 1)
                if layer == 0:
                    if not fixed(j) or j >= 2:
                        pe.wait_ge(pre_ready, j - 1)
                    w = mem.w1[:, bass.ds(of(0), 1), :].rearrange("p o (k f) -> p (o k) f", k=KD)
                    for k in range(KD):
                        ins = nc.tensor.matmul(mem.ps[:, GU[p], :], xgT[:, p, k, :], w[:, k, :],
                                               start=(k == 0), stop=(k == KD - 1))
                else:
                    pe.wait_ge(mem.w_loaded, 32 * of(0))
                    if not fixed(j) or j >= 1:
                        pe.wait_ge(hact_ready, j)
                    buffer = nc.tensor.snap((of(0) + 1) % 2)
                    w = mem.ring_gu[:, bass.ds(buffer, 1), :].rearrange("p o (k f) -> p (o k) f", k=KD)
                    for q in range(4):
                        for k in range(KD):
                            ins = nc.tensor.matmul(mem.ps[:, GU[0] + q, :], xgT[:, p, k, :],
                                                   w[:, k, q * N:(q + 1) * N], start=(k == 0), stop=(k == KD - 1))
                ins.then_inc(gu_ps, 1)

            def turn_activations(j, p):
                pe.wait_ge(hact_ready, j + 1)
                if not fixed(j) or j >= 1:
                    pe.wait_ge(hT_kept, copies * j)
                for c in range(FT):
                    ins = nc.tensor.transpose(mem.ps[:, HT + c // 4, (c % 4) * P:(c % 4 + 1) * P],
                                              hact[:, p, c * P:(c + 1) * P], mem.ident)
                    if c % 4 == 3 or c == FT - 1:
                        ins.then_inc(hT_ps, 1)

            def second_product(j, p, e):
                pe.wait_ge(hT_kept, copies * (j + 1))
                if not fixed(j) or j >= 1:
                    pe.wait_ge(y_step if layer == 0 else y_ready, j)
                if layer == 0:
                    w2 = mem.w2[:, bass.ds(e, 1), :]
                else:
                    w2 = mem.ring_dn[:, bass.ds(nc.tensor.snap((e + 1) % 2), 1), :]
                w2 = w2.rearrange("p o (c n) -> p (o c) n", c=FT)
                for c in range(FT):
                    ins = nc.tensor.matmul(mem.ps[:, Y, 0:D], hT[:, p, c, :], w2[:, c, :],
                                           start=(c == 0), stop=(c == FT - 1))
                ins.then_inc(y_ps, 1)

            def body(j, s, of, r=None, u=None):
                if r is not None:
                    fill[(s + 1) % 4] = 16 * (r + (u + 1) // 4 + 1)
                if not fixed(j) or j < n_tiles - 1:
                    turn_rows(j + 1, (s + 1) % 4)
                turn = not fixed(j) or 1 <= j <= n_tiles
                if layer == 1 and turn:
                    turn_activations(j - 1, (s - 1) % 2)
                if not fixed(j) or j < n_tiles:
                    first_product(j, s % 2, of)
                if layer == 0 and turn:
                    turn_activations(j - 1, (s - 1) % 2)
                if not fixed(j) or j >= LAG:
                    second_product(j - LAG, (s - LAG) % 2, of(-LAG))

            turn_rows(0, 0)
            steps(body, nc.tensor, layer)



def stage_chebyshev(nc, mem, io, sem):
    W = T // 2
    G32 = P // 32
    a = Arena(mem.arena, 0)
    feat = a.take(2 * M * W).rearrange("p (s m t) -> p s m t", s=2, m=M)
    kv = a.take(2 * B * M * P).rearrange("p (o b m c) -> p o b m c", o=2, b=B, m=M)
    turned_kv = a.take(M * 32).rearrange("p (m c) -> p m c", m=M)
    w_in = a.take(KD * 3 * D).rearrange("p (k n) -> p k n", k=KD)
    mem.w_out = a.take(KD * D).rearrange("p (k n) -> p k n", k=KD)
    V1 = mem.xw
    SUMS, RING = 0, (4, 5, 6, 7)

    w_ready, step, stats_done, means_done = (sem("e_" + n) for n in ("w", "step", "stats", "means"))
    var_ready, sd_ready, xn_ready, turned, xT_ready = (sem("e_" + n) for n in ("var", "sd", "xn", "turned", "xT"))
    kv_ps, kv_taken, q_ps, scaled, x_ready = (sem("e_" + n) for n in ("kv_ps", "kv_taken", "q_ps", "scaled", "x"))
    ones_set, squared, even_ready, product, odd_ready, used, kv_ready, o_kept = (
        sem("e_" + n) for n in ("ones", "squared", "even", "product", "odd", "used", "kv", "o_kept"))

    def order(c, m):
        return feat[:, c % 2, m, :]

    with nc.Block() as block:
        @block.sync
        def _(sp):
            sp.dma_start(w_in, io["w_in"]).then_inc(w_ready, 16)
            sp.dma_start(mem.w_out, io["w_out"]).then_inc(w_ready, 16)
            sp.dma_start(mem.beta[:, :, :], io["beta"]).then_inc(w_ready, 16)
            sp.wait_ge(w_ready, 48)

        @block.gpsimd
        def _(pool):
            nc.gpsimd.memset(feat[:, :, 0, :], 1.0).then_inc(ones_set, 1)

        @block.scalar
        def _(act):
            root_and_keep(nc, act, mem, var_ready, sd_ready, turned, xT_ready)

            def keep_v(c):
                for i in range(4 * c, 4 * c + 4):
                    act.wait_ge(kv_ps, i + 1)
                    nc.scalar.activation(V1[:, i, 0:D], mem.ps[:, RING[i % 4], D:2 * D], ACT.Copy).then_inc(kv_taken, 1)

            def even(c, m):
                n = 5 * c + m // 2
                if m == 2:
                    act.wait_ge(x_ready, c + 1)
                elif m in (4, 8):
                    act.wait_ge(even_ready, 5 * c + m // 4)
                else:
                    act.wait_ge(odd_ready, 4 * c + m // 4)
                nc.scalar.activation(order(c, m), order(c, m // 2), ACT.Square).then_inc(squared, 1)
                act.wait_ge(squared, n)
                nc.scalar.activation(order(c, m), order(c, m), ACT.Identity, scale=2.0,
                                     bias=mem.const[:, K_MINUS:K_MINUS + 1]).then_inc(even_ready, 1)

            def keep_out(c):
                o, b = c % 2, (c - 4) // 2
                act.wait_ge(used, c + 1)
                for h in range(2):
                    nc.scalar.activation(mem.xT[:, o, b * S + h * N:b * S + (h + 1) * N],
                                         mem.ps[:, 2 * o + h, :], ACT.Copy).then_inc(o_kept, 1)

            keep_v(0)
            keep_v(1)
            for c in range(8):
                if c == 1:
                    keep_v(2)
                even(c, 2)
                even(c, 4)
                if c == 2:
                    keep_v(3)
                if c >= 6:
                    keep_out(c - 2)
                for m in (6, 8, 10):
                    even(c, m)
            keep_out(6)
            keep_out(7)

        @block.vector
        def _(dve):
            link = step_counter(dve, step)
            norm_rows(nc, dve, link, mem, lambda c: dve.wait_ge(mem.h_back[c], 16), lambda c: None,
                      stats_done, means_done, var_ready, sd_ready, xn_ready)
            dve.wait_ge(w_ready, 48)

            def clip(c):
                if c >= 2:
                    dve.wait_ge(used, c - 1)
                if c < 4:
                    for i in range(4 * c, 4 * c + 4):
                        dve.wait_ge(kv_taken, i + 1)
                        nc.vector.tensor_scalar(order(c, 1)[:, (i % 4) * D:(i % 4 + 1) * D], mem.ps[:, RING[i % 4], 0:D],
                                                0.25, 1.0, ALU.mult, ALU.min).then_inc(scaled, 1)
                    dve.wait_ge(scaled, 4 * c + 4)
                else:
                    for h in range(2):
                        n = 2 * (c - 4) + h
                        dve.wait_ge(q_ps, n + 1)
                        nc.vector.tensor_scalar(order(c, 1)[:, h * N:(h + 1) * N], mem.ps[:, RING[(NT + n) % 4], :],
                                                0.25, 1.0, ALU.mult, ALU.min).then_inc(scaled, 1)
                    dve.wait_ge(scaled, NT + 2 * (c - 4) + 2)
                nc.vector.tensor_scalar(order(c, 1), order(c, 1), -1.0, None, ALU.max).then_inc(x_ready, 1)

            def odd(c, m):
                n = 4 * c + m // 2
                lo = m // 2
                if m == 3:
                    dve.wait_ge(x_ready, c + 1)
                if m in (3, 7):
                    dve.wait_ge(even_ready, 5 * c + (m + 1) // 4)
                if m > 3:
                    dve.wait_ge(odd_ready, 4 * c + (m + 1) // 4 if m < 9 else 4 * c + 2)
                nc.vector.tensor_tensor(order(c, m), order(c, lo), order(c, lo + 1), ALU.mult).then_inc(product, 1)
                dve.wait_ge(product, n)
                nc.vector.scalar_tensor_tensor(order(c, m), order(c, m), 2.0, order(c, 1), ALU.mult,
                                               ALU.subtract).then_inc(odd_ready, 1)

            def assemble(b):
                dve.wait_ge(used, 2 * b + 2)
                block = mem.const[:, K_BLOCK:K_BLOCK + P]
                for o in range(2):
                    link(nc.vector.transpose(turned_kv.rearrange("p m c -> p (m c)"),
                                             mem.ps[:, SUMS + 2 * b + o, 0:M * 32]))
                    link(nc.vector.tensor_tensor(turned_kv, turned_kv,
                                                 mem.beta[:, o, :, None].broadcast_to([P, M, 32]), ALU.mult))
                    nc.vector.tensor_tensor(
                        kv[:, o, b, :, :].rearrange("p m (g c) -> p m g c", g=G32),
                        turned_kv[:, :, None, :].broadcast_to([P, M, G32, 32]),
                        block.rearrange("p (g c) -> p g c", g=G32)[:, None, :, :].broadcast_to([P, M, G32, 32]),
                        ALU.mult).then_inc(kv_ready, 1)
                    dve.wait_ge(kv_ready, 2 * b + o + 1)

            clip(0)
            clip(1)
            for c in range(8):
                odd(c, 3)
                odd(c, 5)
                odd(c, 7)
                if 1 <= c < 7:
                    clip(c + 1)
                odd(c, 9)
                if c in (2, 4):
                    assemble(c // 2 - 1)

        @block.tensor
        def _(pe):
            transpose_rows(nc, pe, mem, lambda i, k: mem.xw[:, i, k * P:(k + 1) * P],
                           lambda i: pe.wait_ge(xn_ready, i + 1), turned)
            pe.wait_ge(xT_ready, 8)
            pe.wait_ge(w_ready, 48)

            def project_kv(c):
                for i in range(4 * c, 4 * c + 4):
                    if i >= 4:
                        pe.wait_ge(scaled, i - 3)
                    for k in range(KD):
                        ins = nc.tensor.matmul(mem.ps[:, RING[i % 4], :], mem.xT[:, k, i * P:(i + 1) * P],
                                               w_in[:, k, D:3 * D], start=(k == 0), stop=(k == KD - 1))
                    ins.then_inc(kv_ps, 1)

            def project_q(c):
                o, b = c % 2, (c - 4) // 2
                for h in range(2):
                    n = 2 * (c - 4) + h
                    pe.wait_ge(scaled, NT + n - 3)
                    for k in range(KD):
                        ins = nc.tensor.matmul(mem.ps[:, RING[(NT + n) % 4], :], w_in[:, k, o * P:(o + 1) * P],
                                               mem.xT[:, k, b * S + h * N:b * S + (h + 1) * N],
                                               start=(k == 0), stop=(k == KD - 1))
                    ins.then_inc(q_ps, 1)

            def sum_kv(c):
                b = c // 2
                pe.wait_ge(ones_set, 1)
                pe.wait_ge(kv_taken, 4 * c + 4)
                pe.wait_ge(even_ready, 5 * c + 5)
                pe.wait_ge(odd_ready, 4 * c + 4)
                for i in range(4 * c, 4 * c + 4):
                    first, last = i % QT == 0, i % QT == QT - 1
                    for o in range(2):
                        for g in range(G32):
                            d0 = o * P + 32 * g
                            ins = nc.tensor.matmul(mem.ps[32 * g:32 * g + 32, SUMS + 2 * b + o, 0:M * 32],
                                                   V1[:, i, d0:d0 + 32],
                                                   feat[:, c % 2, :, (i % 4) * D + d0:(i % 4) * D + d0 + 32],
                                                   start=first, stop=last)
                ins.then_inc(used, 1)

            def times_kv(c):
                o, b = c % 2, (c - 4) // 2
                if c < 6:
                    pe.wait_ge(kv_ready, 2 * o + 2)
                else:
                    pe.wait_ge(kv_ready, 2 * b + o + 1)
                    pe.wait_ge(o_kept, 2 * (c - 6) + 2)
                for m in range(M):
                    if m == 1:
                        pe.wait_ge(x_ready, c + 1)
                    elif m and m % 2 == 0:
                        pe.wait_ge(even_ready, 5 * c + m // 2)
                    elif m:
                        pe.wait_ge(odd_ready, 4 * c + m // 2)
                    for h in range(2):
                        ins = nc.tensor.matmul(mem.ps[:, 2 * o + h, :], kv[:, o, b, m, :],
                                               order(c, m)[:, h * N:(h + 1) * N], start=(m == 0), stop=(m == M - 1))
                ins.then_inc(used, 1)

            project_kv(0)
            project_kv(1)
            project_kv(2)
            sum_kv(0)
            project_kv(3)
            sum_kv(1)
            project_q(4)
            sum_kv(2)
            project_q(5)
            sum_kv(3)
            times_kv(4)
            project_q(6)
            times_kv(5)
            project_q(7)
            times_kv(6)
            times_kv(7)



class Memory:
    pass


def build_tower(nc, io, out):
    with ExitStack() as ctx:
        def sb(name, shape, dt=F32):
            return ctx.enter_context(nc.sbuf_tensor(name, shape, dt))[(slice(None),) * len(shape)]

        def sem(name):
            return ctx.enter_context(nc.semaphore(name))

        mem = Memory()
        mem.ps = ctx.enter_context(nc.psum_tensor("banks", [P, 8, N], F32))[:, :, :]
        mem.h = sb("h", [P, NT, D])
        mem.xw = sb("xw", [P, NT, ROW])
        mem.xT = sb("xT", [P, KD, T])
        mem.arena = sb("arena", [P, ARENA])
        mem.const = sb("const", [P, K_ALL])
        mem.ident = mem.const[:, K_IDENT:K_IDENT + P]
        mem.ident_bf = sb("ident_bf", [P, P], BF16)
        mem.zero_bf = sb("zero_bf", [P, P], BF16)
        mem.ones_bf = sb("ones_bf", [P, P], BF16)
        mem.tri_bf = sb("tri_bf", [P, P], BF16)
        mem.ones = sb("ones", [P, N])
        mem.ids = sb("ids", [P, NT], I32)
        mem.bo = sb("bo", [P, D])
        wo = sb("wo_sb", [P, KD, D])
        mem.wo = wo[:, :, :]
        mem.gate = sb("gate", [P, KD, NE])
        mem.gate_b = sb("gate_b", [P, NE])
        mem.beta = sb("beta", [P, 2, M])
        mem.bn = sb("bn", [P, NT, 6])
        mem.mv = sb("mv", [P, NT, 2])
        mem.ve, mem.r2, mem.sd, mem.rstd = (sb(n, [P, NT]) for n in ("ve", "r2", "sd", "rstd"))
        mem.lg = sb("lg", [P, NT * NE])
        mem.s16 = sb("s16", [P, NT])
        mem.rank = sb("rank", [P, NT * NE])
        mem.mask = sb("mask", [P, 3, NT * NE])
        mem.mask_bf = sb("mask_bf", [P, NT * NE], BF16)
        mem.small = sb("small", [P, 6, NE])
        mem.slots = sb("slots", [P, TOP_K, NT], I32)
        mem.tf = sb("tf", [P, 2, 4 * N_WORDS + 2])
        mem.words = sb("words", [P, 2, N_WORDS])
        mem.tab = sb("tab", [P, 2, N_WORDS], I32)
        mem.places = sb("places", [P, 4, NE], I32)
        mem.n_has = sb("n_has", [P, 2])
        mem.b1_shared = sb("b1_shared", [P, 2 * F0 // P])
        mem.NM = sb("NM", [P, 2, 16])
        mem.mr = sb("mr", [P, 2, 16])
        mem.MP = sb("MP", [P, 2, P], BF16)
        mem.mTs = sb("mTs", [48, 2, P], BF16)
        mem.den = sb("den", [P, 16])

        a = Arena(mem.arena, 0)
        mem.QO = a.take(3 * HG * S // 2).bitcast(BF16).rearrange("p (s h t) -> p s h t", s=3, h=HG)
        mem.e = a.take(4 * 2 * N).rearrange("p (s n) -> p s n", s=4)
        mem.po = a.take(2 * N).rearrange("p (s n) -> p s n", s=2)
        mem.KO = a.take(3 * HG * S // 2).bitcast(BF16).rearrange("p (s h t) -> p s h t", s=3, h=HG)
        mem.V = a.take(NIT * QT * HG * DH).rearrange("p (i c x) -> p i c x", i=NIT, c=QT)
        mem.vst = a.take(3 * QT * HG * 32).rearrange("p (s c h x) -> p s c h x", s=3, c=QT, h=HG)
        mem.ao = mem.xT[:, :, :].rearrange("p k (i q x) -> p (k i) q x", i=NIT // KD // 2, q=QT)
        mem.free_at = a.at
        assert a.at <= ARENA - (NE + 1) * KD * 2 * F0
        mem.qk_in = [sem(f"qk_in{s}") for s in range(3)]
        a = Arena(mem.arena, 0)
        mem.w2 = a.take((NE + 1) * F0 // P * D).rearrange("p (e n) -> p e n", e=NE + 1)
        mem.b1 = a.take(NE * 2 * F0).rearrange("p (e n) -> p e n", e=NE)
        mem.b2 = a.take((NE + 1) * D).rearrange("p (e n) -> p e n", e=NE + 1)
        mem.layer0_at = a.at
        mem.w1_at = ARENA - (NE + 1) * KD * 2 * F0
        mem.w1 = Arena(mem.arena, mem.w1_at).take((NE + 1) * KD * 2 * F0).rearrange("p (e n) -> p e n", e=NE + 1)
        mem.ring_at = ARENA - 2 * (KD * 2 * F1 + F1 // P * D)
        a = Arena(mem.arena, mem.ring_at)
        mem.ring_gu = a.take(2 * KD * 2 * F1).rearrange("p (s n) -> p s n", s=2)
        mem.ring_dn = a.take(2 * F1 // P * D).rearrange("p (s n) -> p s n", s=2)

        def dram(name, shape, dt=F32):
            return nc.dram_tensor(name, shape, dt, kind="Internal").ap()

        mem.qk_dram = dram("qk_parts", [2, 3, B * D, S], BF16)
        mem.row_dram = dram("max_rows", [2, 48, P], BF16)
        mem.rows = [dram(f"rows{i}", [NRT * P, ROW]) for i in range(2)]
        mem.acc = (dram("acc0", [T + TRASH, D]), out)
        mem.pads_in, mem.experts_in, mem.w_loaded = sem("pads_in"), sem("experts_in"), sem("w_loaded")
        mem.acc_in = [sem(f"acc{i}_in") for i in range(2)]

        stage_embed_qkv(nc, mem, io, sem)
        stage_attention(nc, mem, io, sem)
        stage_router(nc, mem, io, sem, 0)
        stage_experts(nc, mem, io, sem, 0)
        stage_chebyshev(nc, mem, io, sem)
        stage_router(nc, mem, io, sem, 1)
        stage_experts(nc, mem, io, sem, 1)


def constants():
    p = np.arange(P)
    c = np.zeros((P, K_ALL), np.float32)
    c[:, K_IDENT:K_IDENT + P] = np.eye(P)
    c[:, K_TRI:K_TRI + P] = p[:, None] < p[None, :]
    c[:, K_BLOCK:K_BLOCK + P] = p[:, None] // DH == p[None, :] // DH
    e = np.arange(NE)
    c[:, K_LT:K_LT + NE * NE] = (e[None, :] < e[:, None]).reshape(1, -1)
    c[:, K_J128:K_J128 + NT] = P * np.arange(NT)
    c[:, K_J:K_J + NRT] = np.arange(NRT)
    c[:, K_PAD + C_ID] = (T + p).astype(np.int32).view(np.float32)
    c[:, K_MINUS] = -1.0
    c[:, K_TOK:K_TOK + NT] = P * np.arange(NT)[None, :] + p[:, None]
    return c


def kernel(**inputs):
    import concourse.bacc as bacc
    from concourse.bass_utils import run_bass_kernel_spmd

    x = {k: np.asarray(v) for k, v in inputs.items()}

    def halves(w):
        return w.reshape(-1, P, w.shape[-1]).transpose(1, 0, 2)

    def experts(w):
        return w.reshape(w.shape[0], -1, P, w.shape[-1]).transpose(0, 2, 1, 3).reshape(w.shape[0], P, -1)

    cat = np.concatenate
    arrays = {
        "ids": x["x"].reshape(NT, P).T,
        "tok": cat([x["L0_tok_weight"], x["L0_tok_scales"]], 1),
        "const": constants(),
        "wq": halves(x["L0_attn_Wq"].T), "wk": halves(x["L0_attn_Wk"].T), "wv": halves(x["L0_attn_Wv"].T),
        "wo": halves(x["L0_attn_Wo"].T), "bo": x["L0_attn_bo"],
        "gate0": halves(x["L0_ffn_gate_w"]), "gate_b": x["L0_ffn_gate_b"],
        "w1": experts(cat([x["L0_ffn_rw1"], x["L0_ffn_sw1"]])),
        "w2": experts(cat([x["L0_ffn_rw2"], x["L0_ffn_sw2"]])),
        "b1": x["L0_ffn_rb1"], "b1_shared": x["L0_ffn_sb1"].reshape(-1, P).T,
        "b2": cat([x["L0_ffn_rb2"], x["L0_ffn_sb2"]]),
        "w_in": halves(x["L1_attn_w_in"].T), "w_out": halves(x["L1_attn_w_out"].T),
        "beta": np.repeat(x["L1_attn_beta"], DH, axis=0).reshape(2, P, M).transpose(1, 0, 2),
        "gate1": halves(x["L1_ffn_gate_w"].T),
        "gu": experts(x["L1_ffn_gate_up_w"].transpose(0, 2, 1)),
        "dn": experts(x["L1_ffn_down_w"].transpose(0, 2, 1)),
    }
    nc = bacc.Bacc("TRN2", target_bir_lowering=False, num_devices=1)
    io, feeds = {}, {}
    for name, a in arrays.items():
        a = np.ascontiguousarray(a)
        feeds["in_" + name] = a
        io[name] = nc.dram_tensor("in_" + name, a.shape, mybir.dt.from_np(a.dtype), kind="ExternalInput").ap()
    out = nc.dram_tensor("out_rows", (T + TRASH, D), F32, kind="ExternalOutput").ap()
    build_tower(nc, io, out)
    r = run_bass_kernel_spmd(nc, [feeds], core_ids=[0])
    return r.results[0]["out_rows"][0:T].reshape(B, S, D)
```
